# Optimizing a Trainium2 kernel written in Bass

```python
import numpy as np
import jax
import jax.numpy as jnp

def _softmax(x, axis=-1):
    return jax.nn.softmax(x, axis=axis)

def _gelu(x):
    return jax.nn.gelu(x, approximate=True)

def _silu(x):
    return jax.nn.silu(x)

def _sigmoid(x):
    return jax.nn.sigmoid(x)

def _layernorm(x, axis=-1, eps=1e-05):
    m = jnp.mean(x, axis=axis, keepdims=True)
    v = jnp.var(x, axis=axis, keepdims=True)
    return (x - m) / jnp.sqrt(v + eps)

def _scatter_add(tgt, idx, src, axis=0):
    return tgt.at[idx].add(src)

def _segment_sum(src, seg, n):
    return jax.ops.segment_sum(src, seg, n)
kernel_name = 'mk_vit_tower_d2_tok_img256_r4_d0c51f'

def setup_inputs(seed: int=0):
    np.random.seed(seed)
    _w = jnp.asarray

    def _rec_inputs():
        import jax
        import jax.numpy as jnp
        _rk = jax.random.key(seed)
        x = -0.000596345 + 1.00056 * jax.random.normal(jax.random.fold_in(_rk, 1), (64, 64, 64, 3), jnp.float32)
        return x
    x = _rec_inputs()

    def _L0_tok_setup():
        import jax, jax.numpy as jnp
        import numpy as np
        M1, M2, WIDTH, LAYERS = (16, 16, 64, 4)
        B, H, W = (16, 64, 64)
        EPS = 1e-05

        def _spectral_conv(h, w1, w2):
            xf = jnp.fft.rfft2(h)
            top = jnp.einsum('bixy,ioxy->boxy', xf[:, :, :M1, :M2], w1)
            bot = jnp.einsum('bixy,ioxy->boxy', xf[:, :, -M1:, :M2], w2)
            of = jnp.zeros(xf.shape, dtype=xf.dtype)
            of = of.at[:, :, :M1, :M2].set(top)
            of = of.at[:, :, -M1:, :M2].set(bot)
            return jnp.fft.irfft2(of, s=(h.shape[-2], h.shape[-1]))
        key = jax.random.key(seed)
        ks = jax.random.split(key, 16)
        scale = 1.0 / (WIDTH * WIDTH)
        inp = {'x': jax.random.normal(ks[0], (B, H, W, 3), dtype=jnp.float32), 'fc0_w': jax.random.normal(ks[1], (3, WIDTH), dtype=jnp.float32) * 0.3, 'fc0_b': jnp.zeros((WIDTH,), jnp.float32), 'w1r': jax.random.normal(ks[2], (LAYERS, WIDTH, WIDTH, M1, M2), dtype=jnp.float32) * scale, 'w1i': jax.random.normal(ks[3], (LAYERS, WIDTH, WIDTH, M1, M2), dtype=jnp.float32) * scale, 'w2r': jax.random.normal(ks[4], (LAYERS, WIDTH, WIDTH, M1, M2), dtype=jnp.float32) * scale, 'w2i': jax.random.normal(ks[5], (LAYERS, WIDTH, WIDTH, M1, M2), dtype=jnp.float32) * scale, 'pw_w': jax.random.normal(ks[6], (LAYERS, WIDTH, WIDTH), dtype=jnp.float32) * (1.0 / np.sqrt(WIDTH)), 'pw_b': jnp.zeros((LAYERS, WIDTH), jnp.float32), 'gamma': jnp.ones((LAYERS, WIDTH), jnp.float32), 'beta': jnp.zeros((LAYERS, WIDTH), jnp.float32), 'fc1_w': jax.random.normal(ks[7], (WIDTH, 128), dtype=jnp.float32) * (1.0 / np.sqrt(WIDTH)), 'fc1_b': jnp.zeros((128,), jnp.float32), 'fc2_w': jax.random.normal(ks[8], (128, 1), dtype=jnp.float32) * (1.0 / np.sqrt(128.0)), 'fc2_b': jnp.zeros((1,), jnp.float32)}
        return inp
    _L0_tok_all = _L0_tok_setup()
    _L0_tok_in = {k: v for k, v in _L0_tok_all.items() if k in ('fc0_w', 'fc0_b', 'w1r', 'w1i', 'w2r', 'w2i', 'pw_w', 'pw_b', 'gamma', 'beta', 'fc1_w', 'fc1_b', 'fc2_w', 'fc2_b')}
    del _L0_tok_all

    def _L0_attn_setup():
        import jax, jax.numpy as jnp
        import numpy as np
        DIM = 64
        HEADS = 4
        DIM_HEAD = 32
        NUM_MEM = 4
        HIDDEN = HEADS * DIM_HEAD
        SCALE = DIM_HEAD ** (-0.5)

        def rmsnorm(x, g):
            n = jnp.linalg.norm(x, axis=-1, keepdims=True)
            return x / jnp.maximum(n, 1e-12) * g * x.shape[-1] ** 0.5
        key = jax.random.key(seed)
        ks = jax.random.split(key, 8)
        B, N = (4, 4096)
        return {'x': jax.random.normal(ks[0], (B, N, DIM), jnp.float32), 't': jax.random.normal(ks[1], (B,), jnp.float32), 'w_qkv': jax.random.normal(ks[2], (DIM, 3 * HIDDEN), jnp.float32) * 0.02, 'mem_kv': jax.random.normal(ks[3], (2, HEADS, DIM_HEAD, NUM_MEM), jnp.float32), 'w_out': jax.random.normal(ks[4], (HIDDEN, DIM), jnp.float32) * 0.02, 'b_out': jnp.zeros((DIM,), jnp.float32), 'g_out': jnp.ones((DIM,), jnp.float32), 'g_pre': jnp.ones((DIM,), jnp.float32)}
    _L0_attn_all = _L0_attn_setup()
    _L0_attn_in = {k: v for k, v in _L0_attn_all.items() if k in ('t', 'w_qkv', 'mem_kv', 'w_out', 'b_out', 'g_out', 'g_pre')}
    del _L0_attn_all

    def _L0_ffn_setup():
        import jax, jax.numpy as jnp
        import numpy as np
        B, S, D, H, E, K = (8, 2048, 64, 256, 8, 2)
        key = jax.random.key(seed)
        ks = jax.random.split(key, 7)
        s_in = 1.0 / np.sqrt(D)
        s_hid = 1.0 / np.sqrt(H)
        return {'x': jax.random.normal(ks[0], (B, S, D), dtype=jnp.float32), 'Wg': jax.random.uniform(ks[1], (E, D), jnp.float32, -s_in, s_in), 'bg': jax.random.uniform(ks[2], (E,), jnp.float32, -s_in, s_in), 'W1': jax.random.uniform(ks[3], (E, H, D), jnp.float32, -s_in, s_in), 'b1': jax.random.uniform(ks[4], (E, H), jnp.float32, -s_in, s_in), 'W2': jax.random.uniform(ks[5], (E, D, H), jnp.float32, -s_hid, s_hid), 'b2': jax.random.uniform(ks[6], (E, D), jnp.float32, -s_hid, s_hid)}
    _L0_ffn_all = _L0_ffn_setup()
    _L0_ffn_in = {k: v for k, v in _L0_ffn_all.items() if k in ('Wg', 'bg', 'W1', 'b1', 'W2', 'b2')}
    del _L0_ffn_all

    def _L1_attn_setup():
        import jax, jax.numpy as jnp
        import numpy as np
        import math
        B, S, D = (4, 1024, 64)
        key = jax.random.key(seed)
        ks = jax.random.split(key, 9)
        s = 1.0 / math.sqrt(D)
        return {'src': jax.random.normal(ks[0], (B, S, D), dtype=jnp.float32), 'Wq': jax.random.normal(ks[1], (D, D), dtype=jnp.float32) * s, 'bq': jax.random.normal(ks[2], (D,), dtype=jnp.float32) * s, 'Wk': jax.random.normal(ks[3], (D, D), dtype=jnp.float32) * s, 'bk': jax.random.normal(ks[4], (D,), dtype=jnp.float32) * s, 'Wv': jax.random.normal(ks[5], (D, D), dtype=jnp.float32) * s, 'bv': jax.random.normal(ks[6], (D,), dtype=jnp.float32) * s, 'Wo': jax.random.normal(ks[7], (D, D), dtype=jnp.float32) * s, 'bo': jax.random.normal(ks[8], (D,), dtype=jnp.float32) * s}
    _L1_attn_all = _L1_attn_setup()
    _L1_attn_in = {k: v for k, v in _L1_attn_all.items() if k in ('Wq', 'bq', 'Wk', 'bk', 'Wv', 'bv', 'Wo', 'bo')}
    del _L1_attn_all

    def _L1_ffn_setup():
        import jax, jax.numpy as jnp
        import numpy as np
        B, S, H, F, E, K = (8, 1024, 64, 128, 16, 2)
        EPS = 1e-05
        key = jax.random.key(seed)
        ks = jax.random.split(key, 9)
        sc = 0.02
        return {'x': jax.random.normal(ks[0], (B, S, H), dtype=jnp.float32), 'gate_w': jax.random.normal(ks[1], (H, E), dtype=jnp.float32) * sc, 'gate_b': jnp.zeros((E,), dtype=jnp.float32), 'w1': jax.random.normal(ks[2], (E, H, F), dtype=jnp.float32) * sc, 'b1': jnp.zeros((E, F), dtype=jnp.float32), 'w2': jax.random.normal(ks[3], (E, F, H), dtype=jnp.float32) * sc, 'b2': jnp.zeros((E, H), dtype=jnp.float32), 'gamma': jnp.ones((H,), dtype=jnp.float32), 'beta': jnp.zeros((H,), dtype=jnp.float32)}
    _L1_ffn_all = _L1_ffn_setup()
    _L1_ffn_in = {k: v for k, v in _L1_ffn_all.items() if k in ('gate_w', 'gate_b', 'w1', 'b1', 'w2', 'b2', 'gamma', 'beta')}
    del _L1_ffn_all
    return {'x': x, 'L0_tok_fc0_w': _L0_tok_in['fc0_w'], 'L0_tok_fc0_b': _L0_tok_in['fc0_b'], 'L0_tok_w1r': _L0_tok_in['w1r'], 'L0_tok_w1i': _L0_tok_in['w1i'], 'L0_tok_w2r': _L0_tok_in['w2r'], 'L0_tok_w2i': _L0_tok_in['w2i'], 'L0_tok_pw_w': _L0_tok_in['pw_w'], 'L0_tok_pw_b': _L0_tok_in['pw_b'], 'L0_tok_gamma': _L0_tok_in['gamma'], 'L0_tok_beta': _L0_tok_in['beta'], 'L0_tok_fc1_w': _L0_tok_in['fc1_w'], 'L0_tok_fc1_b': _L0_tok_in['fc1_b'], 'L0_tok_fc2_w': _L0_tok_in['fc2_w'], 'L0_tok_fc2_b': _L0_tok_in['fc2_b'], 'L0_attn_t': _L0_attn_in['t'], 'L0_attn_w_qkv': _L0_attn_in['w_qkv'], 'L0_attn_mem_kv': _L0_attn_in['mem_kv'], 'L0_attn_w_out': _L0_attn_in['w_out'], 'L0_attn_b_out': _L0_attn_in['b_out'], 'L0_attn_g_out': _L0_attn_in['g_out'], 'L0_attn_g_pre': _L0_attn_in['g_pre'], 'L0_ffn_Wg': _L0_ffn_in['Wg'], 'L0_ffn_bg': _L0_ffn_in['bg'], 'L0_ffn_W1': _L0_ffn_in['W1'], 'L0_ffn_b1': _L0_ffn_in['b1'], 'L0_ffn_W2': _L0_ffn_in['W2'], 'L0_ffn_b2': _L0_ffn_in['b2'], 'L1_attn_Wq': _L1_attn_in['Wq'], 'L1_attn_bq': _L1_attn_in['bq'], 'L1_attn_Wk': _L1_attn_in['Wk'], 'L1_attn_bk': _L1_attn_in['bk'], 'L1_attn_Wv': _L1_attn_in['Wv'], 'L1_attn_bv': _L1_attn_in['bv'], 'L1_attn_Wo': _L1_attn_in['Wo'], 'L1_attn_bo': _L1_attn_in['bo'], 'L1_ffn_gate_w': _L1_ffn_in['gate_w'], 'L1_ffn_gate_b': _L1_ffn_in['gate_b'], 'L1_ffn_w1': _L1_ffn_in['w1'], 'L1_ffn_b1': _L1_ffn_in['b1'], 'L1_ffn_w2': _L1_ffn_in['w2'], 'L1_ffn_b2': _L1_ffn_in['b2'], 'L1_ffn_gamma': _L1_ffn_in['gamma'], 'L1_ffn_beta': _L1_ffn_in['beta']}

def reference(x, L0_tok_fc0_w, L0_tok_fc0_b, L0_tok_w1r, L0_tok_w1i, L0_tok_w2r, L0_tok_w2i, L0_tok_pw_w, L0_tok_pw_b, L0_tok_gamma, L0_tok_beta, L0_tok_fc1_w, L0_tok_fc1_b, L0_tok_fc2_w, L0_tok_fc2_b, L0_attn_t, L0_attn_w_qkv, L0_attn_mem_kv, L0_attn_w_out, L0_attn_b_out, L0_attn_g_out, L0_attn_g_pre, L0_ffn_Wg, L0_ffn_bg, L0_ffn_W1, L0_ffn_b1, L0_ffn_W2, L0_ffn_b2, L1_attn_Wq, L1_attn_bq, L1_attn_Wk, L1_attn_bk, L1_attn_Wv, L1_attn_bv, L1_attn_Wo, L1_attn_bo, L1_ffn_gate_w, L1_ffn_gate_b, L1_ffn_w1, L1_ffn_b1, L1_ffn_w2, L1_ffn_b2, L1_ffn_gamma, L1_ffn_beta):
    import jax
    import jax.numpy as jnp

    def _L0_tok_ref(x, fc0_w, fc0_b, w1r, w1i, w2r, w2i, pw_w, pw_b, gamma, beta, fc1_w, fc1_b, fc2_w, fc2_b):
        import jax, jax.numpy as jnp
        import numpy as np
        M1, M2, WIDTH, LAYERS = (16, 16, 64, 4)
        B, H, W = (16, 64, 64)
        EPS = 1e-05

        def _spectral_conv(h, w1, w2):
            xf = jnp.fft.rfft2(h)
            top = jnp.einsum('bixy,ioxy->boxy', xf[:, :, :M1, :M2], w1)
            bot = jnp.einsum('bixy,ioxy->boxy', xf[:, :, -M1:, :M2], w2)
            of = jnp.zeros(xf.shape, dtype=xf.dtype)
            of = of.at[:, :, :M1, :M2].set(top)
            of = of.at[:, :, -M1:, :M2].set(bot)
            return jnp.fft.irfft2(of, s=(h.shape[-2], h.shape[-1]))
        h = jnp.einsum('bhwi,ic->bhwc', x, fc0_w) + fc0_b
        h = h.transpose(0, 3, 1, 2)
        for l in range(LAYERS):
            sc = _spectral_conv(h, w1r[l] + 1j * w1i[l], w2r[l] + 1j * w2i[l])
            pw = jnp.einsum('bihw,oi->bohw', h, pw_w[l]) + pw_b[l][None, :, None, None]
            y = sc + pw
            mean = y.mean(axis=(0, 2, 3), keepdims=True)
            var = y.var(axis=(0, 2, 3), keepdims=True)
            y = (y - mean) * jax.lax.rsqrt(var + EPS)
            y = y * gamma[l][None, :, None, None] + beta[l][None, :, None, None]
            h = jax.nn.gelu(y, approximate=False)
        h = h.transpose(0, 2, 3, 1)
        h = jax.nn.gelu(h @ fc1_w + fc1_b, approximate=False)
        out = (h @ fc2_w + fc2_b).squeeze(-1)
        return out

    def _L0_attn_ref(x, t, w_qkv, mem_kv, w_out, b_out, g_out, g_pre):
        import jax, jax.numpy as jnp
        import numpy as np
        DIM = 64
        HEADS = 4
        DIM_HEAD = 32
        NUM_MEM = 4
        HIDDEN = HEADS * DIM_HEAD
        SCALE = DIM_HEAD ** (-0.5)

        def rmsnorm(x, g):
            n = jnp.linalg.norm(x, axis=-1, keepdims=True)
            return x / jnp.maximum(n, 1e-12) * g * x.shape[-1] ** 0.5
        b, n, c = x.shape
        xn = rmsnorm(x, g_pre)
        qkv = xn @ w_qkv
        q, k, v = jnp.split(qkv, 3, axis=-1)

        def to_heads(z):
            return z.reshape(b, n, HEADS, DIM_HEAD).transpose(0, 2, 3, 1)
        q, k, v = map(to_heads, (q, k, v))
        mk = jnp.broadcast_to(mem_kv[0], (b, HEADS, DIM_HEAD, NUM_MEM))
        mv = jnp.broadcast_to(mem_kv[1], (b, HEADS, DIM_HEAD, NUM_MEM))
        k = jnp.concatenate([mk, k], axis=-1)
        v = jnp.concatenate([mv, v], axis=-1)
        q = jax.nn.softmax(q, axis=-2) * SCALE
        k = jax.nn.softmax(k, axis=-1)
        context = jnp.einsum('bhdn,bhen->bhde', k, v)
        out = jnp.einsum('bhde,bhdn->bhen', context, q)
        out = out.transpose(0, 3, 1, 2).reshape(b, n, HIDDEN)
        out = rmsnorm(out @ w_out + b_out, g_out)
        return out + x

    def _L0_ffn_ref(x, Wg, bg, W1, b1, W2, b2):
        import jax, jax.numpy as jnp
        import numpy as np
        B, S, D, H, E, K = (8, 2048, 64, 256, 8, 2)
        gate_scores = jnp.einsum('bsd,ed->bse', x, Wg) + bg
        topk_scores, topk_idx = jax.lax.top_k(gate_scores, K)
        topk_probs = jax.nn.softmax(topk_scores, axis=-1)
        combine = jnp.sum(topk_probs[..., None] * jax.nn.one_hot(topk_idx, E, dtype=x.dtype), axis=-2)
        out = jnp.zeros_like(x)
        for e in range(E):
            h = jax.nn.relu(jnp.einsum('bsd,hd->bsh', x, W1[e]) + b1[e])
            y = jnp.einsum('bsh,dh->bsd', h, W2[e]) + b2[e]
            out = out + combine[..., e:e + 1] * y
        return out

    def _L1_attn_ref(src, Wq, bq, Wk, bk, Wv, bv, Wo, bo):
        import jax, jax.numpy as jnp
        import numpy as np
        import math
        B, S, D = (4, 1024, 64)
        q = src @ Wq.T + bq
        k = src @ Wk.T + bk
        v = src @ Wv.T + bv
        row_mask = (q[:, :, 0] != 0) & (k[:, :, 0] != 0)
        mask = row_mask[:, :, None]
        scale = 1.0 / math.sqrt(D)
        scores = jnp.einsum('bid,bjd->bij', q, k) * scale
        scores = jnp.where(mask, scores, jnp.float32(-1000000000.0))
        prob = jax.nn.softmax(scores, axis=-1)
        prob = jnp.where(mask, prob, 0.0)
        out = jnp.einsum('bij,bjd->bid', prob, v)
        return out @ Wo.T + bo

    def _L1_ffn_ref(x, gate_w, gate_b, w1, b1, w2, b2, gamma, beta):
        import jax, jax.numpy as jnp
        import numpy as np
        B, S, H, F, E, K = (8, 1024, 64, 128, 16, 2)
        EPS = 1e-05
        gate_logits = x @ gate_w + gate_b
        topk_vals, topk_idx = jax.lax.top_k(gate_logits, K)
        topk_w = jax.nn.softmax(topk_vals, axis=-1)
        h = jax.nn.relu(jnp.einsum('bsh,ehf->bsef', x, w1) + b1)
        expert_out = jnp.einsum('bsef,efh->bseh', h, w2) + b2
        sel = jnp.take_along_axis(expert_out, topk_idx[:, :, :, None], axis=2)
        moe = jnp.sum(topk_w[..., None] * sel, axis=2)
        y = x + moe
        mu = jnp.mean(y, axis=-1, keepdims=True)
        var = jnp.var(y, axis=-1, keepdims=True)
        return (y - mu) / jnp.sqrt(var + EPS) * gamma + beta
    h = _L0_tok_ref(x, L0_tok_fc0_w, L0_tok_fc0_b, L0_tok_w1r, L0_tok_w1i, L0_tok_w2r, L0_tok_w2i, L0_tok_pw_w, L0_tok_pw_b, L0_tok_gamma, L0_tok_beta, L0_tok_fc1_w, L0_tok_fc1_b, L0_tok_fc2_w, L0_tok_fc2_b)
    h = h + _L0_attn_ref(_layernorm(h, axis=-1), L0_attn_t, L0_attn_w_qkv, L0_attn_mem_kv, L0_attn_w_out, L0_attn_b_out, L0_attn_g_out, L0_attn_g_pre)
    h = h + _L0_ffn_ref(_layernorm(h, axis=-1), L0_ffn_Wg, L0_ffn_bg, L0_ffn_W1, L0_ffn_b1, L0_ffn_W2, L0_ffn_b2)
    h = h + _L1_attn_ref(_layernorm(h, axis=-1), L1_attn_Wq, L1_attn_bq, L1_attn_Wk, L1_attn_bk, L1_attn_Wv, L1_attn_bv, L1_attn_Wo, L1_attn_bo)
    h = h + _L1_ffn_ref(_layernorm(h, axis=-1), L1_ffn_gate_w, L1_ffn_gate_b, L1_ffn_w1, L1_ffn_b1, L1_ffn_w2, L1_ffn_b2, L1_ffn_gamma, L1_ffn_beta)
    return h

_drawn_inputs = setup_inputs


def setup_inputs(seed=0):
    import zlib

    import numpy as np

    out = dict(_drawn_inputs(seed))
    spreads = {'L0_tok_fc0_b': (0.0, 0.8),
     'L0_tok_pw_b': (0.0, 0.8),
     'L0_tok_gamma': (1.0, 0.2),
     'L0_tok_beta': (0.0, 0.1),
     'L0_tok_fc1_b': (0.0, 0.1),
     'L0_attn_b_out': (0.0, 0.1),
     'L0_attn_g_out': (1.0, 0.2),
     'L0_attn_g_pre': (1.0, 0.6),
     'L1_ffn_gate_b': (0.0, 0.352),
     'L1_ffn_b1': (0.0, 0.8),
     'L1_ffn_b2': (0.0, 0.345),
     'L1_ffn_gamma': (1.0, 0.2),
     'L1_ffn_beta': (0.0, 0.1)}
    factors = {'L0_tok_w1r': 8.0,
     'L0_tok_w1i': 8.0,
     'L0_tok_w2r': 8.0,
     'L0_tok_w2i': 8.0,
     'L0_attn_w_qkv': 8.0,
     'L0_attn_mem_kv': 5.608,
     'L0_attn_w_out': 5.067,
     'L0_ffn_b1': 4.764,
     'L0_ffn_b2': 3.821,
     'L1_attn_bq': 5.993,
     'L1_attn_bk': 8.0,
     'L1_ffn_w1': 8.0,
     'L1_ffn_w2': 8.0}
    for name, (base, spread) in spreads.items():
        noise = np.random.default_rng([zlib.crc32(name.encode()), seed]).standard_normal(out[name].shape)
        drawn = base * np.exp(spread * noise) if base else spread * noise
        out[name] = jnp.asarray(drawn.astype(out[name].dtype))
    for name, factor in factors.items():
        out[name] = (out[name] * factor).astype(out[name].dtype)
    return out
```

```python
from contextlib import ExitStack

import numpy as np

import concourse.bass as bass
from concourse import mybir

F32 = mybir.dt.float32
ACT = mybir.ActivationFunctionType
ALU = mybir.AluOpType
AX = mybir.AxisListType

P = 128
C = 64
S = 64
PX = S * S
M1, M2 = 16, 16
K1 = 2 * M1
L = 4
CH = 4
NCH = K1 // CH
MC = CH * M2
Q = 4
GI = 2 * Q
BK = 512
EPS = 1e-5
ENGINES = 5


def dft_constants():
    h = np.arange(S)
    k1 = np.concatenate([np.arange(M1), np.arange(S - M1, S)])
    k2 = np.arange(M2)
    w_ang = 2 * np.pi * np.outer(h, k2) / S
    h_ang = 2 * np.pi * np.outer(h, k1) / S
    fw2 = np.kron(np.eye(2), np.stack([np.cos(w_ang), -np.sin(w_ang)], -1).reshape(S, 2 * M2))
    gh = np.block([[np.cos(h_ang), -np.sin(h_ang)], [np.sin(h_ang), np.cos(h_ang)]])
    ga = np.block([[np.cos(h_ang).T, np.sin(h_ang).T], [-np.sin(h_ang).T, np.cos(h_ang).T]]) / S
    fb = np.stack([2 * np.cos(w_ang).T, -2 * np.sin(w_ang).T], 1)
    fb[0, 0], fb[0, 1] = 1.0, 0.0
    fb4 = np.kron(np.eye(4), fb.reshape(2 * M2, S) / S)
    g0 = np.stack([np.kron(np.eye(2), np.cos(h_ang)), np.kron(np.eye(2), -np.sin(h_ang))], 1)
    cs, sn = np.cos(w_ang), np.sin(w_ang)
    part = np.stack([np.stack([cs, -sn], 1), np.stack([sn, cs], 1)], 0)
    f0 = np.einsum("pwrk,ij->pwirjk", part, np.eye(3)).reshape(2, 2, 96, 6 * M2).transpose(2, 0, 1, 3)
    dc = np.zeros((1, K1))
    dc[0, 0] = PX
    consts = {"c_fw2": fw2, "c_gh": gh, "c_ga": ga, "c_fb4": fb4, "c_g0": g0.reshape(P, 4 * K1),
              "c_f0": f0.reshape(96, 4, 96), "c_dc": dc, "c_ident": np.eye(P),
              "c_half": np.kron(np.full((2, 2), 0.5), np.eye(C))}
    return {k: np.ascontiguousarray(v, dtype=np.float32) for k, v in consts.items()}


def tower_layout(x, fc0_w, fc0_b, w1r, w1i, w2r, w2i, pw_w):
    x, fc0_w, fc0_b, pw_w, w1r, w1i, w2r, w2i = (
        np.asarray(t) for t in (x, fc0_w, fc0_b, pw_w, w1r, w1i, w2r, w2i))
    B = x.shape[0]
    out = {}
    out["x_pair"] = np.ascontiguousarray(
        x.reshape(B // GI, 2, Q, PX, 3).transpose(0, 2, 1, 4, 3).reshape(B // 2, 6, PX))
    out["x_rows"] = np.ascontiguousarray(x.reshape(B // 2, 2 * S, S * 3))
    r, i = (np.concatenate(t, 3).reshape(L, C, C, NCH, MC).transpose(0, 3, 1, 4, 2)
            for t in ((w1r, w2r), (w1i, w2i)))
    w = np.empty((L, NCH, 2, C, MC, 2, C), np.float32)
    w[:, :, 0, :, :, 0] = r
    w[:, :, 0, :, :, 1] = i
    w[:, :, 1, :, :, 0] = i
    w[:, :, 1, :, :, 1] = r
    out["w_modes"] = w.reshape(L, NCH, P, MC, P)
    out["pw_t"] = np.ascontiguousarray(pw_w.transpose(0, 2, 1))
    f = np.zeros((6 * M2 + 1, M2, 2, C), np.float32)
    for ri in range(2):
        for j in range(3):
            for k in range(M2):
                f[(ri * 3 + j) * M2 + k, k, ri] = fc0_w[j]
    f[6 * M2, 0, 0] = fc0_b
    out["fc0_modes"] = f.reshape(6 * M2 + 1, M2, P)
    out["fc0_t"] = np.ascontiguousarray(fc0_w.T)
    out["fc0_b"] = fc0_b
    return out


def build(nc, d, B, out):
    NP, NG = B // 2, B // GI
    MB = 16
    NB = B // MB

    with ExitStack() as ctx:
        def sem(name):
            return ctx.enter_context(nc.semaphore(name))

        def sb(name, shape):
            return ctx.enter_context(nc.sbuf_tensor(name, shape, F32))

        spec_in = nc.dram_tensor("spec_in", [2, C, NCH, B, MC], F32, kind="Internal").ap()
        spec_out = nc.dram_tensor("spec_out", [NG, 2, K1, C, GI * M2], F32, kind="Internal").ap()
        y_dram = nc.dram_tensor("y_dram", [NP, P, PX], F32, kind="Internal").ap()

        ident = sb("ident", [P, P])
        fw2 = sb("fw2", [P, 4 * M2])
        gh = sb("gh", [P, 2 * K1])
        ga = sb("ga", [2 * K1, 2 * S])
        fb4 = sb("fb4", [P, 4 * S])
        half = sb("half", [P, P])
        pw = sb("pw", [P, P])
        pwb = sb("pwb", [P, 1])
        gamma = sb("gamma", [P, 1])
        beta = sb("beta", [P, 1])
        pw0 = sb("pw0", [6, P])
        fc0t = sb("fc0t", [P, 6])
        fc0b = sb("fc0b", [P, 1])
        scale = sb("scale", [P, 1])
        shift = sb("shift", [P, 1])
        bn = sb("bn", [P, 12])
        stats = sb("stats", [P, NP * 48])
        fc1 = sb("fc1", [P, P])
        fc1b = sb("fc1b", [P, 1])
        fc2 = sb("fc2", [P, 1])
        fc2b = sb("fc2b", [P, 1])
        ARENA = 44800
        arena = sb("arena", [P, ARENA])

        def at(off, *shape, parts=P):
            n = int(np.prod(shape))
            assert off + n <= ARENA, (off, shape)
            v = arena[0:parts, off:off + n]
            if len(shape) == 2:
                v = v.rearrange("p (a b) -> p a b", a=shape[0])
            if len(shape) == 3:
                v = v.rearrange("p (a b c) -> p a b c", a=shape[0], b=shape[1])
            if len(shape) == 4:
                v = v.rearrange("p (a b c e) -> p a b c e", a=shape[0], b=shape[1], c=shape[2])
            return v

        bank = [ctx.enter_context(nc.psum_tensor(f"bank{i}", [P, BK], F32)) for i in range(8)]

        phase_done = sem("phase_done")
        zeroed = sem("zeroed")
        waited = {e.engine: sem(f"waited_{n}") for n, e in (
            ("sync", nc.sync), ("tensor", nc.tensor), ("scalar", nc.scalar), ("vector", nc.vector), ("gpsimd", nc.gpsimd))}

        def phase_end(eng, n):
            eng.sem_inc(waited[eng.engine], 1)
            eng.drain().then_inc(phase_done, 1)
            eng.wait_ge(phase_done, ENGINES * n)
            eng.sem_inc(waited[eng.engine], 1)

        const_loaded = sem("const_loaded")
        x0_loaded = [sem("x0_loaded_even"), sem("x0_loaded_odd")]
        rows0_done, rows0_copied, cols0_done, cols0_copied = (
            sem("rows0_done"), sem("rows0_copied"), sem("cols0_done"), sem("cols0_copied"))
        fc0_done, fc0_copied = sem("fc0_done"), sem("fc0_copied")
        spec0_stored, pw0_done, pw0_copied = sem("spec0_stored"), sem("pw0_done"), sem("pw0_copied")

        x0 = [at(192 * u, 192) for u in range(2)]
        z0 = [at(384 + 256 * u, 256, parts=96) for u in range(2)]
        v0 = at(1024, B, K1, parts=6 * M2 + 1)
        f0m = at(1024 + B * K1, M2, P, parts=6 * M2 + 1)
        f0c = at(1024 + B * K1 + M2 * P, 4, 96, parts=96)
        g0 = at(1024 + B * K1 + M2 * P + 384, P)
        spec0 = [at(8192 + u * NCH * MB * MC, NCH, MB, CH, M2) for u in range(2)]
        assert 1024 + B * K1 + M2 * P + 512 <= 8192

        def sync_spectrum0(sp):
            loads = [(ident[:], "c_ident"), (fw2[:], "c_fw2"), (gh[:], "c_gh"), (ga[:], "c_ga"), (fb4[:], "c_fb4"),
                     (half[:], "c_half"), (f0m, "fc0_modes"), (f0c, "c_f0"), (g0, "c_g0")]
            for dst, name in loads:
                sp.dma_start(dst, d[name]).then_inc(const_loaded, 16)
            sp.dma_start(v0[6 * M2:6 * M2 + 1, :, :],
                         d["c_dc"].rearrange("a (b k) -> a b k", b=1).to_broadcast([1, B, K1])).then_inc(const_loaded, 16)
            sp.wait_ge(zeroed, 3)
            for u in range(2):
                half_p = slice(u * C, (u + 1) * C)
                sp.dma_start(fc0b[half_p, :], d["fc0_b"].rearrange("(c a) -> c a", a=1)).then_inc(const_loaded, 16)
                sp.dma_start(fc0t[half_p, 3 * u:3 * u + 3], d["fc0_t"]).then_inc(const_loaded, 16)
                sp.dma_start(pw[half_p, u * C:(u + 1) * C], d["pw_t"][0]).then_inc(const_loaded, 16)
                sp.dma_start(pwb[half_p, :], d["pw_b"][0].rearrange("(c a) -> c a", a=1)).then_inc(const_loaded, 16)
                sp.dma_start(fc1[half_p, :], d["fc1_w"]).then_inc(const_loaded, 16)
            sp.dma_start(fc1b[:], d["fc1_b"].rearrange("(c a) -> c a", a=1)).then_inc(const_loaded, 16)
            sp.dma_start(fc2[:], d["fc2_w"]).then_inc(const_loaded, 16)
            sp.dma_start(fc2b[:], d["fc2_b"].rearrange("(c a) -> c a", a=1).to_broadcast([P, 1])).then_inc(const_loaded, 16)
            with sp.Fori(0, NP // 2) as i:
                for u in range(2):
                    sp.wait_ge(rows0_done, i * 2 + (u + 1))
                    sp.dma_start(x0[u], d["x_rows"][i * 2 + u]).then_inc(x0_loaded[u], 16)

        N_CONST = 16 * (10 + 10 + 3)

        def tensor_spectrum0(pe):
            pe.sem_inc(rows0_done, 2)
            pe.wait_ge(const_loaded, N_CONST)
            pe.matmul(bank[0][0:6, 0:P], fc0t[:], pw[:], start=True, stop=True)
            pe.matmul(bank[1][:, 0:1], pw[:], fc0b[:], start=True, stop=True).then_inc(pw0_done, 1)
            pe.wait_ge(pw0_copied, 2)
            with pe.Fori(0, NP // 2) as i:
                for u in range(2):
                    pe.wait_ge(rows0_copied, i * 2 + (u + 1))
                    pe.wait_ge(x0_loaded[u], i * 16 + 16)
                    for wh in range(2):
                        mm = pe.matmul(bank[u][0:96, wh * P:(wh + 1) * P], x0[u][:, wh * 96:(wh + 1) * 96], g0,
                                       start=True, stop=True)
                    mm.then_inc(rows0_done, 1)
                    pe.wait_ge(rows0_copied, i * 2 + (u + 3))
                    pe.wait_ge(cols0_copied, i * 2 + (u + 1))
                    for k in range(4):
                        part, wh = k // 2, k % 2
                        mm = pe.matmul(bank[2 + u][0:96, 0:2 * K1], f0c[:, part * 2 + wh, :],
                                       z0[u][:, wh * P + part * 2 * K1:wh * P + (part + 1) * 2 * K1],
                                       start=(k == 0), stop=(k == 3))
                    mm.then_inc(cols0_done, 1)
            pe.wait_ge(cols0_copied, NP + 2)
            with pe.Fori(0, NB) as t:
                for k in range(M2):
                    pe.wait_ge(fc0_copied, t * M2 + (k + 1))
                    pe.matmul(bank[4 + k % 4][:], f0m[:, k, :],
                              v0[:, bass.ds(t * MB, MB), :].rearrange("p b k -> p (b k)"),
                              start=True, stop=True).then_inc(fc0_done, 1)

        def vector_spectrum0(dve):
            dve.sem_inc(rows0_copied, 2)
            dve.sem_inc(cols0_copied, 2)
            dve.sem_inc(fc0_copied, 4)
            dve.wait_ge(pw0_done, 1)
            dve.wait_ge(const_loaded, N_CONST)
            dve.tensor_copy(pw0[:], bank[0][0:6, 0:P]).then_inc(pw0_copied, 1)
            dve.tensor_tensor(pwb[:], bank[1][:, 0:1], pwb[:], ALU.add).then_inc(pw0_copied, 1)
            with dve.Fori(0, NP // 2) as i:
                for u in range(2):
                    dve.wait_ge(rows0_done, i * 2 + (u + 3))
                    dve.tensor_copy(z0[u], bank[u][0:96, 0:256]).then_inc(rows0_copied, 1)
                    dve.wait_ge(cols0_done, i * 2 + (u + 1))
                    dve.tensor_scalar(v0[0:96, bass.ds(i * 4 + 2 * u, 2), :].rearrange("p b k -> p (b k)"),
                                      bank[2 + u][0:96, 0:2 * K1], 1.0, None, ALU.mult).then_inc(cols0_copied, 1)
            with dve.Fori(0, NB // 2 if NB > 1 else 1) as t:
                for u in range(2 if NB > 1 else 1):
                    for k in range(M2):
                        dve.wait_ge(fc0_done, t * (2 * M2) + (u * M2 + k + 1))
                        if k == 0:
                            dve.wait_ge(spec0_free, t * 2 + (u + 1))
                        dve.tensor_copy(spec0[u][:, :, :, :, k].rearrange("p h b k -> p b h k"),
                                        bank[4 + k % 4][:].rearrange("p (b h k) -> p b h k", b=MB, h=NCH)).then_inc(fc0_copied, 1)

        spec0_free = sem("spec0_free")

        def scalar_spectrum0(act):
            act.sem_inc(spec0_free, 2)
            for t in range(NB):
                act.wait_ge(fc0_copied, 4 + M2 * (t + 1))
                for ri in range(2):
                    act.dma_start(spec_in[ri, :, :, t * MB:(t + 1) * MB, :],
                                  spec0[t % 2][ri * C:(ri + 1) * C].rearrange("p h b k m -> p h b (k m)")
                                  ).then_inc(spec0_stored, 16)
                act.wait_ge(spec0_stored, 32 * (t + 1))
                act.sem_inc(spec0_free, 1)

        def gpsimd_spectrum0(pool):
            pool.memset(fc0t[:], 0.0).then_inc(zeroed, 1)
            pool.memset(pw[:], 0.0).then_inc(zeroed, 1)
            pool.memset(bn[:], 0.0).then_inc(zeroed, 1)

        w_loaded = [sem("w_loaded_even"), sem("w_loaded_odd")]
        s_loaded = [sem("s_loaded_even"), sem("s_loaded_odd")]
        layer_loaded = sem("layer_loaded")
        w_negated, mix_done, mixed_by_act, mixed_by_dve = (
            sem("w_negated"), sem("mix_done"), sem("mixed_by_act"), sem("mixed_by_dve"))
        mix_free, mixed_stored = sem("mix_free"), [sem("mixed_stored_even"), sem("mixed_stored_odd")]

        w_sb = [at(u * MC * P, MC, P) for u in range(2)]
        s_sb = [at(2 * MC * P + u * B * MC, B, MC) for u in range(2)]
        m_sb = [at(2 * MC * P + 2 * B * MC + u * CH * B * M2, CH, B, M2) for u in range(2)]
        IT = NCH // 2

        def sync_mix(sp, l, first):
            with sp.Fori(0, IT) as i:
                for u in range(2):
                    n = l * NCH + i * 2
                    sp.wait_ge(mix_free, n + (u + 1))
                    sp.dma_start(w_sb[u], d["w_modes"][l, i * 2 + u]).then_inc(w_loaded[u], 16)
                    for ri in range(2):
                        sp.dma_start(s_sb[u][ri * C:(ri + 1) * C], spec_in[ri, :, i * 2 + u]).then_inc(s_loaded[u], 16)
            for u in range(2):
                half_p = slice(u * C, (u + 1) * C)
                for dst, name in ((gamma, "gamma"), (beta, "beta")):
                    sp.dma_start(dst[half_p, :], d[name][l].rearrange("(c a) -> c a", a=1)).then_inc(layer_loaded, 16)
                if not first:
                    sp.dma_start(pw[half_p, u * C:(u + 1) * C], d["pw_t"][l]).then_inc(layer_loaded, 16)
                    sp.dma_start(pwb[half_p, :], d["pw_b"][l].rearrange("(c a) -> c a", a=1)).then_inc(layer_loaded, 16)
            sp.wait_ge(layer_loaded, l * 128 + 64)
            sp.sem_inc(waited[sp.engine], 1)

        def gpsimd_mix(pool, l):
            with pool.Fori(0, IT) as i:
                for u in range(2):
                    pool.wait_ge(w_loaded[u], (l * IT + i) * 16 + 16)
                    pool.sem_inc(waited[pool.engine], 1)
                    pool.tensor_scalar(w_sb[u][C:P, :, 0:C], w_sb[u][C:P, :, 0:C], -1.0, 0.0,
                                       ALU.mult, ALU.add).then_inc(w_negated, 1)

        def tensor_mix(pe, l, first):
            if first:
                pe.sem_inc(mix_free, 2)
            with pe.Fori(0, IT) as i:
                for u in range(2):
                    n = l * NCH + i * 2
                    pe.wait_ge(w_negated, n + (u + 1))
                    pe.wait_ge(s_loaded[u], (l * IT + i) * 32 + 32)
                    for j in range(8):
                        by = mixed_by_act if j % 2 == 0 else mixed_by_dve
                        pe.wait_ge(by, n * 4 + (4 * u + j // 2 + 1))
                        for m in range(8):
                            mm = pe.matmul(bank[j][:, m * B:(m + 1) * B], w_sb[u][:, 8 * j + m, :],
                                           s_sb[u][:, :, 8 * j + m], start=True, stop=True)
                        mm.then_inc(mix_done, 1)
                    pe.wait_ge(mix_done, n * 8 + (8 * u + 8))
                    pe.sem_inc(mix_free, 1)

        def mixed_view(u, j):
            kk, k = j // 2, 8 * (j % 2)
            return m_sb[u][:, kk, :, k:k + 8], bank[j][:, 0:8 * B].rearrange("p (m b) -> p b m", m=8)

        def scalar_mix(act, l, first):
            if first:
                act.sem_inc(mixed_by_act, 4)
                act.sem_inc(mixed_stored[0], 16 * 8)
                act.sem_inc(mixed_stored[1], 16 * 8)
            with act.Fori(0, IT) as i:
                for u in range(2):
                    n = l * NCH + i * 2
                    act.wait_ge(mixed_stored[u], (l * IT + i) * 128 + 128)
                    for j in range(0, 8, 2):
                        act.wait_ge(mix_done, n * 8 + (8 * u + j + 1))
                        o, v = mixed_view(u, j)
                        act.activation(o, v, ACT.Copy).then_inc(mixed_by_act, 1)
                    act.wait_ge(mixed_by_act, n * 4 + (4 * u + 8))
                    act.wait_ge(mixed_by_dve, n * 4 + (4 * u + 8))
                    for kk in range(CH):
                        for ri in range(2):
                            act.dma_start(spec_out[:, ri, i * (2 * CH) + (u * CH + kk)].rearrange("g c x -> c g x"),
                                          m_sb[u][ri * C:(ri + 1) * C, kk].rearrange("p (g b) k -> p g (b k)", g=NG)
                                          ).then_inc(mixed_stored[u], 16)
            for u in range(2):
                act.wait_ge(mixed_stored[u], l * (IT * 128) + (IT * 128 + 128))
            act.sem_inc(waited[act.engine], 1)

        def vector_mix(dve, l, first):
            if first:
                dve.sem_inc(mixed_by_dve, 4)
            with dve.Fori(0, IT) as i:
                for u in range(2):
                    n = l * NCH + i * 2
                    dve.wait_ge(mixed_stored[u], (l * IT + i) * 128 + 128)
                    for j in range(1, 8, 2):
                        dve.wait_ge(mix_done, n * 8 + (8 * u + j + 1))
                        o, v = mixed_view(u, j)
                        dve.tensor_copy(o, v).then_inc(mixed_by_dve, 1)

        grp_loaded, grp_free, pair_ready = sem("grp_loaded"), sem("grp_free"), sem("pair_ready")
        in_loaded = [sem("in_loaded_even"), sem("in_loaded_odd")]
        h_ready = sem("h_ready")
        rows_done, rows_copied, turn_done, turn_copied = (
            sem("rows_done"), sem("rows_copied"), sem("turn_done"), sem("turn_copied"))
        y_done, y_copied, y_seen = sem("y_done"), sem("y_copied"), sem("y_seen")
        y_stored = [sem("y_stored_even"), sem("y_stored_odd")]
        stat_taken, stat_kept = sem("stat_taken"), sem("stat_kept")
        bn_step, bn_sum, bn_root = sem("bn_step"), sem("bn_sum"), sem("bn_root")

        hin = [at(u * PX, PX) for u in range(2)]
        yout = [at((2 + u) * PX, PX) for u in range(2)]
        grp = at(4 * PX, C, GI, M2, parts=2 * K1)
        GW = C * GI * M2
        prs = [at(4 * PX + GW + q * M2 * P, M2, P, parts=2 * K1) for q in range(Q)]
        O1 = 4 * PX + GW + Q * M2 * P
        a1 = [at(O1 + u * 2048, S, 2 * M2) for u in range(2)]
        a2 = [at(O1 + 4096 + u * 2048, 16, P) for u in range(2)]
        st = [at(O1 + 8192 + u * 48, 48) for u in range(2)]

        def sync_inverse(sp, l, first):
            if first:
                sp.sem_inc(grp_free, 1)
                for u in range(2):
                    sp.sem_inc(y_stored[u], 16)
            with sp.Fori(0, NG) as g:
                G = l * NG + g
                sp.wait_ge(grp_free, G + 1)
                sp.dma_start(grp.rearrange("p c b k -> p (c b k)"),
                             spec_out[g].rearrange("r k c x -> (r k) (c x)")).then_inc(grp_loaded, 16)
                for q in range(Q):
                    u = q % 2
                    sp.wait_ge(y_done, (G * Q + q) * 8 + 8)
                    if first:
                        sp.dma_start(hin[u][0:6, :], d["x_pair"][g * Q + q]).then_inc(in_loaded[u], 16)
                    else:
                        sp.dma_start(hin[u], y_dram[g * Q + q]).then_inc(in_loaded[u], 16)

        def gpsimd_inverse(pool, l, first):
            with pool.Fori(0, NG) as g:
                G = l * NG + g
                for q in range(Q):
                    pool.wait_ge(rows_done, (G * Q + q) * 4 + 4)
                    pool.wait_ge(grp_loaded, G * 16 + 16)
                    pool.sem_inc(waited[pool.engine], 1)
                    for par in range(2):
                        pool.tensor_copy(prs[q][:, :, par * C:(par + 1) * C],
                                         grp[:, :, par * Q + q, :].rearrange("p c k -> p k c")).then_inc(pair_ready, 1)
                pool.wait_ge(pair_ready, G * (2 * Q) + 2 * Q)
                pool.sem_inc(waited[pool.engine], 1)
                pool.sem_inc(grp_free, 1)

        def tensor_inverse(pe, l, first):
            if first:
                pe.sem_inc(rows_done, 4 * Q)
                pe.sem_inc(y_done, 16)

            def rows(n, q, t):
                if t == 0:
                    pe.wait_ge(pair_ready, n * 2 + 2)
                pe.wait_ge(rows_copied, n * 4 + (t + 1))
                for k in range(4):
                    mm = pe.matmul(bank[t % 2][:, k * P:(k + 1) * P], prs[q][:, 4 * t + k, :], ga[:], start=True, stop=True)
                mm.then_inc(rows_done, 1)

            def turn(n, q, t):
                if t == 0:
                    pe.wait_ge(rows_copied, n * 4 + 6)
                pe.wait_ge(turn_copied, n * 4 + (t + 1))
                for k in range(4):
                    mm = pe.transpose(bank[2 + t % 2][:, k * P:(k + 1) * P],
                                      a1[q % 2][:, 16 * t + 4 * k:16 * t + 4 * k + 4, :].rearrange("p h m -> p (h m)"),
                                      ident[:])
                mm.then_inc(turn_done, 1)

            def columns(n, q, t):
                if t == 0 and first:
                    pe.wait_ge(in_loaded[q % 2], (n - q) * (16 // 2) + (q // 2 * 16 + 16))
                if t == 0 and not first:
                    pe.wait_ge(h_ready, n + 1)
                if t % 2 == 0:
                    pe.wait_ge(turn_copied, n * 4 + (t // 2 + 3))
                pe.wait_ge(y_copied, n * 8 + (t + 1))
                b = bank[4 + t % 4]
                src = hin[q % 2][0:6, :] if first else hin[q % 2]
                pe.matmul(b[:], pw0[:] if first else pw[:], src[:, t * BK:(t + 1) * BK], start=True, stop=False)
                for k in range(2):
                    mm = pe.matmul(b[:, k * 256:(k + 1) * 256], a2[q % 2][:, 2 * t + k, :], fb4[:], start=False, stop=(k == 1))
                mm.then_inc(y_done, 1)

            def group(G, last):
                for q in range(Q):
                    n = G * Q + q
                    for t in range(8):
                        columns(n, q, t)
                        if q < Q - 1 or not last:
                            if t < 4:
                                rows(n + 1, (q + 1) % Q, t)
                            else:
                                turn(n + 1, (q + 1) % Q, t - 4)

            for t in range(4):
                rows(l * (NG * Q), 0, t)
            for t in range(4):
                turn(l * (NG * Q), 0, t)
            with pe.Fori(0, NG - 1) as g:
                group(l * NG + g, False)
            group(l * NG + (NG - 1), True)
            pe.wait_ge(bn_step, l * BN_STEPS + 2)
            pe.wait_ge(y_copied, (l + 1) * (NP * 8) + 4)
            pe.matmul(bank[0][:, 0:1], half[:], bn[:, 0:1], start=True, stop=True).then_inc(bn_sum, 1)
            pe.wait_ge(bn_step, l * BN_STEPS + 4)
            pe.matmul(bank[1][:, 0:1], half[:], bn[:, 4:5], start=True, stop=True).then_inc(bn_sum, 1)

        BN_STEPS = 8

        def scalar_inverse(act, l, first):
            if first:
                act.sem_inc(y_copied, 4)
                act.sem_inc(h_ready, NP)

            def gelu(G, q):
                u = q % 2
                if first:
                    return
                act.wait_ge(in_loaded[u], G * 32 + (q // 2 * 16 + 16))
                act.sem_inc(waited[act.engine], 1)
                act.activation(hin[u], hin[u], ACT.Gelu, bias=shift[:], scale=scale[:]).then_inc(h_ready, 1)

            def y_out(n, G, g, q, t):
                u = q % 2
                if t == 0:
                    act.wait_ge(y_stored[u], G * 32 + (q // 2 * 16 + 16))
                    act.wait_ge(y_seen, n * 8 + 8)
                act.wait_ge(y_done, n * 8 + (t + 17))
                act.activation(yout[u][:, t * BK:(t + 1) * BK], bank[4 + t % 4][:], ACT.Identity,
                               bias=pwb[:]).then_inc(y_copied, 1)
                if t == 7:
                    act.wait_ge(y_copied, n * 8 + 12)
                    act.dma_start(y_dram[g * Q + q], yout[u]).then_inc(y_stored[u], 16)

            def group(G, g, last):
                for q in range(Q):
                    n = G * Q + q
                    for t in range(8):
                        y_out(n, G, g, q, t)
                        if t == 1 and (q < Q - 1 or not last):
                            if q < Q - 1:
                                gelu(G, q + 1)
                            else:
                                gelu(G + 1, 0)

            gelu(l * NG, 0)
            with act.Fori(0, NG - 1) as g:
                group(l * NG + g, g, False)
            group(l * NG + (NG - 1), NG - 1, True)
            for u in range(2):
                act.wait_ge(y_stored[u], l * (NG * 32) + (NG * 32 + 16))
            act.wait_ge(bn_step, l * BN_STEPS + 5)
            act.sem_inc(waited[act.engine], 1)
            act.activation(bn[:, 6:7], bn[:, 5:6], ACT.Sqrt).then_inc(bn_root, 1)

        def vector_inverse(dve, l, first):
            if first:
                dve.sem_inc(rows_copied, 2)
                dve.sem_inc(turn_copied, 2)
                dve.sem_inc(stat_kept, 2)
                dve.sem_inc(y_seen, 16)

            def rows(n, q, t):
                dve.wait_ge(rows_done, n * 4 + (4 * Q + t + 1))
                dve.tensor_copy(a1[q % 2][:, :, 8 * t:8 * t + 8],
                                bank[t % 2][:].rearrange("p (m h) -> p h m", m=8)).then_inc(rows_copied, 1)

            def turn(n, q, t):
                dve.wait_ge(turn_done, n * 4 + (t + 1))
                dve.tensor_copy(a2[q % 2][:, 4 * t:4 * t + 4, :].rearrange("p a b -> p (a b)"),
                                bank[2 + t % 2][:]).then_inc(turn_copied, 1)

            def moments(n, g, q, t):
                u = q % 2
                if t == 0:
                    dve.wait_ge(stat_kept, n + 1)
                dve.wait_ge(y_copied, n * 8 + (t + 5))
                s = dve.bn_stats(st[u][:, 6 * t:6 * t + 6], yout[u][:, t * BK:(t + 1) * BK])
                s.then_inc(y_seen, 1)
                if t == 7:
                    dve.wait_ge(y_seen, n * 8 + 24)
                    dve.tensor_scalar(stats[:, bass.ds((g * Q + q) * 48, 48)], st[u], 1.0, None,
                                      ALU.mult).then_inc(stat_kept, 1)

            def group(G, g, last):
                for q in range(Q):
                    n = G * Q + q
                    for t in range(8):
                        if q < Q - 1 or not last:
                            if t < 4:
                                rows(n + 1, (q + 1) % Q, t)
                            else:
                                turn(n + 1, (q + 1) % Q, t - 4)
                        moments(n, g, q, t)

            for t in range(4):
                rows(l * (NG * Q), 0, t)
            for t in range(4):
                turn(l * (NG * Q), 0, t)
            with dve.Fori(0, NG - 1) as g:
                group(l * NG + g, g, False)
            group(l * NG + (NG - 1), NG - 1, True)
            base = l * BN_STEPS
            dve.wait_ge(stat_kept, (l + 1) * NP + 2)
            dve.sem_inc(waited[dve.engine], 1)
            dve.bn_aggr(bn[:, 0:2], stats[:]).then_inc(bn_step, 1)
            dve.wait_ge(bn_step, base + 1)
            dve.tensor_copy(bn[:, 2:3], bn[:, 0:1]).then_inc(bn_step, 1)
            dve.wait_ge(bn_sum, l * 2 + 1)
            dve.tensor_tensor(bn[:, 3:4], bn[:, 0:1], bank[0][:, 0:1], ALU.subtract).then_inc(bn_step, 1)
            dve.wait_ge(bn_step, base + 3)
            dve.scalar_tensor_tensor(out=bn[:, 4:5], in0=bn[:, 3:4], scalar=bn[:, 3:4], in1=bn[:, 1:2],
                                     op0=ALU.mult, op1=ALU.add).then_inc(bn_step, 1)
            dve.wait_ge(bn_sum, l * 2 + 2)
            dve.tensor_scalar(bn[:, 5:6], bank[1][:, 0:1], EPS, None, ALU.add).then_inc(bn_step, 1)
            dve.wait_ge(bn_root, l + 1)
            dve.reciprocal(bn[:, 7:8], bn[:, 6:7]).then_inc(bn_step, 1)
            dve.wait_ge(bn_step, base + 6)
            dve.tensor_tensor(scale[:], bn[:, 7:8], gamma[:], ALU.mult).then_inc(bn_step, 1)
            dve.wait_ge(bn_step, base + 7)
            dve.tensor_tensor(bn[:, 8:9], scale[:], bank[0][:, 0:1], ALU.mult).then_inc(bn_step, 1)
            dve.wait_ge(bn_step, base + 8)
            dve.tensor_tensor(shift[:], beta[:], bn[:, 8:9], ALU.subtract).then_inc(stat_taken, 1)
            dve.wait_ge(stat_taken, l + 1)
            dve.sem_inc(waited[dve.engine], 1)

        f_loaded = [sem(f"f_loaded{i}") for i in range(Q)]
        f_ready = sem("f_ready")
        ht_done, ht_copied, fc_done, fc_copied = sem("ht_done"), sem("ht_copied"), sem("fcol_done"), sem("fcol_copied")
        ft_done, ft_copied, fr_done, fr_copied = sem("ft_done"), sem("ft_copied"), sem("frow_done"), sem("frow_copied")
        spec_stored = [sem("spec_stored_a"), sem("spec_stored_b")]

        hf = [at(q * PX, PX) for q in range(Q)]
        FO = Q * PX
        ht = [at(FO + u * BK, 4, P) for u in range(2)]
        t1 = [at(FO + 1024 + u * 2048, 2 * M2, S) for u in range(2)]
        t2 = [at(FO + 5120 + u * BK, 4, P) for u in range(2)]
        xs = [at(FO + 6144 + u * 4096, 2, NCH, 2, MC) for u in range(2)]

        def sync_forward(sp, lf, first):
            with sp.Fori(0, NG) as g:
                F = lf * NG + g
                for q in range(Q):
                    sp.wait_ge(ht_done, (F * Q + q) * 8 + 8)
                    sp.dma_start(hf[q], y_dram[g * Q + q]).then_inc(f_loaded[q], 16)

        def tensor_forward(pe, lf):
            def turn(n, q, t):
                if t % 4 == 0:
                    pe.wait_ge(f_ready, n * 2 + (t // 4 + 1))
                pe.wait_ge(ht_copied, n * 8 + (t + 1))
                for k in range(4):
                    mm = pe.transpose(bank[t % 2][:, k * P:(k + 1) * P], hf[q][:, (4 * t + k) * P:(4 * t + k + 1) * P], ident[:])
                mm.then_inc(ht_done, 1)

            def columns(n, t):
                pe.wait_ge(ht_copied, n * 8 + (t + 3))
                if t % 2 == 0:
                    pe.wait_ge(fc_copied, n * 4 + (t // 2 + 1))
                b = bank[2 + t // 2 % 2]
                for k in range(4):
                    mm = pe.matmul(b[:, (t % 2) * 256 + k * 64:(t % 2) * 256 + (k + 1) * 64], ht[t % 2][:, k, :], fw2[:],
                                   start=True, stop=True)
                mm.then_inc(fc_done, 1)

            def turn_rows(n, q, t):
                if t == 0:
                    pe.wait_ge(fc_copied, n * 4 + 6)
                pe.wait_ge(ft_copied, n * 4 + (t + 1))
                for k in range(4):
                    mm = pe.transpose(bank[4 + t % 2][:, k * P:(k + 1) * P],
                                      t1[q % 2][:, 8 * t + 2 * k:8 * t + 2 * k + 2, :].rearrange("p m h -> p (m h)"), ident[:])
                mm.then_inc(ft_done, 1)

            def rows(n, t):
                pe.wait_ge(ft_copied, n * 4 + (t + 3))
                if t % 2 == 0:
                    pe.wait_ge(fr_copied, n * 2 + (t // 2 + 1))
                for k in range(4):
                    mm = pe.matmul(bank[6 + t // 2][:, (t % 2) * 256 + k * 64:(t % 2) * 256 + (k + 1) * 64], t2[t % 2][:, k, :],
                                   gh[:], start=True, stop=True)
                mm.then_inc(fr_done, 1)

            def group(F, first):
                for q in range(Q):
                    n = F * Q + q
                    before = q > 0 or not first
                    for t in range(8):
                        turn(n, q, t)
                        if t > 0:
                            columns(n, t - 1)
                        elif before:
                            columns(n - 1, 7)
                        if before and 2 <= t < 6:
                            turn_rows(n - 1, (q - 1) % Q, t - 2)
                        if before and 3 <= t < 7:
                            rows(n - 1, t - 3)

            group(lf * NG, True)
            with pe.Fori(1, NG) as g:
                group(lf * NG + g, False)
            n = lf * NP + (NP - 1)
            columns(n, 7)
            for t in range(5):
                if t < 4:
                    turn_rows(n, Q - 1, t)
                if t > 0:
                    rows(n, t - 1)

        def scalar_forward(act, lf, first_time):
            def gelu(F, n, q):
                act.wait_ge(f_loaded[q], F * 16 + 16)
                act.sem_inc(waited[act.engine], 1)
                for v in range(2):
                    x = hf[q][:, v * 2048:(v + 1) * 2048]
                    act.activation(x, x, ACT.Gelu, bias=shift[:], scale=scale[:]).then_inc(f_ready, 1)

            def t2_copies(n):
                for t in range(4):
                    act.wait_ge(ft_done, n * 4 + (t + 1))
                    act.activation(t2[t % 2].rearrange("p a b -> p (a b)"), bank[4 + t % 2][:], ACT.Copy).then_inc(ft_copied, 1)

            def store(n_last, b0, v):
                act.wait_ge(fr_copied, n_last * 2 + 4)
                for ri in range(2):
                    for par in range(2):
                        act.dma_start(spec_in[ri, :, :, bass.ds(b0 + (par * Q + 2 * v), 2), :],
                                      xs[v][par * C:(par + 1) * C, ri]).then_inc(spec_stored[v], 16)

            def group(F, g, first):
                for q in range(Q):
                    n = F * Q + q
                    gelu(F, n, q)
                    if q == 3:
                        store(n - 2, g * GI, 0)
                    if q == 1 and not first:
                        store(n - 2, g * GI - GI, 1)
                    if q > 0 or not first:
                        t2_copies(n - 1)

            group(lf * NG, 0, True)
            with act.Fori(1, NG) as g:
                group(lf * NG + g, g, False)
            n = lf * NP + (NP - 1)
            t2_copies(n)
            store(n, (NG - 1) * GI, 1)
            for v in range(2):
                act.wait_ge(spec_stored[v], lf * (NG * 64) + (NG * 64 + 64))
            act.sem_inc(waited[act.engine], 1)

        def vector_forward(dve, lf):
            def ht_copy(n, t):
                dve.wait_ge(ht_done, n * 8 + (8 * Q + t + 1))
                dve.tensor_copy(ht[t % 2].rearrange("p a b -> p (a b)"), bank[t % 2][:]).then_inc(ht_copied, 1)

            def column_copy(n, q, t):
                dve.wait_ge(fc_done, n * 8 + (2 * t + 2))
                dve.tensor_copy(t1[q % 2][:, :, 16 * t:16 * t + 16],
                                bank[2 + t % 2][:].rearrange("p (h m) -> p m h", h=16)).then_inc(fc_copied, 1)

            def row_copy(n, q, t):
                v = q // 2
                if q % 2 == 0 and t == 0:
                    dve.wait_ge(spec_stored[v], (n - q) * (64 // Q) + 64)
                dve.wait_ge(fr_done, n * 4 + (2 * t + 2))
                for ri in range(2):
                    o = xs[v][:, ri, :, q % 2, :].rearrange("p h (k m) -> p h k m", k=CH)[:, :, :, 8 * t:8 * t + 8]
                    cp = dve.tensor_copy(o, bank[6 + t][:].rearrange("p (m r h k) -> p r h k m", m=8, r=2, h=NCH)[:, ri])
                cp.then_inc(fr_copied, 1)

            def group(F, first):
                for q in range(Q):
                    n = F * Q + q
                    before = q > 0 or not first
                    for t in range(8):
                        ht_copy(n, t)
                        if t == 0 and before:
                            column_copy(n - 1, (q - 1) % Q, 3)
                        if t % 2 == 0 and t > 0:
                            column_copy(n, q, t // 2 - 1)
                        if before and t in (4, 6):
                            row_copy(n - 1, (q - 1) % Q, (t - 4) // 2)

            group(lf * NG, True)
            with dve.Fori(1, NG) as g:
                group(lf * NG + g, False)
            n = lf * NP + (NP - 1)
            column_copy(n, Q - 1, 3)
            for t in range(2):
                row_copy(n, Q - 1, t)

        e_loaded = [sem(f"e_loaded{i}") for i in range(Q)]
        e_ready, fc1_done, fc1_used, fc1_gelu, fc2_done = (
            sem("e_ready"), sem("fc1_done"), sem("fc1_used"), sem("fc1_gelu"), sem("fc2_done"))
        px_copied, px_turned, px_out, tok_stored = sem("px_copied"), sem("px_turned"), sem("px_out"), sem("tok_stored")
        NGB = 4
        gb = [at(FO + u * BK, BK) for u in range(NGB)]
        pxs = at(FO + NGB * BK, 256)
        pxt = at(FO + NGB * BK + 256, 2, P)
        TB = 16
        LAG = 2

        def sync_head(sp):
            with sp.Fori(0, NG) as g:
                for q in range(Q):
                    sp.wait_ge(fc1_done, (g * Q + q) * TB + TB)
                    sp.dma_start(hf[q], y_dram[g * Q + q]).then_inc(e_loaded[q], 16)

        def tensor_head(pe):
            pe.sem_inc(fc1_done, TB * Q)
            pe.sem_inc(fc1_used, NGB)

            def first(n, q, t):
                par, tt = t // 8, t % 8
                if t % 8 == 0:
                    pe.wait_ge(e_ready, n * 2 + 2)
                pe.wait_ge(fc1_gelu, n * TB + (t + 1))
                mm = pe.matmul(bank[t % 4][:], fc1[par * C:(par + 1) * C, :], hf[q][par * C:(par + 1) * C, tt * BK:(tt + 1) * BK],
                               start=True, stop=True)
                mm.then_inc(fc1_done, 1)

            def second(n, q, t):
                par, tt = t // 8, t % 8
                pe.wait_ge(fc1_gelu, n * TB + (t + 5))
                col = (par * Q + q) * 32 + tt * 4
                for k in range(4):
                    mm = pe.matmul(bank[6][:, col + k:col + k + 1], gb[t % NGB][:, k * P:(k + 1) * P], fc2[:], start=True, stop=True)
                mm.then_inc(fc1_used, 1)

            with pe.Fori(0, NG) as g:
                pe.wait_ge(px_copied, g + 1)
                for i in range(Q * TB + LAG):
                    if i < Q * TB:
                        first(g * Q + i // TB, i // TB, i % TB)
                    if i >= LAG:
                        j = i - LAG
                        second(g * Q + j // TB, j // TB, j % TB)
                pe.wait_ge(fc1_used, g * (Q * TB) + (Q * TB + NGB))
                pe.sem_inc(fc2_done, 1)
                pe.wait_ge(px_copied, g + 2)
                pe.wait_ge(px_out, g + 1)
                for v in range(2):
                    mm = pe.transpose(bank[7][:, v * P:(v + 1) * P], pxs[:, v * P:(v + 1) * P], ident[:])
                mm.then_inc(px_turned, 1)

        def scalar_head(act):
            act.sem_inc(fc1_gelu, 4)

            def gelu(G, q, v):
                if v == 0:
                    act.wait_ge(e_loaded[q], G * 16 + 16)
                    act.sem_inc(waited[act.engine], 1)
                x = hf[q][:, v * 2048:(v + 1) * 2048]
                act.activation(x, x, ACT.Gelu, bias=shift[:], scale=scale[:]).then_inc(e_ready, 1)

            def hidden(n, t):
                act.wait_ge(fc1_done, n * TB + (TB * Q + t + 1))
                act.wait_ge(fc1_used, n * TB + (t + 1))
                act.activation(gb[t % NGB], bank[t % 4][:], ACT.Gelu, bias=fc1b[:]).then_inc(fc1_gelu, 1)

            def group(g, last):
                for q in range(Q):
                    for t in range(TB):
                        hidden(g * Q + q, t)
                        if t in (4, 10) and (q < Q - 1 or not last):
                            v = (t - 4) // 6
                            if q < Q - 1:
                                gelu(g, q + 1, v)
                            else:
                                gelu(g + 1, 0, v)

            for v in range(2):
                gelu(0, 0, v)
            with act.Fori(0, NG - 1) as g:
                group(g, False)
            group(NG - 1, True)

        def vector_head(dve):
            dve.sem_inc(px_copied, 1)
            dve.sem_inc(px_out, 1)
            with dve.Fori(0, NG) as g:
                dve.wait_ge(fc2_done, g + 1)
                dve.tensor_copy(pxs, bank[6][:, 0:256]).then_inc(px_copied, 1)
                dve.wait_ge(px_turned, g + 1)
                dve.wait_ge(px_free, g + 1)
                dve.tensor_scalar(pxt.rearrange("p a b -> p (a b)"), bank[7][:, 0:256], fc2b[:], None, ALU.add).then_inc(px_out, 1)

        px_free = sem("px_free")

        def gpsimd_head(pool, tok):
            pool.sem_inc(px_free, 1)
            with pool.Fori(0, NG) as g:
                pool.wait_ge(px_out, g + 2)
                pool.dma_start(tok[bass.ds(g * 256, 256), :].rearrange("(v p) x -> p v x", v=2), pxt).then_inc(tok_stored, 16)
                pool.wait_ge(tok_stored, g * 16 + 16)
                pool.sem_inc(px_free, 1)
            pool.wait_ge(tok_stored, NG * 16)

        tok = nc.dram_tensor("tok", [B * S, S], F32, kind="Internal").ap().rearrange("(a two) x -> a (two x)", two=2)

        NT = B * S // P
        TG = NT // 4
        HD, HEADS, MEM = 32, 4, 4
        HID = HEADS * HD
        E0, E1 = 8, 16
        EB = 8

        h_tok = at(0, NT, C)
        x_tok = at(NT * C, NT, C)
        o_tok = at(2 * NT * C, NT, C)
        sq = at(3 * NT * C, NT, C)
        TO = 4 * NT * C
        xT_all = at(TO, B * S, parts=C)
        red = at(TO + B * S, 8, NT)
        TO += B * S + 8 * NT
        wqkv = at(TO, 3 * HID, parts=C); TO += 3 * HID
        w_out = at(TO, C); TO += C
        gpre_b = at(TO, C); TO += C
        gout_b = at(TO, C); TO += C
        bout_b = at(TO, C); TO += C
        memk = at(TO, MEM); TO += MEM
        memk_max = at(TO, 4); TO += 4
        headmask = at(TO, HID); TO += HID
        wg = [at(TO, E0, parts=C), at(TO + E0, E1, parts=C)]; TO += E0 + E1
        bg_b = [at(TO, E0), at(TO + E0, E1)]; TO += E0 + E1
        w1 = [at(TO, E0 * 2, P, parts=C), at(TO + E0 * 2 * P, E1, P, parts=C)]; TO += 2 * E0 * 2 * P
        b1 = [at(TO, 16), at(TO + 16, 16)]; TO += 32
        w2 = [at(TO, 16, C), at(TO + 16 * C, 16, C)]; TO += 32 * C
        b2_b = [at(TO, E0 * C), at(TO + E0 * C, E1 * C)]; TO += (E0 + E1) * C
        wqT, wkT, wvT, woT = (at(TO + i * C, C, parts=C) for i in range(4)); TO += 4 * C
        wqk0 = at(TO, 2, parts=C); TO += 2
        bqk0_b = at(TO, 2); TO += 2
        bq_c, bk_c = at(TO, 1, parts=C), at(TO + 1, 1, parts=C); TO += 2
        bv_b, bo_b, gamma_b, beta_b = (at(TO + i * C, C) for i in range(4)); TO += 4 * C
        rank = at(TO, E1); TO += E1
        xg = at(TO, 4, C); TO += 4 * C
        xT = at(TO, BK, parts=C); TO += BK
        work = TO

        tok_loaded, ln_step, rms_step, attn_step = sem("tok_loaded"), sem("ln_step"), sem("rms_step"), sem("attn_step")
        gate_step, top_step, self_step = sem("gate_step"), sem("top_step"), sem("self_step")

        def steps(*names):
            return {n: i + 2 for i, n in enumerate(names)}, len(names)

        def over_c(v):
            return v.unsqueeze(2).to_broadcast([P, NT, C])

        def row4(v, n=4, w=C):
            return v.unsqueeze(1).to_broadcast([v.shape[0], n, w])

        def sync_load_tokens(sp):
            load = lambda dst, src: sp.dma_start(dst, src).then_inc(tok_loaded, 16)
            row = lambda name: d[name].rearrange("(a c) -> a c", a=1)
            load(h_tok, tok.rearrange("a (two x) -> (a two) x", two=2).rearrange("(t p) c -> p t c", p=P))
            load(wqkv, d["w_qkv"])
            load(w_out, d["w_out"])
            load(gpre_b, row("g_pre").to_broadcast([P, C]))
            load(gout_b, row("g_out").to_broadcast([P, C]))
            load(bout_b, row("b_out").to_broadcast([P, C]))
            load(memk, d["mem_k"])
            for u in range(2):
                load(vmem[u], d["mem_v"].unsqueeze(1).to_broadcast([MEM, GI // 2, HID]))
            load(headmask, d["c_headmask"])
            load(rank, d["c_rank"].to_broadcast([P, E1]))
            for m in range(2):
                load(wg[m], d[f"wg{m}"])
                load(bg_b[m], row(f"bg{m}").to_broadcast([P, (E0, E1)[m]]))
                load(w1[m], d[f"w1_{m}"])
                load(b1[m], d[f"b1_{m}"])
                load(w2[m], d[f"w2_{m}"])
                load(b2_b[m], row(f"b2_{m}").to_broadcast([P, (E0, E1)[m] * C]))
            for dst, name in ((wqT, "wq_t"), (wkT, "wk_t"), (wvT, "wv_t"), (woT, "wo_t")):
                load(dst, d[name])
            load(wqk0, d["wqk0"])
            load(bqk0_b, row("bqk0").to_broadcast([P, 2]))
            load(bq_c, d["bq"].rearrange("(c a) -> c a", a=1))
            load(bk_c, d["bk"].rearrange("(c a) -> c a", a=1))
            for dst, name in ((bv_b, "bv"), (bo_b, "bo"), (gamma_b, "ln_gamma"), (beta_b, "ln_beta")):
                load(dst, row(name).to_broadcast([P, C]))

        N_TOK = 16 * (7 + 2 + 2 + 12 + 4 + 2 + 2 + 4)

        LN, NLN = steps("sum", "mean", "centre", "square", "sumsq", "var", "root", "inverse", "scale")

        def vector_norm(dve, k, src, dst):
            base = k * NLN
            dve.tensor_reduce(red[:, 0, :], src, AX.X, ALU.add).then_inc(ln_step, 1)
            dve.wait_ge(ln_step, base + LN["sum"])
            dve.tensor_scalar(red[:, 1, :], red[:, 0, :], -1.0 / C, None, ALU.mult).then_inc(ln_step, 1)
            dve.wait_ge(ln_step, base + LN["mean"])
            dve.tensor_tensor(dst, src, over_c(red[:, 1, :]), ALU.add).then_inc(ln_step, 1)
            dve.wait_ge(ln_step, base + LN["centre"])
            dve.tensor_tensor(sq, dst, dst, ALU.mult).then_inc(ln_step, 1)
            dve.wait_ge(ln_step, base + LN["square"])
            dve.tensor_reduce(red[:, 2, :], sq, AX.X, ALU.add).then_inc(ln_step, 1)
            dve.wait_ge(ln_step, base + LN["sumsq"])
            dve.tensor_scalar(red[:, 3, :], red[:, 2, :], 1.0 / C, EPS, ALU.mult, ALU.add).then_inc(ln_step, 1)
            dve.wait_ge(ln_step, base + LN["root"])
            dve.reciprocal(red[:, 5, :], red[:, 4, :]).then_inc(ln_step, 1)
            dve.wait_ge(ln_step, base + LN["inverse"])
            dve.tensor_tensor(dst, dst, over_c(red[:, 5, :]), ALU.mult).then_inc(ln_step, 1)
            dve.wait_ge(ln_step, base + LN["scale"])

        def scalar_norm(act, k):
            act.wait_ge(ln_step, k * NLN + LN["var"])
            act.activation(red[:, 4, :], red[:, 3, :], ACT.Sqrt).then_inc(ln_step, 1)

        RMS, NRMS = steps("square", "sumsq", "root", "floor", "inverse", "scale")

        def vector_rms(dve, k, src):
            base = k * NRMS
            dve.tensor_tensor(sq, src, src, ALU.mult).then_inc(rms_step, 1)
            dve.wait_ge(rms_step, base + RMS["square"])
            dve.tensor_reduce(red[:, 2, :], sq, AX.X, ALU.add).then_inc(rms_step, 1)
            dve.wait_ge(rms_step, base + RMS["root"])
            dve.tensor_scalar(red[:, 5, :], red[:, 4, :], 1e-12, None, ALU.max).then_inc(rms_step, 1)
            dve.wait_ge(rms_step, base + RMS["floor"])
            dve.reciprocal(red[:, 6, :], red[:, 5, :]).then_inc(rms_step, 1)
            dve.wait_ge(rms_step, base + RMS["inverse"])
            dve.tensor_scalar(red[:, 7, :], red[:, 6, :], float(C) ** 0.5, None, ALU.mult).then_inc(rms_step, 1)
            dve.wait_ge(rms_step, base + RMS["scale"])

        def scalar_rms(act, k):
            act.wait_ge(rms_step, k * NRMS + RMS["sumsq"])
            act.activation(red[:, 4, :], red[:, 2, :], ACT.Sqrt).then_inc(rms_step, 1)

        A, NA = steps("xr", "xn", "turn", "xT", "proj", "k_max", "k_top", "k_sub", "k_exp", "k_sum", "k_inv", "kT", "kT_copy",
                      "ctx", "ctx_scale", "ctx_mask", "q_max", "q_sub", "q_exp", "q_sum", "q_inv", "q_scale", "q_norm",
                      "qT", "qT_copy", "att", "att_copy", "out", "out_bias")
        W = work
        vkv = [at(W + i * 512, 4, HID) for i in range(2)]; W += 1024
        vmem = [v[C:C + MEM] for v in vkv]
        ke = at(W, GI, C + MEM); W += GI * (C + MEM)
        kst = at(W, 4, GI); W += 4 * GI
        kTs = at(W, GI, HID, parts=C + MEM); W += GI * HID
        ctx_s = at(W, GI, HID); W += GI * HID
        qs = at(W, 4, HID); W += 4 * HID
        qst = at(W, 4, 16); W += 64
        qT = at(W, BK); W += BK
        attT = at(W, BK); W += BK
        SCALE = HD ** -0.5

        def tensor_attention(pe):
            with pe.Fori(0, TG) as g:
                def at_(s):
                    pe.wait_ge(attn_step, g * NA + A[s])
                    pe.sem_inc(waited[pe.engine], 1)

                at_("xn")
                for t in range(4):
                    mm = pe.transpose(bank[0][0:C, t * P:(t + 1) * P], xg[:, t, :], ident[:])
                mm.then_inc(attn_step, 1)
                at_("xT")
                pe.matmul(bank[1][:], wqkv[:, HID:2 * HID], xT, start=True, stop=True)
                for t in range(4):
                    pe.matmul(bank[2][:, t * P:(t + 1) * P], xT[:, t * P:(t + 1) * P], wqkv[:, 0:HID], start=True, stop=True)
                for b in range(GI):
                    mm = pe.matmul(bank[3 + b // 4][0:C, b % 4 * HID:(b % 4 + 1) * HID], xT[:, b * S:(b + 1) * S],
                                   wqkv[:, 2 * HID:3 * HID], start=True, stop=True)
                mm.then_inc(attn_step, 1)
                at_("k_inv")
                for b in range(GI):
                    mm = pe.transpose(bank[5 + b // 4][0:C + MEM, b % 4 * HID:(b % 4 + 1) * HID], ke[:, b, :], ident[:])
                mm.then_inc(attn_step, 1)
                at_("kT_copy")
                for b in range(GI):
                    mm = pe.matmul(bank[3 + b // 4][:, b % 4 * HID:(b % 4 + 1) * HID], kTs[:, b, :], vkv[b // 4][0:C + MEM, b % 4, :],
                                   start=True, stop=True)
                mm.then_inc(attn_step, 1)
                at_("q_norm")
                for t in range(4):
                    mm = pe.transpose(bank[7][:, t * P:(t + 1) * P], qs[:, t, :], ident[:])
                mm.then_inc(attn_step, 1)
                at_("qT_copy")
                for b in range(GI):
                    mm = pe.matmul(bank[1][:, b * S:(b + 1) * S], ctx_s[:, b, :], qT[:, b * S:(b + 1) * S], start=True, stop=True)
                mm.then_inc(attn_step, 1)
                at_("att_copy")
                for t in range(4):
                    mm = pe.matmul(bank[0][:, t * C:(t + 1) * C], attT[:, t * P:(t + 1) * P], w_out, start=True, stop=True)
                mm.then_inc(attn_step, 1)

        def scalar_attention(act):
            with act.Fori(0, TG) as g:
                at_ = lambda s: act.wait_ge(attn_step, g * NA + A[s])
                at_("turn")
                act.activation(xT, bank[0][0:C, :], ACT.Copy).then_inc(attn_step, 1)
                at_("k_sub")
                act.activation(ke, ke, ACT.Exp).then_inc(attn_step, 1)
                at_("kT")
                for i in range(2):
                    c = act.activation(kTs[:, 4 * i:4 * i + 4, :], bank[5 + i][0:C + MEM, :].rearrange("p (b x) -> p b x", b=4), ACT.Copy)
                c.then_inc(attn_step, 1)
                at_("q_sub")
                act.activation(qs, qs, ACT.Exp).then_inc(attn_step, 1)
                at_("qT")
                act.activation(qT, bank[7][:], ACT.Copy).then_inc(attn_step, 1)
                at_("att")
                act.activation(attT, bank[1][:], ACT.Copy).then_inc(attn_step, 1)

        def vector_attention(dve):
            dve.wait_ge(tok_loaded, N_TOK)
            dve.tensor_reduce(memk_max[:, 0:1], memk, AX.X, ALU.max).then_inc(attn_step, 1)
            vector_norm(dve, 0, h_tok, x_tok)
            vector_rms(dve, 0, x_tok)
            with dve.Fori(0, TG) as g:
                at_ = lambda s: dve.wait_ge(attn_step, g * NA + A[s])

                def then(ins):
                    ins.then_inc(attn_step, 1)

                dve.wait_ge(attn_step, g * NA + 1)
                then(dve.tensor_tensor(xg, x_tok[:, bass.ds(g * 4, 4), :],
                                       red[:, 7, bass.ds(g * 4, 4)].unsqueeze(2).to_broadcast([P, 4, C]), ALU.mult))
                at_("xr")
                then(dve.tensor_tensor(xg, xg, row4(gpre_b), ALU.mult))
                at_("proj")
                for i in range(2):
                    dve.tensor_copy(vkv[i][0:C], bank[3 + i][0:C, :].rearrange("p (b x) -> p b x", b=4))
                k = bank[1][:].rearrange("p (b n) -> p b n", b=GI)
                then(dve.tensor_reduce(kst[:, 0, :], k, AX.X, ALU.max))
                at_("k_max")
                then(dve.tensor_scalar(kst[:, 1, :], kst[:, 0, :], memk_max[:, 0:1], None, ALU.max))
                at_("k_top")
                dve.tensor_tensor(ke[:, :, C:C + MEM], memk.unsqueeze(1).to_broadcast([P, GI, MEM]),
                                  kst[:, 1, :].unsqueeze(2).to_broadcast([P, GI, MEM]), ALU.subtract)
                then(dve.tensor_tensor(ke[:, :, 0:C], k, kst[:, 1, :].unsqueeze(2).to_broadcast([P, GI, C]), ALU.subtract))
                at_("k_exp")
                then(dve.tensor_reduce(kst[:, 2, :], ke, AX.X, ALU.add))
                at_("k_sum")
                then(dve.reciprocal(kst[:, 3, :], kst[:, 2, :]))
                at_("ctx")
                for i in range(2):
                    c = dve.tensor_tensor(ctx_s[:, 4 * i:4 * i + 4, :], bank[3 + i][:].rearrange("p (b x) -> p b x", b=4),
                                          kst[:, 3, 4 * i:4 * i + 4].unsqueeze(2).to_broadcast([P, 4, HID]), ALU.mult)
                then(c)
                at_("ctx_scale")
                then(dve.tensor_tensor(ctx_s, ctx_s, row4(headmask, GI, HID), ALU.mult))
                at_("ctx_mask")
                q = bank[2][:].rearrange("p (a e) -> p a e", e=HD)
                q_s = qs.rearrange("p t (a e) -> p (t a) e", e=HD)
                then(dve.tensor_reduce(qst[:, 0, :], q, AX.X, ALU.max))
                at_("q_max")
                then(dve.tensor_tensor(q_s, q, qst[:, 0, :].unsqueeze(2).to_broadcast([P, 16, HD]), ALU.subtract))
                at_("q_exp")
                then(dve.tensor_reduce(qst[:, 1, :], q_s, AX.X, ALU.add))
                at_("q_sum")
                then(dve.reciprocal(qst[:, 2, :], qst[:, 1, :]))
                at_("q_inv")
                then(dve.tensor_scalar(qst[:, 3, :], qst[:, 2, :], SCALE, None, ALU.mult))
                at_("q_scale")
                then(dve.tensor_tensor(q_s, q_s, qst[:, 3, :].unsqueeze(2).to_broadcast([P, 16, HD]), ALU.mult))
                at_("out")
                then(dve.tensor_tensor(o_tok[:, bass.ds(g * 4, 4), :], bank[0][:, 0:4 * C].rearrange("p (t c) -> p t c", t=4),
                                       row4(bout_b), ALU.add))
            dve.wait_ge(attn_step, TG * NA + 1)
            vector_rms(dve, 1, o_tok)
            for i, (a, b) in enumerate(((o_tok, over_c(red[:, 7, :])), (o_tok, row4(gout_b, NT)))):
                dve.tensor_tensor(a, a, b, ALU.mult).then_inc(attn_step, 1)
                dve.wait_ge(attn_step, TG * NA + i + 2)
            dve.tensor_tensor(o_tok, o_tok, x_tok, ALU.add).then_inc(attn_step, 1)
            dve.wait_ge(attn_step, TG * NA + 4)
            dve.tensor_tensor(h_tok, h_tok, o_tok, ALU.add).then_inc(attn_step, 1)
            dve.wait_ge(attn_step, TG * NA + 5)

        ME = (E0, E1)
        HT = (2, 1)
        SETS = (1, 2)
        G, NGS = steps("xg", "turn", "xT", "all", "gate", "score")
        T_, NTS = steps("m1", "eq1", "rk1", "top1", "oh1", "keep", "rest", "low", "m2", "eq2", "rk2", "top2", "oh2",
                        "diff", "p", "p1", "r1", "r2", "c1", "c2", "comb")
        W = work
        score, s2, oh1, oh2, tw = (at(W + i * NT * E1, NT, E1) for i in range(5)); W += 5 * NT * E1
        comb = at(W, NT, E1); W += NT * E1
        tp = at(W, 8, NT); W += 8 * NT
        hid = [at(W + i * BK, BK) for i in range(4)]; W += 4 * BK
        ys = [at(W + i * BK, EB, C) for i in range(4)]; W += 4 * BK
        yr = at(W, 4, C); W += 4 * C
        hid_done, hid_ready, y_sum, y_taken, y_step = (
            sem("hid_done"), sem("hid_ready"), sem("y_sum"), sem("y_taken"), sem("y_step"))
        ex_used = sem("ex_used")

        def tensor_gate(pe, m):
            with pe.Fori(0, TG) as g:
                def at_(s):
                    pe.wait_ge(gate_step, (m * TG + g) * NGS + G[s])
                    pe.sem_inc(waited[pe.engine], 1)

                at_("xg")
                for t in range(4):
                    mm = pe.transpose(bank[0][0:C, t * P:(t + 1) * P], xg[:, t, :], ident[:])
                mm.then_inc(gate_step, 1)
                at_("all")
                for t in range(4):
                    mm = pe.matmul(bank[1][:, t * ME[m]:(t + 1) * ME[m]], xT[:, t * P:(t + 1) * P], wg[m], start=True, stop=True)
                mm.then_inc(gate_step, 1)

        def scalar_gate(act, m):
            with act.Fori(0, TG) as g:
                act.wait_ge(gate_step, (m * TG + g) * NGS + G["turn"])
                act.activation(xT, bank[0][0:C, :], ACT.Copy).then_inc(gate_step, 1)

        def vector_gate(dve, m):
            with dve.Fori(0, TG) as g:
                base = (m * TG + g) * NGS
                dve.wait_ge(gate_step, base + 1)
                dve.tensor_scalar(xg, x_tok[:, bass.ds(g * 4, 4), :], 1.0, None, ALU.mult).then_inc(gate_step, 1)
                dve.wait_ge(gate_step, base + G["xT"])
                dve.tensor_scalar(xT_all[:, bass.ds(g * BK, BK)], bank[0][0:C, :], 1.0, None, ALU.mult).then_inc(gate_step, 1)
                dve.wait_ge(gate_step, base + G["gate"])
                dve.tensor_tensor(score[:, bass.ds(g * 4, 4), 0:ME[m]], bank[1][:, 0:4 * ME[m]].rearrange("p (t e) -> p t e", t=4),
                                  row4(bg_b[m], 4, ME[m]), ALU.add).then_inc(gate_step, 1)

        def vector_top2(dve, m):
            E = ME[m]
            base = m * NTS
            f = lambda v: v[:, :, 0:E]
            e = lambda v: v.unsqueeze(2).to_broadcast([P, NT, E])
            sc, lo, o1, o2, w, cb = (f(v) for v in (score, s2, oh1, oh2, tw, comb))
            rk = rank[:, 0:E].unsqueeze(1).to_broadcast([P, NT, E])
            at_ = lambda s: dve.wait_ge(top_step, base + T_[s])
            then = lambda ins: ins.then_inc(top_step, 1)

            def pick(s, one, i, n):
                then(dve.tensor_reduce(tp[:, i, :], s, AX.X, ALU.max))
                at_("m" + n)
                then(dve.tensor_tensor(one, s, e(tp[:, i, :]), ALU.is_equal))
                at_("eq" + n)
                then(dve.tensor_tensor(w, one, rk, ALU.mult))
                at_("rk" + n)
                then(dve.tensor_reduce(tp[:, 2, :], w, AX.X, ALU.max))
                at_("top" + n)
                then(dve.tensor_tensor(one, w, e(tp[:, 2, :]), ALU.is_equal))
                at_("oh" + n)

            pick(sc, o1, 0, "1")
            then(dve.tensor_scalar(w, o1, -1.0, 1.0, ALU.mult, ALU.add))
            at_("keep")
            then(dve.tensor_tensor(lo, sc, w, ALU.mult))
            at_("rest")
            then(dve.scalar_tensor_tensor(out=lo, in0=o1, scalar=-3.0e38, in1=lo, op0=ALU.mult, op1=ALU.add))
            at_("low")
            pick(lo, o2, 1, "2")
            then(dve.tensor_tensor(tp[:, 3, :], tp[:, 1, :], tp[:, 0, :], ALU.subtract))
            at_("p")
            then(dve.tensor_scalar(tp[:, 5, :], tp[:, 4, :], 1.0, None, ALU.add))
            at_("p1")
            then(dve.reciprocal(tp[:, 6, :], tp[:, 5, :]))
            at_("r1")
            then(dve.tensor_tensor(tp[:, 7, :], tp[:, 4, :], tp[:, 6, :], ALU.mult))
            at_("r2")
            then(dve.tensor_tensor(w, o1, e(tp[:, 6, :]), ALU.mult))
            at_("c1")
            then(dve.tensor_tensor(lo, o2, e(tp[:, 7, :]), ALU.mult))
            at_("c2")
            then(dve.tensor_tensor(cb, w, lo, ALU.add))
            at_("comb")

        def scalar_top2(act, m):
            act.wait_ge(top_step, m * NTS + T_["diff"])
            act.activation(tp[:, 4, :], tp[:, 3, :], ACT.Exp).then_inc(top_step, 1)

        HIDN = (EB * HT[0], EB * HT[1])
        H0 = (0, TG * SETS[0] * HIDN[0])
        Y0 = (0, TG * SETS[0] * 4)

        def tensor_experts(pe, m):
            if m == 0:
                pe.sem_inc(hid_done, 0 + 0 + 1)
                pe.sem_inc(ex_used, 4)
            pe.wait_ge(top_step, m * NTS + T_["comb"])
            N = HIDN[m]
            with pe.Fori(0, TG) as g:
                for s in range(SETS[m]):
                    hb = (g * SETS[m] + s) * N + H0[m]
                    yb = (g * SETS[m] + s) * 4 + Y0[m]

                    def second(i):
                        e, j = i // HT[m], i % HT[m]
                        pe.wait_ge(hid_ready, hb + (i + 5))
                        for t in range(4):
                            if i == 0:
                                pe.wait_ge(y_taken, yb + (t + 1))
                            mm = pe.matmul(bank[4 + t][:, e * C:(e + 1) * C], hid[i % 4][:, t * P:(t + 1) * P],
                                           w2[m][:, (s * EB + e) * HT[m] + j, :], start=(j == 0), stop=(j == HT[m] - 1))
                        mm.then_inc(ex_used, 1)

                    for i in range(N + 2):
                        if i < N:
                            pe.wait_ge(hid_ready, hb + (i + 1))
                            pe.sem_inc(waited[pe.engine], 1)
                            pe.matmul(bank[i % 4][:], w1[m][:, s * N + i, :], xT_all[:, bass.ds(g * BK, BK)],
                                      start=True, stop=True).then_inc(hid_done, 1)
                        if i >= 2:
                            second(i - 2)
                    pe.wait_ge(ex_used, hb + (N + 4))
                    pe.sem_inc(y_sum, 1)

        def scalar_experts(act, m):
            if m == 0:
                act.sem_inc(hid_ready, 4)
            N = HIDN[m]
            with act.Fori(0, TG) as g:
                for s in range(SETS[m]):
                    hb = (g * SETS[m] + s) * N + H0[m]
                    for i in range(N):
                        act.wait_ge(hid_done, hb + (i + 2))
                        act.wait_ge(ex_used, hb + (i + 1))
                        act.activation(hid[i % 4], bank[i % 4][:], ACT.Relu, bias=b1[m][:, s * N + i:s * N + i + 1]).then_inc(hid_ready, 1)

        def vector_experts(dve, m):
            if m == 0:
                dve.sem_inc(y_taken, 4)
                dve.sem_inc(y_step, 1)
            with dve.Fori(0, TG) as g:
                for s in range(SETS[m]):
                    yb = (g * SETS[m] + s) * 4 + Y0[m]
                    st_ = ((g * SETS[m] + s) + (0, TG * SETS[0])[m]) * 3
                    dve.wait_ge(y_sum, (g * SETS[m] + s) + ((0, TG * SETS[0])[m] + 1))
                    for t in range(4):
                        dve.tensor_tensor(ys[t], bank[4 + t][:].rearrange("p (e c) -> p e c", e=EB),
                                          b2_b[m][:, s * EB * C:(s + 1) * EB * C].rearrange("p (e c) -> p e c", e=EB),
                                          ALU.add).then_inc(y_taken, 1)
                    dve.wait_ge(y_taken, yb + 8)
                    for t in range(4):
                        c = dve.tensor_tensor(ys[t], ys[t], comb[:, bass.ds(g * 4 + t, 1), s * EB:(s + 1) * EB].rearrange("p a e -> p (a e)")
                                              .unsqueeze(2).to_broadcast([P, EB, C]), ALU.mult)
                    c.then_inc(y_step, 1)
                    dve.wait_ge(y_step, st_ + 2)
                    for t in range(4):
                        c = dve.tensor_reduce(yr[:, t, :], ys[t].rearrange("p e c -> p c e"), AX.X, ALU.add)
                    c.then_inc(y_step, 1)
                    dve.wait_ge(y_step, st_ + 3)
                    o = o_tok[:, bass.ds(g * 4, 4), :]
                    if s == 0:
                        c = dve.tensor_scalar(o, yr, 1.0, None, ALU.mult)
                    else:
                        c = dve.tensor_tensor(o, o, yr, ALU.add)
                    c.then_inc(y_step, 1)
                    dve.wait_ge(y_step, st_ + 4)
                    dve.sem_inc(waited[dve.engine], 1)

        F, NF = steps("xg", "turn", "xT", "proj", "qT", "kT", "v", "zero_sum", "zero_test", "mask", "score", "s_max", "s_sub", "s_exp",
                      "s_sum", "s_inv", "s_mask", "s_norm", "pT", "pT_copy", "att", "att_copy", "out", "bias", "add")
        W = work
        qT1, kT1 = at(W, BK, parts=C), at(W + BK, BK, parts=C); W += 2 * BK
        v1 = at(W, GI, C, parts=C); W += GI * C
        zt = at(W, 4, 2); W += 8
        mk = at(W, 4); W += 4
        pr = at(W, 4, C); W += 4 * C
        ps_ = at(W, 4, 4); W += 16
        pT = at(W, BK, parts=C); W += BK
        oT = at(W, BK, parts=C); W += BK
        ob = at(W, 4, C); W += 4 * C

        def tensor_self(pe):
            with pe.Fori(0, TG) as g:
                def at_(s):
                    pe.wait_ge(self_step, g * NF + F[s])
                    pe.sem_inc(waited[pe.engine], 1)

                at_("xg")
                for t in range(4):
                    mm = pe.transpose(bank[0][0:C, t * P:(t + 1) * P], xg[:, t, :], ident[:])
                mm.then_inc(self_step, 1)
                at_("xT")
                pe.matmul(bank[1][0:C, :], wqT, xT, start=True, stop=True)
                pe.matmul(bank[2][0:C, :], wkT, xT, start=True, stop=True)
                for b in range(GI):
                    pe.matmul(bank[3][0:C, b * C:(b + 1) * C], xT[:, b * S:(b + 1) * S], wvT, start=True, stop=True)
                for t in range(4):
                    mm = pe.matmul(bank[4][:, 2 * t:2 * t + 2], xT[:, t * P:(t + 1) * P], wqk0, start=True, stop=True)
                mm.then_inc(self_step, 1)
                at_("mask")
                for b in range(GI):
                    hp = slice(b % 2 * C, (b % 2 + 1) * C)
                    mm = pe.matmul(bank[5][hp, b // 2 * C:(b // 2 + 1) * C], qT1[:, b * S:(b + 1) * S], kT1[:, b * S:(b + 1) * S],
                                   start=True, stop=True)
                mm.then_inc(self_step, 1)
                at_("s_norm")
                for t in range(4):
                    mm = pe.transpose(bank[6][0:C, t * P:(t + 1) * P], pr[:, t, :], ident[:])
                mm.then_inc(self_step, 1)
                at_("pT_copy")
                for b in range(GI):
                    mm = pe.matmul(bank[7][0:C, b * S:(b + 1) * S], v1[:, b, :], pT[:, b * S:(b + 1) * S], start=True, stop=True)
                mm.then_inc(self_step, 1)
                at_("att_copy")
                for t in range(4):
                    mm = pe.matmul(bank[0][:, t * C:(t + 1) * C], oT[:, t * P:(t + 1) * P], woT, start=True, stop=True)
                mm.then_inc(self_step, 1)

        def scalar_self(act):
            with act.Fori(0, TG) as g:
                at_ = lambda s: act.wait_ge(self_step, g * NF + F[s])
                at_("turn")
                act.activation(xT, bank[0][0:C, :], ACT.Copy).then_inc(self_step, 1)
                at_("proj")
                act.activation(qT1, bank[1][0:C, :], ACT.Identity, bias=bq_c).then_inc(self_step, 1)
                at_("s_sub")
                act.activation(pr, pr, ACT.Exp, scale=float(C) ** -0.5).then_inc(self_step, 1)
                at_("pT")
                act.activation(pT, bank[6][0:C, :], ACT.Copy).then_inc(self_step, 1)
                at_("att")
                act.activation(oT, bank[7][0:C, :], ACT.Copy).then_inc(self_step, 1)

        def vector_self(dve):
            with dve.Fori(0, TG) as g:
                at_ = lambda s: dve.wait_ge(self_step, g * NF + F[s])
                then = lambda ins: ins.then_inc(self_step, 1)
                dve.wait_ge(self_step, g * NF + 1)
                then(dve.tensor_scalar(xg, x_tok[:, bass.ds(g * 4, 4), :], 1.0, None, ALU.mult))
                at_("qT")
                then(dve.tensor_scalar(kT1, bank[2][0:C, :], bk_c, None, ALU.add))
                at_("kT")
                then(dve.tensor_tensor(v1, bank[3][0:C, :].rearrange("p (b c) -> p b c", b=GI), row4(bv_b[0:C], GI), ALU.add))
                at_("v")
                then(dve.tensor_tensor(zt, bank[4][:, 0:8].rearrange("p (t a) -> p t a", t=4), row4(bqk0_b, 4, 2), ALU.add))
                at_("zero_sum")
                then(dve.tensor_scalar(zt, zt, 0.0, None, ALU.not_equal))
                at_("zero_test")
                then(dve.tensor_tensor(mk, zt[:, :, 0], zt[:, :, 1], ALU.mult))
                at_("score")
                sc = bank[5][:, 0:4 * C].rearrange("p (t j) -> p t j", t=4)
                then(dve.tensor_reduce(ps_[:, 0, :], sc, AX.X, ALU.max))
                at_("s_max")
                then(dve.tensor_tensor(pr, sc, ps_[:, 0, :].unsqueeze(2).to_broadcast([P, 4, C]), ALU.subtract))
                at_("s_exp")
                then(dve.tensor_reduce(ps_[:, 1, :], pr, AX.X, ALU.add))
                at_("s_sum")
                then(dve.reciprocal(ps_[:, 2, :], ps_[:, 1, :]))
                at_("s_inv")
                then(dve.tensor_tensor(ps_[:, 3, :], ps_[:, 2, :], mk, ALU.mult))
                at_("s_mask")
                then(dve.tensor_tensor(pr, pr, ps_[:, 3, :].unsqueeze(2).to_broadcast([P, 4, C]), ALU.mult))
                at_("out")
                then(dve.tensor_tensor(ob, bank[0][:, 0:4 * C].rearrange("p (t c) -> p t c", t=4), row4(bo_b), ALU.add))
                at_("bias")
                hg = h_tok[:, bass.ds(g * 4, 4), :]
                then(dve.tensor_tensor(hg, hg, ob, ALU.add))
            dve.wait_ge(self_step, TG * NF + 1)

        fin_step, out_stored = sem("fin_step"), sem("out_stored")

        def tail_sync(sp):
            sync_load_tokens(sp)
            sp.wait_ge(fin_step, 6)
            sp.dma_start(out.rearrange("(t p) c -> p t c", p=P), h_tok).then_inc(out_stored, 16)
            sp.wait_ge(out_stored, 16)

        def tail_tensor(pe):
            pe.wait_ge(tok_loaded, N_TOK)
            tensor_attention(pe)
            for m in range(2):
                if m == 1:
                    tensor_self(pe)
                tensor_gate(pe, m)
                tensor_experts(pe, m)

        def tail_scalar(act):
            act.wait_ge(tok_loaded, N_TOK)
            scalar_norm(act, 0)
            scalar_rms(act, 0)
            scalar_attention(act)
            scalar_rms(act, 1)
            for m in range(2):
                if m == 1:
                    scalar_norm(act, 2)
                    scalar_self(act)
                scalar_norm(act, (1, 3)[m])
                scalar_gate(act, m)
                scalar_top2(act, m)
                scalar_experts(act, m)
            scalar_norm(act, 4)

        def tail_vector(dve):
            for s in (ln_step, rms_step, gate_step, top_step, self_step):
                dve.sem_inc(s, 1)
            vector_attention(dve)
            for m in range(2):
                if m == 1:
                    vector_norm(dve, 2, h_tok, x_tok)
                    vector_self(dve)
                vector_norm(dve, (1, 3)[m], h_tok, x_tok)
                vector_gate(dve, m)
                dve.wait_ge(gate_step, (m + 1) * (TG * NGS) + 1)
                vector_top2(dve, m)
                vector_experts(dve, m)
                dve.wait_ge(y_step, (TG * SETS[0] * 3, TG * (SETS[0] + SETS[1]) * 3)[m] + 1)
                if m == 0:
                    dve.tensor_tensor(h_tok, h_tok, o_tok, ALU.add).then_inc(fin_step, 1)
                    dve.wait_ge(fin_step, 1)
            dve.tensor_tensor(x_tok, x_tok, o_tok, ALU.add).then_inc(fin_step, 1)
            dve.wait_ge(fin_step, 2)
            vector_norm(dve, 4, x_tok, o_tok)
            dve.tensor_tensor(o_tok, o_tok, row4(gamma_b, NT), ALU.mult).then_inc(fin_step, 1)
            dve.wait_ge(fin_step, 3)
            dve.tensor_tensor(o_tok, o_tok, row4(beta_b, NT), ALU.add).then_inc(fin_step, 1)
            dve.wait_ge(fin_step, 4)
            dve.tensor_tensor(h_tok, h_tok, o_tok, ALU.add).then_inc(fin_step, 2)

        block = ctx.enter_context(nc.Block())
        TOWER = 3 * L

        @block.sync
        def _(sp):
            sync_spectrum0(sp)
            phase_end(sp, 1)
            sync_mix(sp, 0, True)
            phase_end(sp, 2)
            sync_inverse(sp, 0, True)
            phase_end(sp, 3)
            with sp.Fori(1, L) as l:
                sync_forward(sp, l - 1, False)
                phase_end(sp, l * 3 + 1)
                sync_mix(sp, l, False)
                phase_end(sp, l * 3 + 2)
                sync_inverse(sp, l, False)
                phase_end(sp, l * 3 + 3)
            sync_head(sp)
            phase_end(sp, TOWER + 1)
            tail_sync(sp)

        @block.tensor
        def _(pe):
            tensor_spectrum0(pe)
            phase_end(pe, 1)
            tensor_mix(pe, 0, True)
            phase_end(pe, 2)
            tensor_inverse(pe, 0, True)
            pe.sem_inc(ht_done, 8 * Q)
            phase_end(pe, 3)
            with pe.Fori(1, L) as l:
                tensor_forward(pe, l - 1)
                phase_end(pe, l * 3 + 1)
                tensor_mix(pe, l, False)
                phase_end(pe, l * 3 + 2)
                tensor_inverse(pe, l, False)
                phase_end(pe, l * 3 + 3)
            tensor_head(pe)
            phase_end(pe, TOWER + 1)
            tail_tensor(pe)

        @block.scalar
        def _(act):
            scalar_spectrum0(act)
            phase_end(act, 1)
            scalar_mix(act, 0, True)
            phase_end(act, 2)
            scalar_inverse(act, 0, True)
            act.sem_inc(ft_copied, 2)
            for v in range(2):
                act.sem_inc(spec_stored[v], 64)
            phase_end(act, 3)
            with act.Fori(1, L) as l:
                scalar_forward(act, l - 1, False)
                phase_end(act, l * 3 + 1)
                scalar_mix(act, l, False)
                phase_end(act, l * 3 + 2)
                scalar_inverse(act, l, False)
                phase_end(act, l * 3 + 3)
            scalar_head(act)
            phase_end(act, TOWER + 1)
            tail_scalar(act)

        @block.vector
        def _(dve):
            vector_spectrum0(dve)
            phase_end(dve, 1)
            vector_mix(dve, 0, True)
            phase_end(dve, 2)
            vector_inverse(dve, 0, True)
            dve.sem_inc(ht_copied, 2)
            dve.sem_inc(fc_copied, 2)
            dve.sem_inc(fr_copied, 2)
            phase_end(dve, 3)
            with dve.Fori(1, L) as l:
                vector_forward(dve, l - 1)
                phase_end(dve, l * 3 + 1)
                vector_mix(dve, l, False)
                phase_end(dve, l * 3 + 2)
                vector_inverse(dve, l, False)
                phase_end(dve, l * 3 + 3)
            vector_head(dve)
            phase_end(dve, TOWER + 1)
            tail_vector(dve)

        @block.gpsimd
        def _(pool):
            gpsimd_spectrum0(pool)
            phase_end(pool, 1)
            gpsimd_mix(pool, 0)
            phase_end(pool, 2)
            gpsimd_inverse(pool, 0, True)
            phase_end(pool, 3)
            with pool.Fori(1, L) as l:
                phase_end(pool, l * 3 + 1)
                gpsimd_mix(pool, l)
                phase_end(pool, l * 3 + 2)
                gpsimd_inverse(pool, l, False)
                phase_end(pool, l * 3 + 3)
            gpsimd_head(pool, tok)
            phase_end(pool, TOWER + 1)
            pass


def block_layout(t, E, H):
    return np.ascontiguousarray(t.transpose(2, 0, 1).reshape(C, E * (H // P), P))


def kernel(x, **inputs):
    import concourse.bacc as bacc
    from concourse.bass_utils import run_bass_kernel_spmd as run

    v = {k: np.asarray(a) for k, a in inputs.items()}
    tower = {k[len("L0_tok_"):]: a for k, a in v.items() if k.startswith("L0_tok_")}
    arrays = dft_constants()
    arrays.update(tower_layout(x, *(tower[k] for k in ("fc0_w", "fc0_b", "w1r", "w1i", "w2r", "w2i", "pw_w"))))
    for k in ("pw_b", "gamma", "beta", "fc1_w", "fc1_b", "fc2_w", "fc2_b"):
        arrays[k] = tower[k]
    for k in ("w_qkv", "w_out", "b_out", "g_out", "g_pre"):
        arrays[k] = v["L0_attn_" + k]
    mem = v["L0_attn_mem_kv"]
    arrays["mem_k"] = np.ascontiguousarray(mem[0].reshape(P, -1))
    arrays["mem_v"] = np.ascontiguousarray(mem[1].reshape(P, -1).T)
    head = np.arange(P) // 32
    arrays["c_headmask"] = (head[:, None] == head[None, :]).astype(np.float32)
    arrays["c_rank"] = (16 - np.arange(16, dtype=np.float32))[None, :]
    arrays["wg0"] = np.ascontiguousarray(v["L0_ffn_Wg"].T)
    arrays["bg0"] = v["L0_ffn_bg"]
    W1, W2 = v["L0_ffn_W1"], v["L0_ffn_W2"]
    E, H, _ = W1.shape
    arrays["w1_0"] = block_layout(W1, E, H)
    arrays["b1_0"] = np.ascontiguousarray(v["L0_ffn_b1"].reshape(E * H // P, P).T)
    arrays["w2_0"] = np.ascontiguousarray(W2.transpose(0, 2, 1).reshape(E * H // P, P, C).transpose(1, 0, 2))
    arrays["b2_0"] = v["L0_ffn_b2"].reshape(-1)
    arrays["wg1"] = v["L1_ffn_gate_w"]
    arrays["bg1"] = v["L1_ffn_gate_b"]
    arrays["w1_1"] = np.ascontiguousarray(v["L1_ffn_w1"].transpose(1, 0, 2))
    arrays["b1_1"] = np.ascontiguousarray(v["L1_ffn_b1"].T)
    arrays["w2_1"] = np.ascontiguousarray(v["L1_ffn_w2"].transpose(1, 0, 2))
    arrays["b2_1"] = v["L1_ffn_b2"].reshape(-1)
    arrays["ln_gamma"], arrays["ln_beta"] = v["L1_ffn_gamma"], v["L1_ffn_beta"]
    for k in "qkvo":
        arrays[f"w{k}_t"] = np.ascontiguousarray(v["L1_attn_W" + k].T)
        arrays[f"b{k}"] = v["L1_attn_b" + k]
    arrays["wqk0"] = np.stack([v["L1_attn_Wq"][0], v["L1_attn_Wk"][0]], 1)
    arrays["bqk0"] = np.stack([v["L1_attn_bq"][0], v["L1_attn_bk"][0]])

    nc = bacc.Bacc("TRN2", target_bir_lowering=False, num_devices=1)
    d = {k: nc.dram_tensor("in_" + k, a.shape, F32, kind="ExternalInput").ap() for k, a in arrays.items()}
    B = x.shape[0]
    out = nc.dram_tensor("out", [B * S, S], F32, kind="ExternalOutput").ap()
    build(nc, d, B, out)
    r = run(nc, [{"in_" + k: a for k, a in arrays.items()}], core_ids=[0])
    return r.results[0]["out"].reshape(B, S, S)
```

```python
from contextlib import ExitStack

import numpy as np

import concourse.bass as bass
from concourse import mybir

F32 = mybir.dt.float32
ACT = mybir.ActivationFunctionType
ALU = mybir.AluOpType
AX = mybir.AxisListType

P = 128
C = 64
S = 64
PX = S * S
M1, M2 = 16, 16
K1 = 2 * M1
L = 4
CH = 4
NCH = K1 // CH
MC = CH * M2
Q = 4
GI = 2 * Q
BK = 512
EPS = 1e-5
ENGINES = 5


def dft_constants():
    h = np.arange(S)
    k1 = np.concatenate([np.arange(M1), np.arange(S - M1, S)])
    k2 = np.arange(M2)
    w_ang = 2 * np.pi * np.outer(h, k2) / S
    h_ang = 2 * np.pi * np.outer(h, k1) / S
    fw2 = np.kron(np.eye(2), np.stack([np.cos(w_ang), -np.sin(w_ang)], -1).reshape(S, 2 * M2))
    gh = np.block([[np.cos(h_ang), -np.sin(h_ang)], [np.sin(h_ang), np.cos(h_ang)]])
    ga = np.block([[np.cos(h_ang).T, np.sin(h_ang).T], [-np.sin(h_ang).T, np.cos(h_ang).T]]) / S
    ga = ga.reshape(2 * K1, 2, S)
    ga = np.stack([np.roll(ga, 2, axis=2), ga], 1)
    fb = np.stack([2 * np.cos(w_ang).T, -2 * np.sin(w_ang).T], 1)
    fb[0, 0], fb[0, 1] = 1.0, 0.0
    fb2 = np.kron(np.eye(2), fb.reshape(2 * M2, S) / S)
    g0 = np.stack([np.kron(np.eye(2), np.cos(h_ang)), np.kron(np.eye(2), -np.sin(h_ang))], 1)
    cs, sn = np.cos(w_ang), np.sin(w_ang)
    part = np.stack([np.stack([cs, -sn], 1), np.stack([sn, cs], 1)], 0)
    f0 = np.einsum("pwrk,ij->pwirjk", part, np.eye(3)).reshape(2, 2, 96, 6 * M2).transpose(2, 0, 1, 3)
    dc = np.zeros((1, K1))
    dc[0, 0] = PX
    consts = {"c_fw2": fw2, "c_gh": gh, "c_ga": ga.reshape(2 * K1, 4 * S), "c_fb2": fb2, "c_g0": g0.reshape(P, 4 * K1),
              "c_f0": f0.reshape(96, 4, 96), "c_dc": dc, "c_ident": np.eye(P),
              "c_half": np.kron(np.full((2, 2), 0.5), np.eye(C))}
    return {k: np.ascontiguousarray(v, dtype=np.float32) for k, v in consts.items()}


def tower_layout(x, fc0_w, fc0_b, w1r, w1i, w2r, w2i, pw_w):
    x, fc0_w, fc0_b, pw_w, w1r, w1i, w2r, w2i = (
        np.asarray(t) for t in (x, fc0_w, fc0_b, pw_w, w1r, w1i, w2r, w2i))
    B = x.shape[0]
    out = {}
    out["x_pair"] = np.ascontiguousarray(
        x.reshape(B // GI, 2, Q, PX, 3).transpose(0, 2, 1, 4, 3).reshape(B // 2, 6, PX))
    out["x_rows"] = np.ascontiguousarray(x.reshape(B // 2, 2 * S, S * 3))
    r, i = (np.concatenate(t, 3).reshape(L, C, C, NCH, MC).transpose(0, 3, 1, 4, 2)
            for t in ((w1r, w2r), (w1i, w2i)))
    out["w_modes"] = np.stack([r, i], 2).reshape(L, NCH, P, MC, C)
    out["pw_t"] = np.ascontiguousarray(pw_w.transpose(0, 2, 1))
    f = np.zeros((6 * M2 + 1, M2, 2, C), np.float32)
    for ri in range(2):
        for j in range(3):
            for k in range(M2):
                f[(ri * 3 + j) * M2 + k, k, ri] = fc0_w[j]
    f[6 * M2, 0, 0] = fc0_b
    out["fc0_modes"] = f.reshape(6 * M2 + 1, M2, P)
    out["fc0_t"] = np.ascontiguousarray(fc0_w.T)
    out["fc0_b"] = fc0_b
    return out


def build(nc, d, B, out):
    NP, NG = B // 2, B // GI
    MB = 16
    NB = B // MB

    with ExitStack() as ctx:
        def sem(name):
            return ctx.enter_context(nc.semaphore(name))

        def sb(name, shape):
            return ctx.enter_context(nc.sbuf_tensor(name, shape, F32))

        spec_in = nc.dram_tensor("spec_in", [2, C, NCH, B, MC], F32, kind="Internal").ap()
        spec_out = nc.dram_tensor("spec_out", [NG, 2, K1, C, GI * M2], F32, kind="Internal").ap()
        y_dram = nc.dram_tensor("y_dram", [NP, P, PX], F32, kind="Internal").ap()

        ident = sb("ident", [P, P])
        fw2 = sb("fw2", [P, 4 * M2])
        gh = sb("gh", [P, 2 * K1])
        ga = sb("ga", [2 * K1, 4 * S])
        fb2 = sb("fb2", [P, 2 * S])
        half = sb("half", [P, P])
        pw = sb("pw", [P, P])
        wst = sb("wst", [P, C])
        pwb = sb("pwb", [P, 1])
        gamma = sb("gamma", [P, 1])
        beta = sb("beta", [P, 1])
        fc0t = sb("fc0t", [P, P])
        fc0b = sb("fc0b", [P, 1])
        scale = sb("scale", [P, 1])
        shift = sb("shift", [P, 1])
        bn = sb("bn", [P, 12])
        stats = sb("stats", [P, NP * 48])
        fc1 = sb("fc1", [P, P])
        fc1b = sb("fc1b", [P, 1])
        fc2 = sb("fc2", [P, 1])
        fc2b = sb("fc2b", [P, 1])
        ARENA = 45800
        arena = sb("arena", [P, ARENA])

        def at(off, *shape, parts=P):
            n = int(np.prod(shape))
            assert off + n <= ARENA, (off, shape)
            v = arena[0:parts, off:off + n]
            if len(shape) == 2:
                v = v.rearrange("p (a b) -> p a b", a=shape[0])
            if len(shape) == 3:
                v = v.rearrange("p (a b c) -> p a b c", a=shape[0], b=shape[1])
            if len(shape) == 4:
                v = v.rearrange("p (a b c e) -> p a b c e", a=shape[0], b=shape[1], c=shape[2])
            return v

        bank = [ctx.enter_context(nc.psum_tensor(f"bank{i}", [P, BK], F32)) for i in range(8)]

        phase_done = sem("phase_done")
        zeroed = sem("zeroed")
        waited = {e.engine: sem(f"waited_{n}") for n, e in (
            ("sync", nc.sync), ("tensor", nc.tensor), ("scalar", nc.scalar), ("vector", nc.vector), ("gpsimd", nc.gpsimd))}

        def phase_end(eng, n):
            eng.sem_inc(waited[eng.engine], 1)
            eng.drain().then_inc(phase_done, 1)
            eng.wait_ge(phase_done, ENGINES * n)
            eng.sem_inc(waited[eng.engine], 1)

        const_loaded = sem("const_loaded")
        x0_loaded = [sem("x0_loaded_even"), sem("x0_loaded_odd")]
        rows0_done, rows0_copied, cols0_done, cols0_copied = (
            sem("rows0_done"), sem("rows0_copied"), sem("cols0_done"), sem("cols0_copied"))
        fc0_done, fc0_copied = sem("fc0_done"), sem("fc0_copied")
        spec0_stored, pw0_done, pw0_copied = sem("spec0_stored"), sem("pw0_done"), sem("pw0_copied")

        x0 = [at(192 * u, 192) for u in range(2)]
        z0 = [at(384 + 256 * u, 256, parts=96) for u in range(2)]
        v0 = at(1024, B, K1, parts=6 * M2 + 1)
        f0m = at(1024 + B * K1, M2, P, parts=6 * M2 + 1)
        f0c = at(1024 + B * K1 + M2 * P, 4, 96, parts=96)
        g0 = at(1024 + B * K1 + M2 * P + 384, P)
        spec0 = [at(8192 + u * NCH * MB * MC, NCH, MB, CH, M2) for u in range(2)]
        assert 1024 + B * K1 + M2 * P + 512 <= 8192

        def sync_spectrum0(sp):
            loads = [(ident[:], "c_ident"), (fw2[:], "c_fw2"), (gh[:], "c_gh"), (ga[:], "c_ga"),
                     (half[:], "c_half"), (f0m, "fc0_modes"), (f0c, "c_f0"), (g0, "c_g0")]
            for dst, name in loads:
                sp.dma_start(dst, d[name]).then_inc(const_loaded, 16)
            for u in range(2):
                sp.dma_start(fb2[u * C:(u + 1) * C, :], d["c_fb2"]).then_inc(const_loaded, 16)
            sp.dma_start(v0[6 * M2:6 * M2 + 1, :, :],
                         d["c_dc"].rearrange("a (b k) -> a b k", b=1).to_broadcast([1, B, K1])).then_inc(const_loaded, 16)
            sp.wait_ge(zeroed, 3)
            for u in range(2):
                half_p = slice(u * C, (u + 1) * C)
                sp.dma_start(fc0b[half_p, :], d["fc0_b"].rearrange("(c a) -> c a", a=1)).then_inc(const_loaded, 16)
                sp.dma_start(fc0t[half_p, C * u:C * u + 3], d["fc0_t"]).then_inc(const_loaded, 16)
                sp.dma_start(pw[half_p, u * C:(u + 1) * C], d["pw_t"][0]).then_inc(const_loaded, 16)
                sp.dma_start(pwb[half_p, :], d["pw_b"][0].rearrange("(c a) -> c a", a=1)).then_inc(const_loaded, 16)
                sp.dma_start(fc1[half_p, :], d["fc1_w"]).then_inc(const_loaded, 16)
            sp.dma_start(fc1b[:], d["fc1_b"].rearrange("(c a) -> c a", a=1)).then_inc(const_loaded, 16)
            sp.dma_start(fc2[:], d["fc2_w"]).then_inc(const_loaded, 16)
            sp.dma_start(fc2b[:], d["fc2_b"].rearrange("(c a) -> c a", a=1).to_broadcast([P, 1])).then_inc(const_loaded, 16)
            with sp.Fori(0, NP // 2) as i:
                for u in range(2):
                    sp.wait_ge(rows0_done, i * 2 + (u + 1))
                    sp.dma_start(x0[u], d["x_rows"][i * 2 + u]).then_inc(x0_loaded[u], 16)

        N_CONST = 16 * (9 + 2 + 10 + 3)

        def tensor_spectrum0(pe):
            pe.sem_inc(rows0_done, 2)
            pe.wait_ge(const_loaded, N_CONST)
            pe.matmul(bank[0][:, 0:P], fc0t[:], pw[:], start=True, stop=True)
            pe.matmul(bank[1][:, 0:1], pw[:], fc0b[:], start=True, stop=True).then_inc(pw0_done, 1)
            pe.wait_ge(pw0_copied, 3)
            with pe.Fori(0, NP // 2) as i:
                for u in range(2):
                    pe.wait_ge(rows0_copied, i * 2 + (u + 1))
                    pe.wait_ge(x0_loaded[u], i * 16 + 16)
                    for wh in range(2):
                        mm = pe.matmul(bank[u][0:96, wh * P:(wh + 1) * P], x0[u][:, wh * 96:(wh + 1) * 96], g0,
                                       start=True, stop=True)
                    mm.then_inc(rows0_done, 1)
                    pe.wait_ge(rows0_copied, i * 2 + (u + 3))
                    pe.wait_ge(cols0_copied, i * 2 + (u + 1))
                    for k in range(4):
                        part, wh = k // 2, k % 2
                        mm = pe.matmul(bank[2 + u][0:96, 0:2 * K1], f0c[:, part * 2 + wh, :],
                                       z0[u][:, wh * P + part * 2 * K1:wh * P + (part + 1) * 2 * K1],
                                       start=(k == 0), stop=(k == 3))
                    mm.then_inc(cols0_done, 1)
            pe.wait_ge(cols0_copied, NP + 2)
            with pe.Fori(0, NB) as t:
                for k in range(M2):
                    pe.wait_ge(fc0_copied, t * M2 + (k + 1))
                    pe.matmul(bank[4 + k % 4][:], f0m[:, k, :],
                              v0[:, bass.ds(t * MB, MB), :].rearrange("p b k -> p (b k)"),
                              start=True, stop=True).then_inc(fc0_done, 1)

        def vector_spectrum0(dve):
            dve.sem_inc(rows0_copied, 2)
            dve.sem_inc(cols0_copied, 2)
            dve.sem_inc(fc0_copied, 4)
            dve.wait_ge(pw0_done, 1)
            dve.wait_ge(const_loaded, N_CONST)
            for u in range(2):
                half_p = slice(u * C, (u + 1) * C)
                dve.tensor_copy(wst[half_p, :], bank[0][half_p, u * C:(u + 1) * C]).then_inc(pw0_copied, 1)
            dve.tensor_tensor(pwb[:], bank[1][:, 0:1], pwb[:], ALU.add).then_inc(pw0_copied, 1)
            with dve.Fori(0, NP // 2) as i:
                for u in range(2):
                    dve.wait_ge(rows0_done, i * 2 + (u + 3))
                    dve.tensor_copy(z0[u], bank[u][0:96, 0:256]).then_inc(rows0_copied, 1)
                    dve.wait_ge(cols0_done, i * 2 + (u + 1))
                    dve.tensor_scalar(v0[0:96, bass.ds(i * 4 + 2 * u, 2), :].rearrange("p b k -> p (b k)"),
                                      bank[2 + u][0:96, 0:2 * K1], 1.0, None, ALU.mult).then_inc(cols0_copied, 1)
            with dve.Fori(0, NB // 2 if NB > 1 else 1) as t:
                for u in range(2 if NB > 1 else 1):
                    for k in range(M2):
                        dve.wait_ge(fc0_done, t * (2 * M2) + (u * M2 + k + 1))
                        if k == 0:
                            dve.wait_ge(spec0_free, t * 2 + (u + 1))
                        dve.tensor_copy(spec0[u][:, :, :, :, k].rearrange("p h b k -> p b h k"),
                                        bank[4 + k % 4][:].rearrange("p (b h k) -> p b h k", b=MB, h=NCH)).then_inc(fc0_copied, 1)

        spec0_free = sem("spec0_free")

        def scalar_spectrum0(act):
            act.sem_inc(spec0_free, 2)
            for t in range(NB):
                act.wait_ge(fc0_copied, 4 + M2 * (t + 1))
                for ri in range(2):
                    act.dma_start(spec_in[ri, :, :, t * MB:(t + 1) * MB, :],
                                  spec0[t % 2][ri * C:(ri + 1) * C].rearrange("p h b k m -> p h b (k m)")
                                  ).then_inc(spec0_stored, 16)
                act.wait_ge(spec0_stored, 32 * (t + 1))
                act.sem_inc(spec0_free, 1)

        def gpsimd_spectrum0(pool):
            pool.memset(fc0t[:], 0.0).then_inc(zeroed, 1)
            pool.memset(pw[:], 0.0).then_inc(zeroed, 1)
            pool.memset(bn[:], 0.0).then_inc(zeroed, 1)

        w_loaded = [sem("w_loaded_even"), sem("w_loaded_odd")]
        s_loaded = [sem("s_loaded_even"), sem("s_loaded_odd")]
        layer_loaded = sem("layer_loaded")
        imag_up, real_down, imag_negated = sem("imag_up"), sem("real_down"), sem("imag_negated")
        mix_done, mixed_by_act, mixed_by_dve = sem("mix_done"), sem("mixed_by_act"), sem("mixed_by_dve")
        mix_free, mixed_stored = sem("mix_free"), [sem("mixed_stored_even"), sem("mixed_stored_odd")]

        w_sb = [at(u * MC * C, MC, C) for u in range(2)]
        s_sb = [at(2 * MC * C + 2 * u * B * MC, 2, B, MC) for u in range(2)]
        m_sb = [at(2 * MC * C + 4 * B * MC + u * CH * B * M2, CH // 2, 2, B, M2) for u in range(2)]
        IT = NCH // 2

        def sync_mix(sp, l, first):
            def load(u, i2):
                sp.wait_ge(mix_free, l * NCH + (i2 + (u + 1)))
                for ri in range(2):
                    sp.dma_start(s_sb[u][ri * C:(ri + 1) * C, 0], spec_in[ri, :, i2 + u]).then_inc(s_loaded[u], 16)
                sp.dma_start(w_sb[u], d["w_modes"][l, i2 + u]).then_inc(w_loaded[u], 16)

            def store(u, i2):
                n = l * NCH + i2
                sp.wait_ge(mixed_by_act, n * 4 + (4 * u + 8))
                sp.wait_ge(mixed_by_dve, n * 4 + (4 * u + 8))
                for kk in range(CH):
                    h, k = kk // 2, kk % 2
                    for ri in range(2):
                        sp.dma_start(spec_out[:, ri, i2 * CH + (u * CH + kk)].rearrange("g c x -> c g x"),
                                     m_sb[u][h * C:(h + 1) * C, k, ri].rearrange("p (g b) k -> p g (b k)", g=NG)
                                     ).then_inc(mixed_stored[u], 16)

            for u in range(2):
                load(u, 0)
            with sp.Fori(0, IT - 1) as i:
                for u in range(2):
                    store(u, i * 2)
                    load(u, i * 2 + 2)
            for u in range(2):
                store(u, (IT - 1) * 2)
            for u in range(2):
                half_p = slice(u * C, (u + 1) * C)
                for dst, name in ((gamma, "gamma"), (beta, "beta")):
                    sp.dma_start(dst[half_p, :], d[name][l].rearrange("(c a) -> c a", a=1)).then_inc(layer_loaded, 16)
                if not first:
                    sp.dma_start(wst[half_p, :], d["pw_t"][l]).then_inc(layer_loaded, 16)
                    sp.dma_start(pwb[half_p, :], d["pw_b"][l].rearrange("(c a) -> c a", a=1)).then_inc(layer_loaded, 16)
            sp.wait_ge(layer_loaded, l * 128 + 64)
            for u in range(2):
                sp.wait_ge(mixed_stored[u], l * (IT * 128) + (IT * 128 + 128))
            sp.sem_inc(waited[sp.engine], 1)

        def tensor_mix(pe, l, first):
            if first:
                pe.sem_inc(mix_free, 2)
            with pe.Fori(0, IT) as i:
                for u in range(2):
                    n = l * NCH + i * 2
                    pe.wait_ge(w_loaded[u], (l * IT + i) * 16 + 16)
                    pe.wait_ge(real_down, n + (u + 1))
                    pe.wait_ge(imag_up, n + (u + 1))
                    pe.wait_ge(imag_negated, n + (u + 1))
                    for j in range(8):
                        by = mixed_by_act if j % 2 == 0 else mixed_by_dve
                        pe.wait_ge(by, n * 4 + (4 * u + j // 2 + 1))
                        pe.sem_inc(waited[pe.engine], 1)
                        for m in range(4):
                            for h in range(2):
                                mode = h * (MC // 2) + 4 * j + m
                                mm = pe.matmul(bank[j][h * C:(h + 1) * C, m * 2 * B:(m + 1) * 2 * B], w_sb[u][:, mode, :],
                                               s_sb[u][:, :, :, mode], start=True, stop=True)
                        mm.then_inc(mix_done, 1)
                    pe.wait_ge(mix_done, n * 8 + (8 * u + 8))
                    pe.sem_inc(mix_free, 1)

        def mixed_view(u, j):
            k = 4 * (j % 4)
            return [(m_sb[u][:, j // 4, r, :, k:k + 4],
                     bank[j][:, 0:8 * B].rearrange("p (m r b) -> p r b m", m=4, r=2)[:, r]) for r in range(2)]

        def scalar_mix(act, l, first):
            if first:
                act.sem_inc(mixed_by_act, 4)
                act.sem_inc(mixed_stored[0], 16 * 8)
                act.sem_inc(mixed_stored[1], 16 * 8)
            with act.Fori(0, IT) as i:
                for u in range(2):
                    n = l * NCH + i * 2
                    act.wait_ge(s_loaded[u], (l * IT + i) * 32 + 32)
                    act.activation(s_sb[u][0:C, 1], s_sb[u][C:P, 0], ACT.Copy).then_inc(imag_up, 1)
                    act.wait_ge(mixed_stored[u], (l * IT + i) * 128 + 128)
                    for j in range(0, 8, 2):
                        act.wait_ge(mix_done, n * 8 + (8 * u + j + 1))
                        for o, v in mixed_view(u, j):
                            c = act.activation(o, v, ACT.Copy)
                        c.then_inc(mixed_by_act, 1)

        def vector_mix(dve, l, first):
            if first:
                dve.sem_inc(mixed_by_dve, 4)
            with dve.Fori(0, IT) as i:
                for u in range(2):
                    n = l * NCH + i * 2
                    dve.wait_ge(s_loaded[u], (l * IT + i) * 32 + 32)
                    dve.sem_inc(waited[dve.engine], 1)
                    dve.tensor_copy(s_sb[u][C:P, 1], s_sb[u][0:C, 0]).then_inc(real_down, 1)
                    dve.wait_ge(imag_up, n + (u + 1))
                    dve.tensor_scalar(s_sb[u][C:P, 0], s_sb[u][C:P, 0], -1.0, None, ALU.mult).then_inc(imag_negated, 1)
                    dve.wait_ge(mixed_stored[u], (l * IT + i) * 128 + 128)
                    for j in range(1, 8, 2):
                        dve.wait_ge(mix_done, n * 8 + (8 * u + j + 1))
                        for o, v in mixed_view(u, j):
                            c = dve.tensor_copy(o, v)
                        c.then_inc(mixed_by_dve, 1)

        grp_loaded, grp_free, pair_ready = sem("grp_loaded"), sem("grp_free"), sem("pair_ready")
        in_loaded = [[sem(f"in_loaded{u}{v}") for v in range(2)] for u in range(2)]
        h_ready = sem("h_ready")
        rows_done, rows_copied, turn_done, turn_copied = (
            sem("rows_done"), sem("rows_copied"), sem("turn_done"), sem("turn_copied"))
        y_done, y_copied, y_seen = sem("y_done"), sem("y_copied"), sem("y_seen")
        y_stored = [sem("y_stored_even"), sem("y_stored_odd")]
        stat_taken, stat_kept = sem("stat_taken"), sem("stat_kept")
        bn_step, bn_sum, bn_root = sem("bn_step"), sem("bn_sum"), sem("bn_root")

        hin = [[at((2 * u + par) * PX, PX) for par in range(2)] for u in range(2)]
        yout = [at((4 + u) * PX, PX) for u in range(2)]
        O1 = 6 * PX
        grp = at(O1, C, GI, M2, parts=2 * K1)
        O1 += C * GI * M2
        prs = [at(O1 + u * M2 * P, M2, P, parts=2 * K1) for u in range(2)]
        O1 += 2 * M2 * P
        RP = S // 2
        a1 = [at(O1 + u * (S + 2) * 2 * M2, S + 2, 2 * M2) for u in range(2)]
        O1 += 2 * (S + 2) * 2 * M2
        a2 = [at(O1 + par * RP * C, RP, C) for par in range(2)]
        O1 += 2 * RP * C
        st = [at(O1 + u * 48, 48) for u in range(2)]
        CHAN = (slice(0, C), slice(C, P))
        FREQ = (slice(C, P), slice(0, C))
        h_zeroed, filled = sem("h_zeroed"), sem("filled")

        def sync_inverse(sp, l, first):
            if first:
                sp.sem_inc(grp_free, 1)
                for u in range(2):
                    sp.sem_inc(y_stored[u], 16)
            def load_group(g):
                sp.wait_ge(grp_free, l * NG + (g + 1))
                sp.dma_start(grp.rearrange("p c b k -> p (c b k)"),
                             spec_out[g].rearrange("r k c x -> (r k) (c x)")).then_inc(grp_loaded, 16)

            def load_pair(g, q):
                u = q % 2
                for v in range(2):
                    px = slice(v * 2048, (v + 1) * 2048)
                    sp.wait_ge(y_done, ((l * NG + g) * Q + q) * 8 + (4 * v + 4))
                    for par in range(2):
                        if first:
                            sp.dma_start(hin[u][par][C * par:C * par + 3, px],
                                         d["x_pair"][g * Q + q, 3 * par:3 * par + 3, px]).then_inc(in_loaded[u][v], 16)
                        else:
                            sp.dma_start(hin[u][par][CHAN[par], px],
                                         y_dram[g * Q + q, CHAN[par], px]).then_inc(in_loaded[u][v], 16)

            load_group(0)
            if first:
                sp.wait_ge(h_zeroed, 4)
            with sp.Fori(0, NG - 1) as g:
                for q in range(Q):
                    if q == Q - 1:
                        load_group(g + 1)
                    load_pair(g, q)
            for q in range(Q):
                load_pair(NG - 1, q)

        def gpsimd_inverse(pool, l, first):
            with pool.Fori(0, NG) as g:
                G = l * NG + g
                for q in range(Q):
                    pool.wait_ge(rows_done, (G * Q + q) * 4 + 4)
                    pool.wait_ge(grp_loaded, G * 16 + 16)
                    pool.sem_inc(waited[pool.engine], 1)
                    for par in range(2):
                        pool.tensor_copy(prs[q % 2][:, :, par * C:(par + 1) * C],
                                         grp[:, :, par * Q + q, :].rearrange("p c k -> p k c")).then_inc(pair_ready, 1)
                pool.wait_ge(pair_ready, G * (2 * Q) + 2 * Q)
                pool.sem_inc(waited[pool.engine], 1)
                pool.sem_inc(grp_free, 1)

        def tensor_inverse(pe, l, first):
            if first:
                pe.sem_inc(rows_done, 8)
                pe.sem_inc(y_done, 16)

            def rows(n, q, t):
                if t == 0:
                    pe.wait_ge(pair_ready, n * 2 + 2)
                pe.wait_ge(rows_copied, n * 5 + (t + 1))
                pe.sem_inc(waited[pe.engine], 1)
                for k in range(4):
                    for par in range(2):
                        mm = pe.matmul(bank[t % 2][CHAN[par], k * P:(k + 1) * P], prs[q % 2][:, 4 * t + k, par * C:(par + 1) * C],
                                       ga[:, par * P:(par + 1) * P], start=True, stop=True)
                mm.then_inc(rows_done, 1)

            def turn(n, q, t):
                if t == 0:
                    pe.wait_ge(rows_copied, n * 5 + 7)
                pe.wait_ge(turn_copied, n * 8 + (t + 1))
                for k in range(4):
                    mm = pe.transpose(bank[2 + t % 2][:, k * P:(k + 1) * P],
                                      a1[q % 2][:, 8 * t + 2 * k:8 * t + 2 * k + 4, :].rearrange("p h m -> p (h m)"), ident[:])
                mm.then_inc(turn_done, 1)

            def columns(n, q, t):
                if t % 4 == 0 and first:
                    pe.wait_ge(in_loaded[q % 2][t // 4], (n - q) * (32 // 2) + (q // 2 * 32 + 32))
                if t % 2 == 0 and not first:
                    pe.wait_ge(h_ready, n * 8 + (t + 2))
                pe.wait_ge(turn_copied, n * 8 + (t + 3))
                pe.wait_ge(y_copied, n * 8 + (t + 1))
                pe.sem_inc(waited[pe.engine], 1)
                for k in range(4):
                    for par in range(2):
                        j = 4 * t + k
                        mm = pe.matmul(bank[4 + t % 4][CHAN[par], k * P:(k + 1) * P], a2[par][:, j, :],
                                       hin[q % 2][par][:, j * P:(j + 1) * P], start=True, stop=True)
                mm.then_inc(y_done, 1)

            def group(G, last):
                for q in range(Q):
                    n = G * Q + q
                    for t in range(8):
                        columns(n, q, t)
                        if q < Q - 1 or not last:
                            if t < 4:
                                rows(n + 1, (q + 1) % Q, t)
                            else:
                                turn(n + 1, (q + 1) % Q, 2 * t - 8)
                                turn(n + 1, (q + 1) % Q, 2 * t - 7)

            for t in range(4):
                rows(l * (NG * Q), 0, t)
            for t in range(8):
                turn(l * (NG * Q), 0, t)
            pe.wait_ge(filled, l * 6 + 6)
            pe.sem_inc(waited[pe.engine], 1)
            with pe.Fori(0, NG - 1) as g:
                group(l * NG + g, False)
            group(l * NG + (NG - 1), True)
            pe.wait_ge(bn_step, l * BN_STEPS + 2)
            pe.wait_ge(y_copied, (l + 1) * (NP * 8) + 4)
            pe.matmul(bank[0][:, 0:1], half[:], bn[:, 0:1], start=True, stop=True).then_inc(bn_sum, 1)
            pe.wait_ge(bn_step, l * BN_STEPS + 4)
            pe.matmul(bank[1][:, 0:1], half[:], bn[:, 4:5], start=True, stop=True).then_inc(bn_sum, 1)

        BN_STEPS = 8

        def scalar_inverse(act, l, first):
            if first:
                act.sem_inc(y_copied, 4)
                act.sem_inc(h_ready, 8 * NP)

            def gelu(G, q, s):
                u, par = q % 2, s % 2
                if first:
                    return
                if s % 4 == 0:
                    act.wait_ge(in_loaded[u][s // 4], G * 64 + (q // 2 * 32 + 32))
                    act.sem_inc(waited[act.engine], 1)
                h = hin[u][par][CHAN[par], s // 2 * 1024:(s // 2 + 1) * 1024]
                act.activation(h, h, ACT.Gelu, bias=shift[CHAN[par], :], scale=scale[CHAN[par], :]).then_inc(h_ready, 1)

            def y_out(n, G, g, q, t):
                u = q % 2
                if t == 0:
                    act.wait_ge(y_stored[u], G * 32 + (q // 2 * 16 + 16))
                    act.wait_ge(y_seen, n * 8 + 8)
                act.wait_ge(y_done, n * 8 + (t + 17))
                act.activation(yout[u][:, t * BK:(t + 1) * BK], bank[4 + t % 4][:], ACT.Identity,
                               bias=pwb[:]).then_inc(y_copied, 1)
                if t == 7:
                    act.wait_ge(y_copied, n * 8 + 12)
                    act.dma_start(y_dram[g * Q + q], yout[u]).then_inc(y_stored[u], 16)

            def group(G, g, last):
                for q in range(Q):
                    n = G * Q + q
                    for t in range(8):
                        y_out(n, G, g, q, t)
                        if t < 4:
                            gelu(G, q, t + 4)
                        elif q < Q - 1:
                            gelu(G, q + 1, t - 4)
                        elif not last:
                            gelu(G + 1, 0, t - 4)

            for par in range(2):
                act.activation(a2[par][CHAN[par]], wst[CHAN[par], :].unsqueeze(1).to_broadcast([C, RP, C]),
                               ACT.Copy).then_inc(filled, 1)
            for s in range(4):
                gelu(l * NG, 0, s)
            with act.Fori(0, NG - 1) as g:
                group(l * NG + g, g, False)
            group(l * NG + (NG - 1), NG - 1, True)
            for u in range(2):
                act.wait_ge(y_stored[u], l * (NG * 32) + (NG * 32 + 16))
            act.wait_ge(bn_step, l * BN_STEPS + 5)
            act.sem_inc(waited[act.engine], 1)
            act.activation(bn[:, 6:7], bn[:, 5:6], ACT.Sqrt).then_inc(bn_root, 1)

        def vector_inverse(dve, l, first):
            if first:
                dve.sem_inc(rows_copied, 2)
                dve.sem_inc(turn_copied, 2)
                dve.sem_inc(stat_kept, 2)
                dve.sem_inc(y_seen, 16)

            def rows(n, q, t):
                dve.wait_ge(rows_done, n * 4 + (8 + t + 1))
                dve.tensor_copy(a1[q % 2][:, 0:S, 8 * t:8 * t + 8],
                                bank[t % 2][:].rearrange("p (m h) -> p h m", m=8)).then_inc(rows_copied, 1)
                if t == 3:
                    dve.wait_ge(rows_copied, n * 5 + 6)
                    dve.sem_inc(waited[dve.engine], 1)
                    dve.tensor_copy(a1[q % 2][:, S:S + 2, :], a1[q % 2][:, 0:2, :]).then_inc(rows_copied, 1)

            def turn(n, q, t):
                dve.wait_ge(turn_done, n * 8 + (t + 1))
                dve.wait_ge(y_done, n * 8 + (t + 9))
                for par in range(2):
                    c = dve.tensor_copy(a2[par][FREQ[par], 4 * t:4 * t + 4, :],
                                        bank[2 + t % 2][FREQ[par], :].rearrange("p (a b) -> p a b", a=4)[:, :, CHAN[par]])
                c.then_inc(turn_copied, 1)

            def moments(n, g, q, t):
                u = q % 2
                if t == 0:
                    dve.wait_ge(stat_kept, n + 1)
                dve.wait_ge(y_copied, n * 8 + (t + 5))
                s = dve.bn_stats(st[u][:, 6 * t:6 * t + 6], yout[u][:, t * BK:(t + 1) * BK])
                s.then_inc(y_seen, 1)
                if t == 7:
                    dve.wait_ge(y_seen, n * 8 + 24)
                    dve.tensor_scalar(stats[:, bass.ds((g * Q + q) * 48, 48)], st[u], 1.0, None,
                                      ALU.mult).then_inc(stat_kept, 1)

            def group(G, g, last):
                for q in range(Q):
                    n = G * Q + q
                    for t in range(8):
                        if q < Q - 1 or not last:
                            if t < 4:
                                rows(n + 1, (q + 1) % Q, t)
                            else:
                                turn(n + 1, (q + 1) % Q, 2 * t - 8)
                                turn(n + 1, (q + 1) % Q, 2 * t - 7)
                        moments(n, g, q, t)

            if first:
                for u in range(2):
                    for par in range(2):
                        dve.memset(hin[u][par][CHAN[par]], 0.0).then_inc(h_zeroed, 1)
            for u in range(2):
                for par in range(2):
                    dve.tensor_copy(hin[u][par][FREQ[par]].rearrange("p (a b) -> p a b", a=RP),
                                    fb2[FREQ[par], :].unsqueeze(1).to_broadcast([C, RP, P])).then_inc(filled, 1)
            for t in range(4):
                rows(l * (NG * Q), 0, t)
            for t in range(8):
                turn(l * (NG * Q), 0, t)
            with dve.Fori(0, NG - 1) as g:
                group(l * NG + g, g, False)
            group(l * NG + (NG - 1), NG - 1, True)
            base = l * BN_STEPS
            dve.wait_ge(stat_kept, (l + 1) * NP + 2)
            dve.sem_inc(waited[dve.engine], 1)
            dve.bn_aggr(bn[:, 0:2], stats[:]).then_inc(bn_step, 1)
            dve.wait_ge(bn_step, base + 1)
            dve.tensor_copy(bn[:, 2:3], bn[:, 0:1]).then_inc(bn_step, 1)
            dve.wait_ge(bn_sum, l * 2 + 1)
            dve.tensor_tensor(bn[:, 3:4], bn[:, 0:1], bank[0][:, 0:1], ALU.subtract).then_inc(bn_step, 1)
            dve.wait_ge(bn_step, base + 3)
            dve.scalar_tensor_tensor(out=bn[:, 4:5], in0=bn[:, 3:4], scalar=bn[:, 3:4], in1=bn[:, 1:2],
                                     op0=ALU.mult, op1=ALU.add).then_inc(bn_step, 1)
            dve.wait_ge(bn_sum, l * 2 + 2)
            dve.tensor_scalar(bn[:, 5:6], bank[1][:, 0:1], EPS, None, ALU.add).then_inc(bn_step, 1)
            dve.wait_ge(bn_root, l + 1)
            dve.reciprocal(bn[:, 7:8], bn[:, 6:7]).then_inc(bn_step, 1)
            dve.wait_ge(bn_step, base + 6)
            dve.tensor_tensor(scale[:], bn[:, 7:8], gamma[:], ALU.mult).then_inc(bn_step, 1)
            dve.wait_ge(bn_step, base + 7)
            dve.tensor_tensor(bn[:, 8:9], scale[:], bank[0][:, 0:1], ALU.mult).then_inc(bn_step, 1)
            dve.wait_ge(bn_step, base + 8)
            dve.tensor_tensor(shift[:], beta[:], bn[:, 8:9], ALU.subtract).then_inc(stat_taken, 1)
            dve.wait_ge(stat_taken, l + 1)
            dve.sem_inc(waited[dve.engine], 1)

        f_loaded = [sem(f"f_loaded{i}") for i in range(Q)]
        f_ready = sem("f_ready")
        ht_done, ht_copied, fc_done, fc_copied = sem("ht_done"), sem("ht_copied"), sem("fcol_done"), sem("fcol_copied")
        ft_done, ft_copied, fr_done, fr_copied = sem("ft_done"), sem("ft_copied"), sem("frow_done"), sem("frow_copied")
        spec_stored = [sem("spec_stored_a"), sem("spec_stored_b")]

        hf = [at(q * PX, PX) for q in range(Q)]
        FO = Q * PX
        ht = [at(FO + u * BK, 4, P) for u in range(2)]
        t1 = [at(FO + 1024 + u * 2048, 2 * M2, S) for u in range(2)]
        t2 = [at(FO + 5120 + u * BK, 4, P) for u in range(2)]
        xs = [at(FO + 6144 + u * 4096, 2, NCH, 2, MC) for u in range(2)]

        def sync_forward(sp, lf, first):
            with sp.Fori(0, NG) as g:
                F = lf * NG + g
                for q in range(Q):
                    sp.wait_ge(ht_done, (F * Q + q) * 8 + 8)
                    sp.dma_start(hf[q], y_dram[g * Q + q]).then_inc(f_loaded[q], 16)

        def tensor_forward(pe, lf):
            def turn(n, q, t):
                if t % 4 == 0:
                    pe.wait_ge(f_ready, n * 2 + (t // 4 + 1))
                pe.wait_ge(ht_copied, n * 8 + (t + 1))
                for k in range(4):
                    mm = pe.transpose(bank[t % 2][:, k * P:(k + 1) * P], hf[q][:, (4 * t + k) * P:(4 * t + k + 1) * P], ident[:])
                mm.then_inc(ht_done, 1)

            def columns(n, t):
                pe.wait_ge(ht_copied, n * 8 + (t + 3))
                if t % 2 == 0:
                    pe.wait_ge(fc_copied, n * 4 + (t // 2 + 1))
                b = bank[2 + t // 2 % 2]
                for k in range(4):
                    mm = pe.matmul(b[:, (t % 2) * 256 + k * 64:(t % 2) * 256 + (k + 1) * 64], ht[t % 2][:, k, :], fw2[:],
                                   start=True, stop=True)
                mm.then_inc(fc_done, 1)

            def turn_rows(n, q, t):
                if t == 0:
                    pe.wait_ge(fc_copied, n * 4 + 6)
                pe.wait_ge(ft_copied, n * 4 + (t + 1))
                for k in range(4):
                    mm = pe.transpose(bank[4 + t % 2][:, k * P:(k + 1) * P],
                                      t1[q % 2][:, 8 * t + 2 * k:8 * t + 2 * k + 2, :].rearrange("p m h -> p (m h)"), ident[:])
                mm.then_inc(ft_done, 1)

            def rows(n, t):
                pe.wait_ge(ft_copied, n * 4 + (t + 3))
                if t % 2 == 0:
                    pe.wait_ge(fr_copied, n * 2 + (t // 2 + 1))
                for k in range(4):
                    mm = pe.matmul(bank[6 + t // 2][:, (t % 2) * 256 + k * 64:(t % 2) * 256 + (k + 1) * 64], t2[t % 2][:, k, :],
                                   gh[:], start=True, stop=True)
                mm.then_inc(fr_done, 1)

            def group(F, first):
                for q in range(Q):
                    n = F * Q + q
                    before = q > 0 or not first
                    for t in range(8):
                        turn(n, q, t)
                        if t > 0:
                            columns(n, t - 1)
                        elif before:
                            columns(n - 1, 7)
                        if before and 2 <= t < 6:
                            turn_rows(n - 1, (q - 1) % Q, t - 2)
                        if before and 3 <= t < 7:
                            rows(n - 1, t - 3)

            group(lf * NG, True)
            with pe.Fori(1, NG) as g:
                group(lf * NG + g, False)
            n = lf * NP + (NP - 1)
            columns(n, 7)
            for t in range(5):
                if t < 4:
                    turn_rows(n, Q - 1, t)
                if t > 0:
                    rows(n, t - 1)

        def scalar_forward(act, lf, first_time):
            def gelu(F, n, q):
                act.wait_ge(f_loaded[q], F * 16 + 16)
                act.sem_inc(waited[act.engine], 1)
                for v in range(2):
                    x = hf[q][:, v * 2048:(v + 1) * 2048]
                    act.activation(x, x, ACT.Gelu, bias=shift[:], scale=scale[:]).then_inc(f_ready, 1)

            def t2_copies(n):
                for t in range(4):
                    act.wait_ge(ft_done, n * 4 + (t + 1))
                    act.activation(t2[t % 2].rearrange("p a b -> p (a b)"), bank[4 + t % 2][:], ACT.Copy).then_inc(ft_copied, 1)

            def store(n_last, b0, v):
                act.wait_ge(fr_copied, n_last * 2 + 4)
                for ri in range(2):
                    for par in range(2):
                        act.dma_start(spec_in[ri, :, :, bass.ds(b0 + (par * Q + 2 * v), 2), :],
                                      xs[v][par * C:(par + 1) * C, ri]).then_inc(spec_stored[v], 16)

            def group(F, g, first):
                for q in range(Q):
                    n = F * Q + q
                    gelu(F, n, q)
                    if q == 3:
                        store(n - 2, g * GI, 0)
                    if q == 1 and not first:
                        store(n - 2, g * GI - GI, 1)
                    if q > 0 or not first:
                        t2_copies(n - 1)

            group(lf * NG, 0, True)
            with act.Fori(1, NG) as g:
                group(lf * NG + g, g, False)
            n = lf * NP + (NP - 1)
            t2_copies(n)
            store(n, (NG - 1) * GI, 1)
            for v in range(2):
                act.wait_ge(spec_stored[v], lf * (NG * 64) + (NG * 64 + 64))
            act.sem_inc(waited[act.engine], 1)

        def vector_forward(dve, lf):
            def ht_copy(n, t):
                dve.wait_ge(ht_done, n * 8 + (8 * Q + t + 1))
                dve.tensor_copy(ht[t % 2].rearrange("p a b -> p (a b)"), bank[t % 2][:]).then_inc(ht_copied, 1)

            def column_copy(n, q, t):
                dve.wait_ge(fc_done, n * 8 + (2 * t + 2))
                dve.tensor_copy(t1[q % 2][:, :, 16 * t:16 * t + 16],
                                bank[2 + t % 2][:].rearrange("p (h m) -> p m h", h=16)).then_inc(fc_copied, 1)

            def row_copy(n, q, t):
                v = q // 2
                if q % 2 == 0 and t == 0:
                    dve.wait_ge(spec_stored[v], (n - q) * (64 // Q) + 64)
                dve.wait_ge(fr_done, n * 4 + (2 * t + 2))
                for ri in range(2):
                    o = xs[v][:, ri, :, q % 2, :].rearrange("p h (k m) -> p h k m", k=CH)[:, :, :, 8 * t:8 * t + 8]
                    cp = dve.tensor_copy(o, bank[6 + t][:].rearrange("p (m r h k) -> p r h k m", m=8, r=2, h=NCH)[:, ri])
                cp.then_inc(fr_copied, 1)

            def group(F, first):
                for q in range(Q):
                    n = F * Q + q
                    before = q > 0 or not first
                    for t in range(8):
                        ht_copy(n, t)
                        if t == 0 and before:
                            column_copy(n - 1, (q - 1) % Q, 3)
                        if t % 2 == 0 and t > 0:
                            column_copy(n, q, t // 2 - 1)
                        if before and t in (4, 6):
                            row_copy(n - 1, (q - 1) % Q, (t - 4) // 2)

            group(lf * NG, True)
            with dve.Fori(1, NG) as g:
                group(lf * NG + g, False)
            n = lf * NP + (NP - 1)
            column_copy(n, Q - 1, 3)
            for t in range(2):
                row_copy(n, Q - 1, t)

        e_loaded = [sem(f"e_loaded{i}") for i in range(Q)]
        e_ready, fc1_done, fc1_gelu, g_split, fc2_used = (
            sem("e_ready"), sem("fc1_done"), sem("fc1_gelu"), sem("g_split"), sem("fc2_used"))
        fc2_ready, fc2_copied, fc2_summed, tok_ready, tok_stored, tok_free = (
            sem("fc2_ready"), sem("fc2_copied"), sem("fc2_summed"), sem("tok_ready"), sem("tok_stored"), sem("tok_free"))
        g_high = sem("g_high")
        F16 = mybir.dt.float16
        NB_G = 4
        NB_S = 6
        HO = FO
        gb = [at(HO + u * BK, BK) for u in range(NB_G)]
        HO += NB_G * BK
        g_hi = [at(HO + u * BK, BK).bitcast(F16)[:, 0:BK] for u in range(NB_S)]
        g_lo = [at(HO + u * BK, BK).bitcast(F16)[:, BK:2 * BK] for u in range(NB_S)]
        HO += NB_S * BK
        RG = GI * 8
        win = [at(HO + u * 96, 96).bitcast(F16) for u in range(2)]
        HO += 192
        w_hi, w_lo = at(HO, 1).bitcast(F16)[:, 0:1], at(HO + 1, 1).bitcast(F16)[:, 0:1]
        w_rest = at(HO + 2, 1)
        fold = at(HO + 4, C)
        HO += 4 + C
        fsum = at(HO, BK)
        tokb = at(HO + BK, BK, parts=RG)
        TB = 16
        LAG = 4
        FIRSTS = Q * TB

        def sync_head(sp):
            with sp.Fori(0, NG) as g:
                for q in range(Q):
                    sp.wait_ge(fc1_done, (g * Q + q) * TB + TB)
                    sp.dma_start(hf[q], y_dram[g * Q + q]).then_inc(e_loaded[q], 16)

        def chunk(i):
            q, t = i // TB, i % TB
            return q, t, ((t // 8) * Q + q) * 8 + t % 8

        def tensor_head(pe):
            pe.sem_inc(fc1_done, TB * Q)
            pe.sem_inc(fc2_used, NB_S)
            pe.wait_ge(fc2_ready, 6)

            def first(g, i):
                q, t, _ = chunk(i)
                par, tt = t // 8, t % 8
                if t == 0:
                    pe.wait_ge(e_ready, (g * Q + q) * 2 + 2)
                pe.wait_ge(fc1_gelu, g * FIRSTS + (i + 1))
                pe.matmul(bank[i % 4][:], fc1[par * C:(par + 1) * C, :], hf[q][par * C:(par + 1) * C, tt * BK:(tt + 1) * BK],
                          start=True, stop=True).then_inc(fc1_done, 1)

            def second(g, i):
                _, _, r = chunk(i)
                pe.wait_ge(g_split, g * FIRSTS + (i + 1 + NB_G))
                w = win[(r + 1) % 2]
                a = RG - 1 - r + (r + 1) % 2
                pe.matmul(bank[6][:], w[:, a:a + P], g_hi[i % NB_S], start=(i == 0), stop=False)
                pe.matmul(bank[6][:], w[:, a:a + P], g_lo[i % NB_S], start=False, stop=(i == FIRSTS - 1)).then_inc(fc2_used, 1)

            with pe.Fori(0, NG) as g:
                for i in range(FIRSTS + LAG):
                    if i < FIRSTS:
                        first(g, i)
                    if i >= LAG:
                        if i == LAG:
                            pe.wait_ge(fc2_copied, g + 1)
                        second(g, i - LAG)
                pe.wait_ge(fc2_copied, g + 2)
                pe.wait_ge(tok_ready, g + 1)
                pe.matmul(bank[7][0:RG, :], fold, fsum, start=True, stop=True).then_inc(fc2_summed, 1)

        def scalar_head(act):
            act.sem_inc(fc1_gelu, 4)

            def gelu(G, q, v):
                if v == 0:
                    act.wait_ge(e_loaded[q], G * 16 + 16)
                    act.sem_inc(waited[act.engine], 1)
                x = hf[q][:, v * 2048:(v + 1) * 2048]
                act.activation(x, x, ACT.Gelu, bias=shift[:], scale=scale[:]).then_inc(e_ready, 1)

            def hidden(g, i):
                act.wait_ge(fc1_done, g * FIRSTS + (i + TB * Q + 1))
                act.wait_ge(g_split, g * FIRSTS + (i + 1))
                act.activation(gb[i % NB_G], bank[i % 4][:], ACT.Gelu, bias=fc1b[:]).then_inc(fc1_gelu, 1)

            def group(g, last):
                for i in range(FIRSTS):
                    hidden(g, i)
                    q, t = i // TB, i % TB
                    if t in (4, 10) and (q < Q - 1 or not last):
                        v = (t - 4) // 6
                        if q < Q - 1:
                            gelu(g, q + 1, v)
                        else:
                            gelu(g + 1, 0, v)

            for v in range(2):
                gelu(0, 0, v)
            with act.Fori(0, NG - 1) as g:
                group(g, False)
            group(NG - 1, True)

        def vector_head(dve):
            dve.sem_inc(g_split, NB_G)
            dve.sem_inc(fc2_copied, 1)
            dve.sem_inc(tok_ready, 1)
            for u in range(2):
                dve.memset(win[u], 0.0).then_inc(fc2_ready, 1)
            dve.tensor_copy(w_hi, fc2[:]).then_inc(fc2_ready, 1)
            dve.wait_ge(fc2_ready, 3)
            dve.tensor_tensor(w_rest, fc2[:], w_hi, ALU.subtract).then_inc(fc2_ready, 1)
            dve.wait_ge(fc2_ready, 4)
            dve.tensor_copy(w_lo, w_rest).then_inc(fc2_ready, 1)
            dve.wait_ge(fc2_ready, 5)
            dve.tensor_tensor(fold, ident[:, 0:C], ident[:, C:P], ALU.add)
            for u in range(2):
                dve.tensor_copy(win[u][:, RG - 1 + u:RG + u], w_hi)
                c = dve.tensor_copy(win[u][:, 2 * RG - 1 + u:2 * RG + u], w_lo)
            c.then_inc(fc2_ready, 1)
            with dve.Fori(0, NG) as g:
                for i in range(FIRSTS):
                    dve.wait_ge(fc1_gelu, g * FIRSTS + (i + 5))
                    dve.wait_ge(fc2_used, g * FIRSTS + (i + 1))
                    dve.tensor_copy(g_hi[i % NB_S], gb[i % NB_G]).then_inc(g_high, 1)
                    dve.wait_ge(g_high, g * FIRSTS + (i + 1))
                    dve.tensor_tensor(g_lo[i % NB_S], gb[i % NB_G], g_hi[i % NB_S], ALU.subtract).then_inc(g_split, 1)
                dve.wait_ge(fc2_used, g * FIRSTS + (FIRSTS + NB_S))
                dve.tensor_copy(fsum, bank[6][:]).then_inc(fc2_copied, 1)
                dve.wait_ge(fc2_summed, g + 1)
                dve.wait_ge(tok_free, g + 1)
                dve.tensor_scalar(tokb, bank[7][0:RG, :], fc2b[0:RG], None, ALU.add).then_inc(tok_ready, 1)

        def gpsimd_head(pool, tok):
            pool.sem_inc(tok_free, 1)
            with pool.Fori(0, NG) as g:
                pool.wait_ge(tok_ready, g + 2)
                pool.dma_start(tok[bass.ds(g * RG, RG), :], tokb).then_inc(tok_stored, 16)
                pool.wait_ge(tok_stored, g * 16 + 16)
                pool.sem_inc(tok_free, 1)
            pool.wait_ge(tok_stored, NG * 16)

        tok = nc.dram_tensor("tok", [B * S, S], F32, kind="Internal").ap().rearrange("(a r) x -> a (r x)", r=GI)

        NT = B * S // P
        TG = NT // 4
        HD, HEADS, MEM = 32, 4, 4
        HID = HEADS * HD
        E0, E1 = 8, 16

        h_tok = at(0, NT, C)
        x_tok = at(NT * C, NT, C)
        o_tok = at(2 * NT * C, NT, C)
        sq = at(3 * NT * C, NT, C)
        TO = 4 * NT * C
        red = at(TO, 8, NT); TO += 8 * NT
        wqkv = at(TO, 3 * HID, parts=C); TO += 3 * HID
        w_out = at(TO, C); TO += C
        gpre_b = at(TO, C); TO += C
        gout_b = at(TO, C); TO += C
        bout_b = at(TO, C); TO += C
        memk = at(TO, MEM); TO += MEM
        memk_max = at(TO, 4); TO += 4
        headmask = at(TO, HID); TO += HID
        wg = [at(TO, E0, parts=C), at(TO + E0, E1, parts=C)]; TO += E0 + E1
        bg_b = [at(TO, E0), at(TO + E0, E1)]; TO += E0 + E1
        w1 = [at(TO, E0 * 2, P, parts=C + 1), at(TO + E0 * 2 * P, E1, P, parts=C + 1)]; TO += 2 * E0 * 2 * P
        w2 = [at(TO, 16, C), at(TO + 16 * C, 16, C)]; TO += 32 * C
        b2 = [at(TO, C, parts=E0), at(TO + C, C, parts=E1)]; TO += 2 * C
        wqT, wkT, wvT, woT = (at(TO + i * C, C, parts=C) for i in range(4)); TO += 4 * C
        wqk0 = at(TO, 2, parts=C); TO += 2
        bqk0_b = at(TO, 2); TO += 2
        bq_c, bk_c = at(TO, 1, parts=C), at(TO + 1, 1, parts=C); TO += 2
        bv_b, bo_b, gamma_b, beta_b = (at(TO + i * C, C) for i in range(4)); TO += 4 * C
        rank = at(TO, E1); TO += E1
        xg = at(TO, 4, C); TO += 4 * C
        xT = at(TO, BK, parts=C); TO += BK
        work = TO

        tok_loaded, ln_step, rms_step, attn_step = sem("tok_loaded"), sem("ln_step"), sem("rms_step"), sem("attn_step")
        gate_step, top_step, self_step = sem("gate_step"), sem("top_step"), sem("self_step")

        def steps(*names):
            return {n: i + 2 for i, n in enumerate(names)}, len(names)

        def over_c(v):
            return v.unsqueeze(2).to_broadcast([P, NT, C])

        def row4(v, n=4, w=C):
            return v.unsqueeze(1).to_broadcast([v.shape[0], n, w])

        def sync_load_tokens(sp):
            load = lambda dst, src: sp.dma_start(dst, src).then_inc(tok_loaded, 16)
            row = lambda name: d[name].rearrange("(a c) -> a c", a=1)
            load(h_tok, tok.rearrange("a (r x) -> (a r) x", r=GI).rearrange("(t p) c -> p t c", p=P))
            load(wqkv, d["w_qkv"])
            load(w_out, d["w_out"])
            load(gpre_b, row("g_pre").to_broadcast([P, C]))
            load(gout_b, row("g_out").to_broadcast([P, C]))
            load(bout_b, row("b_out").to_broadcast([P, C]))
            load(memk, d["mem_k"])
            for u in range(2):
                load(vmem[u], d["mem_v"].unsqueeze(1).to_broadcast([MEM, GI // 2, HID]))
            load(headmask, d["c_headmask"])
            load(rank, d["c_rank"].to_broadcast([P, E1]))
            for m in range(2):
                load(wg[m], d[f"wg{m}"])
                load(bg_b[m], row(f"bg{m}").to_broadcast([P, (E0, E1)[m]]))
                load(w1[m][0:C], d[f"w1_{m}"])
                load(w1[m][C:C + 1].rearrange("p i h -> p (i h)"), row(f"b1_{m}"))
                load(w2[m], d[f"w2_{m}"])
                load(b2[m], d[f"b2_{m}"])
            for dst, name in ((wqT, "wq_t"), (wkT, "wk_t"), (wvT, "wv_t"), (woT, "wo_t")):
                load(dst, d[name])
            load(wqk0, d["wqk0"])
            load(bqk0_b, row("bqk0").to_broadcast([P, 2]))
            load(bq_c, d["bq"].rearrange("(c a) -> c a", a=1))
            load(bk_c, d["bk"].rearrange("(c a) -> c a", a=1))
            for dst, name in ((bv_b, "bv"), (bo_b, "bo"), (gamma_b, "ln_gamma"), (beta_b, "ln_beta")):
                load(dst, row(name).to_broadcast([P, C]))

        N_TOK = 16 * (7 + 2 + 2 + 12 + 4 + 2 + 2 + 4)

        LN, NLN = steps("sum", "mean", "centre", "square", "sumsq", "var", "root", "inverse", "scale")

        def vector_norm(dve, k, src, dst):
            base = k * NLN
            dve.tensor_reduce(red[:, 0, :], src, AX.X, ALU.add).then_inc(ln_step, 1)
            dve.wait_ge(ln_step, base + LN["sum"])
            dve.tensor_scalar(red[:, 1, :], red[:, 0, :], -1.0 / C, None, ALU.mult).then_inc(ln_step, 1)
            dve.wait_ge(ln_step, base + LN["mean"])
            dve.tensor_tensor(dst, src, over_c(red[:, 1, :]), ALU.add).then_inc(ln_step, 1)
            dve.wait_ge(ln_step, base + LN["centre"])
            dve.tensor_tensor(sq, dst, dst, ALU.mult).then_inc(ln_step, 1)
            dve.wait_ge(ln_step, base + LN["square"])
            dve.tensor_reduce(red[:, 2, :], sq, AX.X, ALU.add).then_inc(ln_step, 1)
            dve.wait_ge(ln_step, base + LN["sumsq"])
            dve.tensor_scalar(red[:, 3, :], red[:, 2, :], 1.0 / C, EPS, ALU.mult, ALU.add).then_inc(ln_step, 1)
            dve.wait_ge(ln_step, base + LN["root"])
            dve.reciprocal(red[:, 5, :], red[:, 4, :]).then_inc(ln_step, 1)
            dve.wait_ge(ln_step, base + LN["inverse"])
            dve.tensor_tensor(dst, dst, over_c(red[:, 5, :]), ALU.mult).then_inc(ln_step, 1)
            dve.wait_ge(ln_step, base + LN["scale"])

        def scalar_norm(act, k):
            act.wait_ge(ln_step, k * NLN + LN["var"])
            act.activation(red[:, 4, :], red[:, 3, :], ACT.Sqrt).then_inc(ln_step, 1)

        RMS, NRMS = steps("square", "sumsq", "root", "floor", "inverse", "scale")

        def vector_rms(dve, k, src):
            base = k * NRMS
            dve.tensor_tensor(sq, src, src, ALU.mult).then_inc(rms_step, 1)
            dve.wait_ge(rms_step, base + RMS["square"])
            dve.tensor_reduce(red[:, 2, :], sq, AX.X, ALU.add).then_inc(rms_step, 1)
            dve.wait_ge(rms_step, base + RMS["root"])
            dve.tensor_scalar(red[:, 5, :], red[:, 4, :], 1e-12, None, ALU.max).then_inc(rms_step, 1)
            dve.wait_ge(rms_step, base + RMS["floor"])
            dve.reciprocal(red[:, 6, :], red[:, 5, :]).then_inc(rms_step, 1)
            dve.wait_ge(rms_step, base + RMS["inverse"])
            dve.tensor_scalar(red[:, 7, :], red[:, 6, :], float(C) ** 0.5, None, ALU.mult).then_inc(rms_step, 1)
            dve.wait_ge(rms_step, base + RMS["scale"])

        def scalar_rms(act, k):
            act.wait_ge(rms_step, k * NRMS + RMS["sumsq"])
            act.activation(red[:, 4, :], red[:, 2, :], ACT.Sqrt).then_inc(rms_step, 1)

        A, NA = steps("xr", "xn", "turn", "xT", "proj", "k_max", "k_top", "k_sub", "k_exp", "k_sum", "k_inv", "kT", "kT_copy",
                      "ctx", "ctx_scale", "ctx_mask", "q_max", "q_sub", "q_exp", "q_sum", "q_inv", "q_scale", "q_norm",
                      "qT", "qT_copy", "att", "att_copy", "out", "out_bias")
        W = work
        vkv = [at(W + i * 512, 4, HID) for i in range(2)]; W += 1024
        vmem = [v[C:C + MEM] for v in vkv]
        ke = at(W, GI, C + MEM); W += GI * (C + MEM)
        kst = at(W, 4, GI); W += 4 * GI
        kTs = at(W, GI, HID, parts=C + MEM); W += GI * HID
        ctx_s = at(W, GI, HID); W += GI * HID
        qs = at(W, 4, HID); W += 4 * HID
        qst = at(W, 4, 16); W += 64
        qT = at(W, BK); W += BK
        attT = at(W, BK); W += BK
        SCALE = HD ** -0.5

        def tensor_attention(pe):
            with pe.Fori(0, TG) as g:
                def at_(s):
                    pe.wait_ge(attn_step, g * NA + A[s])
                    pe.sem_inc(waited[pe.engine], 1)

                at_("xn")
                for t in range(4):
                    mm = pe.transpose(bank[0][0:C, t * P:(t + 1) * P], xg[:, t, :], ident[:])
                mm.then_inc(attn_step, 1)
                at_("xT")
                pe.matmul(bank[1][:], wqkv[:, HID:2 * HID], xT, start=True, stop=True)
                for t in range(4):
                    pe.matmul(bank[2][:, t * P:(t + 1) * P], xT[:, t * P:(t + 1) * P], wqkv[:, 0:HID], start=True, stop=True)
                for b in range(GI):
                    mm = pe.matmul(bank[3 + b // 4][0:C, b % 4 * HID:(b % 4 + 1) * HID], xT[:, b * S:(b + 1) * S],
                                   wqkv[:, 2 * HID:3 * HID], start=True, stop=True)
                mm.then_inc(attn_step, 1)
                at_("k_inv")
                for b in range(GI):
                    mm = pe.transpose(bank[5 + b // 4][0:C + MEM, b % 4 * HID:(b % 4 + 1) * HID], ke[:, b, :], ident[:])
                mm.then_inc(attn_step, 1)
                at_("kT_copy")
                for b in range(GI):
                    mm = pe.matmul(bank[3 + b // 4][:, b % 4 * HID:(b % 4 + 1) * HID], kTs[:, b, :], vkv[b // 4][0:C + MEM, b % 4, :],
                                   start=True, stop=True)
                mm.then_inc(attn_step, 1)
                at_("q_norm")
                for t in range(4):
                    mm = pe.transpose(bank[7][:, t * P:(t + 1) * P], qs[:, t, :], ident[:])
                mm.then_inc(attn_step, 1)
                at_("qT_copy")
                for b in range(GI):
                    mm = pe.matmul(bank[1][:, b * S:(b + 1) * S], ctx_s[:, b, :], qT[:, b * S:(b + 1) * S], start=True, stop=True)
                mm.then_inc(attn_step, 1)
                at_("att_copy")
                for t in range(4):
                    mm = pe.matmul(bank[0][:, t * C:(t + 1) * C], attT[:, t * P:(t + 1) * P], w_out, start=True, stop=True)
                mm.then_inc(attn_step, 1)

        def scalar_attention(act):
            with act.Fori(0, TG) as g:
                at_ = lambda s: act.wait_ge(attn_step, g * NA + A[s])
                at_("turn")
                act.activation(xT, bank[0][0:C, :], ACT.Copy).then_inc(attn_step, 1)
                at_("k_sub")
                act.activation(ke, ke, ACT.Exp).then_inc(attn_step, 1)
                at_("kT")
                for i in range(2):
                    c = act.activation(kTs[:, 4 * i:4 * i + 4, :], bank[5 + i][0:C + MEM, :].rearrange("p (b x) -> p b x", b=4), ACT.Copy)
                c.then_inc(attn_step, 1)
                at_("q_sub")
                act.activation(qs, qs, ACT.Exp).then_inc(attn_step, 1)
                at_("qT")
                act.activation(qT, bank[7][:], ACT.Copy).then_inc(attn_step, 1)
                at_("att")
                act.activation(attT, bank[1][:], ACT.Copy).then_inc(attn_step, 1)

        def vector_attention(dve):
            dve.wait_ge(tok_loaded, N_TOK)
            dve.tensor_reduce(memk_max[:, 0:1], memk, AX.X, ALU.max).then_inc(attn_step, 1)
            vector_norm(dve, 0, h_tok, x_tok)
            vector_rms(dve, 0, x_tok)
            with dve.Fori(0, TG) as g:
                at_ = lambda s: dve.wait_ge(attn_step, g * NA + A[s])

                def then(ins):
                    ins.then_inc(attn_step, 1)

                dve.wait_ge(attn_step, g * NA + 1)
                then(dve.tensor_tensor(xg, x_tok[:, bass.ds(g * 4, 4), :],
                                       red[:, 7, bass.ds(g * 4, 4)].unsqueeze(2).to_broadcast([P, 4, C]), ALU.mult))
                at_("xr")
                then(dve.tensor_tensor(xg, xg, row4(gpre_b), ALU.mult))
                at_("proj")
                for i in range(2):
                    dve.tensor_copy(vkv[i][0:C], bank[3 + i][0:C, :].rearrange("p (b x) -> p b x", b=4))
                k = bank[1][:].rearrange("p (b n) -> p b n", b=GI)
                then(dve.tensor_reduce(kst[:, 0, :], k, AX.X, ALU.max))
                at_("k_max")
                then(dve.tensor_scalar(kst[:, 1, :], kst[:, 0, :], memk_max[:, 0:1], None, ALU.max))
                at_("k_top")
                dve.tensor_tensor(ke[:, :, C:C + MEM], memk.unsqueeze(1).to_broadcast([P, GI, MEM]),
                                  kst[:, 1, :].unsqueeze(2).to_broadcast([P, GI, MEM]), ALU.subtract)
                then(dve.tensor_tensor(ke[:, :, 0:C], k, kst[:, 1, :].unsqueeze(2).to_broadcast([P, GI, C]), ALU.subtract))
                at_("k_exp")
                then(dve.tensor_reduce(kst[:, 2, :], ke, AX.X, ALU.add))
                at_("k_sum")
                then(dve.reciprocal(kst[:, 3, :], kst[:, 2, :]))
                at_("ctx")
                for i in range(2):
                    c = dve.tensor_tensor(ctx_s[:, 4 * i:4 * i + 4, :], bank[3 + i][:].rearrange("p (b x) -> p b x", b=4),
                                          kst[:, 3, 4 * i:4 * i + 4].unsqueeze(2).to_broadcast([P, 4, HID]), ALU.mult)
                then(c)
                at_("ctx_scale")
                then(dve.tensor_tensor(ctx_s, ctx_s, row4(headmask, GI, HID), ALU.mult))
                at_("ctx_mask")
                q = bank[2][:].rearrange("p (a e) -> p a e", e=HD)
                q_s = qs.rearrange("p t (a e) -> p (t a) e", e=HD)
                then(dve.tensor_reduce(qst[:, 0, :], q, AX.X, ALU.max))
                at_("q_max")
                then(dve.tensor_tensor(q_s, q, qst[:, 0, :].unsqueeze(2).to_broadcast([P, 16, HD]), ALU.subtract))
                at_("q_exp")
                then(dve.tensor_reduce(qst[:, 1, :], q_s, AX.X, ALU.add))
                at_("q_sum")
                then(dve.reciprocal(qst[:, 2, :], qst[:, 1, :]))
                at_("q_inv")
                then(dve.tensor_scalar(qst[:, 3, :], qst[:, 2, :], SCALE, None, ALU.mult))
                at_("q_scale")
                then(dve.tensor_tensor(q_s, q_s, qst[:, 3, :].unsqueeze(2).to_broadcast([P, 16, HD]), ALU.mult))
                at_("out")
                then(dve.tensor_tensor(o_tok[:, bass.ds(g * 4, 4), :], bank[0][:, 0:4 * C].rearrange("p (t c) -> p t c", t=4),
                                       row4(bout_b), ALU.add))
            dve.wait_ge(attn_step, TG * NA + 1)
            vector_rms(dve, 1, o_tok)
            for i, (a, b) in enumerate(((o_tok, over_c(red[:, 7, :])), (o_tok, row4(gout_b, NT)))):
                dve.tensor_tensor(a, a, b, ALU.mult).then_inc(attn_step, 1)
                dve.wait_ge(attn_step, TG * NA + i + 2)
            dve.tensor_tensor(o_tok, o_tok, x_tok, ALU.add).then_inc(attn_step, 1)
            dve.wait_ge(attn_step, TG * NA + 4)
            dve.tensor_tensor(h_tok, h_tok, o_tok, ALU.add).then_inc(attn_step, 1)
            dve.wait_ge(attn_step, TG * NA + 5)

        ME = (E0, E1)
        HT = (2, 1)
        G, NGS = steps("xg", "turn", "xT", "gate", "score")
        T_, NTS = steps("m1", "eq1", "rk1", "top1", "oh1", "keep", "rest", "low", "m2", "eq2", "rk2", "top2", "oh2",
                        "diff", "p", "p1", "r1", "r2", "c1", "c2", "comb")
        W = work
        score, s2, oh1, oh2, tw = (at(W + i * NT * E1, NT, E1) for i in range(5)); W += 5 * NT * E1
        comb = at(W, NT, E1); W += NT * E1
        tp = at(W, 8, NT); W += 8 * NT
        hid = [at(W + i * BK, BK) for i in range(4)]; W += 4 * BK
        x_st = [at(W + i * 4 * (C + 1), 4, C + 1) for i in range(2)]; W += 8 * (C + 1)
        x_sc = [at(W + i * 4 * (C + 1), 4, C + 1) for i in range(2)]; W += 8 * (C + 1)
        xeT = [at(W + i * BK, BK, parts=C + 1) for i in range(2)]; W += 2 * BK
        c_st = [at(W + i * 4 * E1, 4, E1) for i in range(2)]; W += 8 * E1
        combT = at(W, BK, parts=E1); W += BK
        yT = at(W, BK, parts=C); W += BK
        ones_set, staged, x_scaled, x_turned, x_copied = (
            sem("ones_set"), sem("staged"), sem("x_scaled"), sem("x_turned"), sem("x_copied"))
        hid_done, ex_used, relu_done = sem("hid_done"), sem("ex_used"), [sem("relu_by_act"), sem("relu_by_dve")]
        c_turned, c_copied = sem("c_turned"), sem("c_copied")
        y_sum, ysum_copied, ysum_turned, ysum_taken = sem("y_sum"), sem("ysum_copied"), sem("ysum_turned"), sem("ysum_taken")

        def tensor_gate(pe, m):
            with pe.Fori(0, TG) as g:
                def at_(s):
                    pe.wait_ge(gate_step, (m * TG + g) * NGS + G[s])
                    pe.sem_inc(waited[pe.engine], 1)

                at_("xg")
                for t in range(4):
                    mm = pe.transpose(bank[0][0:C, t * P:(t + 1) * P], xg[:, t, :], ident[:])
                mm.then_inc(gate_step, 1)
                at_("xT")
                for t in range(4):
                    mm = pe.matmul(bank[1][:, t * ME[m]:(t + 1) * ME[m]], xT[:, t * P:(t + 1) * P], wg[m], start=True, stop=True)
                mm.then_inc(gate_step, 1)

        def scalar_gate(act, m):
            with act.Fori(0, TG) as g:
                act.wait_ge(gate_step, (m * TG + g) * NGS + G["turn"])
                act.activation(xT, bank[0][0:C, :], ACT.Copy).then_inc(gate_step, 1)

        def vector_gate(dve, m):
            with dve.Fori(0, TG) as g:
                base = (m * TG + g) * NGS
                dve.wait_ge(gate_step, base + 1)
                dve.tensor_scalar(xg, x_tok[:, bass.ds(g * 4, 4), :], 1.0, None, ALU.mult).then_inc(gate_step, 1)
                dve.wait_ge(gate_step, base + G["gate"])
                dve.tensor_tensor(score[:, bass.ds(g * 4, 4), 0:ME[m]], bank[1][:, 0:4 * ME[m]].rearrange("p (t e) -> p t e", t=4),
                                  row4(bg_b[m], 4, ME[m]), ALU.add).then_inc(gate_step, 1)

        def vector_top2(dve, m):
            E = ME[m]
            base = m * NTS
            f = lambda v: v[:, :, 0:E]
            e = lambda v: v.unsqueeze(2).to_broadcast([P, NT, E])
            sc, lo, o1, o2, w, cb = (f(v) for v in (score, s2, oh1, oh2, tw, comb))
            rk = rank[:, 0:E].unsqueeze(1).to_broadcast([P, NT, E])
            at_ = lambda s: dve.wait_ge(top_step, base + T_[s])
            then = lambda ins: ins.then_inc(top_step, 1)

            def pick(s, one, i, n):
                then(dve.tensor_reduce(tp[:, i, :], s, AX.X, ALU.max))
                at_("m" + n)
                then(dve.tensor_tensor(one, s, e(tp[:, i, :]), ALU.is_equal))
                at_("eq" + n)
                then(dve.tensor_tensor(w, one, rk, ALU.mult))
                at_("rk" + n)
                then(dve.tensor_reduce(tp[:, 2, :], w, AX.X, ALU.max))
                at_("top" + n)
                then(dve.tensor_tensor(one, w, e(tp[:, 2, :]), ALU.is_equal))
                at_("oh" + n)

            pick(sc, o1, 0, "1")
            then(dve.tensor_scalar(w, o1, -1.0, 1.0, ALU.mult, ALU.add))
            at_("keep")
            then(dve.tensor_tensor(lo, sc, w, ALU.mult))
            at_("rest")
            then(dve.scalar_tensor_tensor(out=lo, in0=o1, scalar=-3.0e38, in1=lo, op0=ALU.mult, op1=ALU.add))
            at_("low")
            pick(lo, o2, 1, "2")
            then(dve.tensor_tensor(tp[:, 3, :], tp[:, 1, :], tp[:, 0, :], ALU.subtract))
            at_("p")
            then(dve.tensor_scalar(tp[:, 5, :], tp[:, 4, :], 1.0, None, ALU.add))
            at_("p1")
            then(dve.reciprocal(tp[:, 6, :], tp[:, 5, :]))
            at_("r1")
            then(dve.tensor_tensor(tp[:, 7, :], tp[:, 4, :], tp[:, 6, :], ALU.mult))
            at_("r2")
            then(dve.tensor_tensor(w, o1, e(tp[:, 6, :]), ALU.mult))
            at_("c1")
            then(dve.tensor_tensor(lo, o2, e(tp[:, 7, :]), ALU.mult))
            at_("c2")
            then(dve.tensor_tensor(cb, w, lo, ALU.add))
            at_("comb")

        def scalar_top2(act, m):
            act.wait_ge(top_step, m * NTS + T_["diff"])
            act.activation(tp[:, 4, :], tp[:, 3, :], ACT.Exp).then_inc(top_step, 1)

        HN = ME[0] * HT[0]
        assert HN == ME[1] * HT[1] and HN % 4 == 0

        def passes(eng, m):
            loop = eng.Fori(0, TG // 2)
            return loop, lambda r: (r * 2 + m * TG, r * (2 * HN) + m * TG * HN, r * (2 * ME[m]) + m * TG * ME[0])

        def tensor_experts(pe, m):
            if m == 0:
                pe.sem_inc(x_turned, 2)
                pe.sem_inc(hid_done, 4)
                pe.sem_inc(ex_used, 4)
                pe.sem_inc(y_sum, 1)
                pe.sem_inc(ysum_turned, 1)
                pe.sem_inc(c_turned, 2)
            loop, before = passes(pe, m)
            E, H = ME[m], HT[m]
            with loop as r:
                gb, hb, eb = before(r)

                def held():
                    pe.sem_inc(waited[pe.engine], 1)

                def turn(e):
                    pe.wait_ge(x_scaled, eb + (e + 1))
                    pe.wait_ge(x_copied, eb + (e + 1))
                    held()
                    for t in range(4):
                        mm = pe.transpose(bank[e % 2][0:C + 1, t * P:(t + 1) * P], x_sc[e % 2][:, t, :], ident[:])
                    mm.then_inc(x_turned, 1)

                def hidden(i):
                    pe.wait_ge(x_copied, eb + (i // H + 3))
                    pe.wait_ge(relu_done[i % 2], hb // 2 + (i // 2 + 1))
                    held()
                    pe.matmul(bank[2 + i % 4][:], w1[m][:, i % HN, :], xeT[i // H % 2], start=True, stop=True).then_inc(hid_done, 1)

                def second(i):
                    if i % HN == 0:
                        pe.wait_ge(ysum_copied, gb + (i // HN + 1))
                    pe.wait_ge(relu_done[i % 2], hb // 2 + (i // 2 + 3))
                    held()
                    pe.matmul(bank[6][0:C, :], w2[m][:, i % HN, :], hid[i % 4], start=(i % HN == 0), stop=False).then_inc(ex_used, 1)

                def bias(u):
                    pe.wait_ge(c_copied, gb + (u + 1))
                    held()
                    pe.matmul(bank[6][0:C, :], b2[m], combT[0:E], start=False, stop=True).then_inc(y_sum, 1)

                def turn_comb(u):
                    pe.wait_ge(staged, gb + (u + 1))
                    pe.wait_ge(ysum_taken, gb + (u + 1))
                    held()
                    for t in range(4):
                        mm = pe.transpose(bank[7][0:E, t * P:(t + 1) * P], c_st[u][:, t, 0:E], ident[:])
                    mm.then_inc(c_turned, 1)

                def turn_y(u):
                    pe.wait_ge(ysum_copied, gb + (u + 2))
                    held()
                    for t in range(4):
                        mm = pe.transpose(bank[7][:, t * C:(t + 1) * C], yT[:, t * P:(t + 1) * P], ident[0:C, 0:C])
                    mm.then_inc(ysum_turned, 1)

                turn(0)
                turn(1)
                for i in range(2 * HN + 2):
                    if i < 2 * HN:
                        hidden(i)
                        if i % H == H - 1 and i // H + 2 < 2 * E:
                            turn(i // H + 2)
                    if i in (3, HN + 6):
                        turn_comb(i // HN)
                    if i >= 2:
                        second(i - 2)
                        if (i - 2) % HN == HN - 1:
                            bias((i - 2) // HN)
                    if i == HN + 4:
                        turn_y(0)
                turn_y(1)

        def scalar_experts(act, m):
            if m == 0:
                act.sem_inc(x_copied, 2)
                act.sem_inc(relu_done[0], 2)
                act.sem_inc(ysum_copied, 1)
            loop, before = passes(act, m)
            E, H = ME[m], HT[m]
            with loop as r:
                gb, hb, eb = before(r)

                def copy_x(e):
                    act.wait_ge(x_turned, eb + (e + 3))
                    act.wait_ge(hid_done, hb + ((e - 1) * H + 4))
                    act.activation(xeT[e % 2], bank[e % 2][0:C + 1, :], ACT.Copy).then_inc(x_copied, 1)

                def copy_y(u):
                    act.wait_ge(ysum_turned, gb + (u + 1))
                    act.wait_ge(y_sum, gb + (u + 2))
                    act.activation(yT, bank[6][0:C, :], ACT.Copy).then_inc(ysum_copied, 1)

                copy_x(0)
                copy_x(1)
                for i in range(2 * HN):
                    if i % 2 == 0:
                        act.wait_ge(hid_done, hb + (i + 5))
                        act.wait_ge(ex_used, hb + (i + 1))
                        act.activation(hid[i % 4], bank[2 + i % 4][:], ACT.Relu).then_inc(relu_done[0], 1)
                    if i % H == H - 1 and i // H + 2 < 2 * E:
                        copy_x(i // H + 2)
                    if i == HN + 1:
                        copy_y(0)
                copy_y(1)

        def vector_experts(dve, m):
            if m == 0:
                dve.sem_inc(relu_done[1], 2)
                dve.sem_inc(ysum_taken, 1)
            for u in range(2):
                dve.memset(x_st[u][:, :, C:C + 1], 1.0).then_inc(ones_set, 1)
            dve.wait_ge(ones_set, 2 * m + 2)
            loop, before = passes(dve, m)
            E, H = ME[m], HT[m]
            with loop as r:
                gb, hb, eb = before(r)

                def stage(u):
                    dve.wait_ge(c_turned, gb + (u + 1))
                    dve.tensor_scalar(x_st[u][:, :, 0:C], x_tok[:, bass.ds(r * 8 + 4 * u, 4), :], 1.0, None, ALU.mult)
                    dve.tensor_scalar(c_st[u][:, :, 0:E], comb[:, bass.ds(r * 8 + 4 * u, 4), 0:E], 1.0, None, ALU.mult).then_inc(staged, 1)

                def scale_x(e):
                    u = e // E
                    if e % E == 0:
                        dve.wait_ge(staged, gb + (u + 1))
                    dve.wait_ge(x_turned, eb + (e + 1))
                    dve.tensor_tensor(x_sc[e % 2], x_st[u], c_st[u][:, :, e % E:e % E + 1].to_broadcast([P, 4, C + 1]),
                                      ALU.mult).then_inc(x_scaled, 1)

                def copy_comb(u):
                    dve.wait_ge(y_sum, gb + (u + 1))
                    dve.wait_ge(c_turned, gb + (u + 3))
                    dve.tensor_scalar(combT[0:E], bank[7][0:E, :], 1.0, None, ALU.mult).then_inc(c_copied, 1)

                def take_y(u):
                    dve.wait_ge(ysum_turned, gb + (u + 2))
                    dve.tensor_scalar(o_tok[:, bass.ds(r * 8 + 4 * u, 4), :],
                                      bank[7][:, 0:4 * C].rearrange("p (t c) -> p t c", t=4), 1.0, None, ALU.mult).then_inc(ysum_taken, 1)

                stage(0)
                scale_x(0)
                scale_x(1)
                stage(1)
                for i in range(2 * HN):
                    if i % H == 0 and i // H + 2 < 2 * E:
                        scale_x(i // H + 2)
                    if i % 2 == 1:
                        dve.wait_ge(hid_done, hb + (i + 5))
                        dve.wait_ge(ex_used, hb + (i + 1))
                        dve.tensor_scalar(hid[i % 4], bank[2 + i % 4][:], 0.0, None, ALU.max).then_inc(relu_done[1], 1)
                    if i in (3, HN + 6):
                        copy_comb(i // HN)
                    if i == HN + 4:
                        take_y(0)
                take_y(1)

        F, NF = steps("xg", "turn", "xT", "proj", "qT", "kT", "v", "zero_sum", "zero_test", "mask", "score", "s_max", "s_sub", "s_exp",
                      "s_sum", "s_inv", "s_mask", "s_norm", "pT", "pT_copy", "att", "att_copy", "out", "bias", "add")
        W = work
        qT1, kT1 = at(W, BK, parts=C), at(W + BK, BK, parts=C); W += 2 * BK
        v1 = at(W, GI, C, parts=C); W += GI * C
        zt = at(W, 4, 2); W += 8
        mk = at(W, 4); W += 4
        pr = at(W, 4, C); W += 4 * C
        ps_ = at(W, 4, 4); W += 16
        pT = at(W, BK, parts=C); W += BK
        oT = at(W, BK, parts=C); W += BK
        ob = at(W, 4, C); W += 4 * C

        def tensor_self(pe):
            with pe.Fori(0, TG) as g:
                def at_(s):
                    pe.wait_ge(self_step, g * NF + F[s])
                    pe.sem_inc(waited[pe.engine], 1)

                at_("xg")
                for t in range(4):
                    mm = pe.transpose(bank[0][0:C, t * P:(t + 1) * P], xg[:, t, :], ident[:])
                mm.then_inc(self_step, 1)
                at_("xT")
                pe.matmul(bank[1][0:C, :], wqT, xT, start=True, stop=True)
                pe.matmul(bank[2][0:C, :], wkT, xT, start=True, stop=True)
                for b in range(GI):
                    pe.matmul(bank[3][0:C, b * C:(b + 1) * C], xT[:, b * S:(b + 1) * S], wvT, start=True, stop=True)
                for t in range(4):
                    mm = pe.matmul(bank[4][:, 2 * t:2 * t + 2], xT[:, t * P:(t + 1) * P], wqk0, start=True, stop=True)
                mm.then_inc(self_step, 1)
                at_("mask")
                for b in range(GI):
                    hp = slice(b % 2 * C, (b % 2 + 1) * C)
                    mm = pe.matmul(bank[5][hp, b // 2 * C:(b // 2 + 1) * C], qT1[:, b * S:(b + 1) * S], kT1[:, b * S:(b + 1) * S],
                                   start=True, stop=True)
                mm.then_inc(self_step, 1)
                at_("s_norm")
                for t in range(4):
                    mm = pe.transpose(bank[6][0:C, t * P:(t + 1) * P], pr[:, t, :], ident[:])
                mm.then_inc(self_step, 1)
                at_("pT_copy")
                for b in range(GI):
                    mm = pe.matmul(bank[7][0:C, b * S:(b + 1) * S], v1[:, b, :], pT[:, b * S:(b + 1) * S], start=True, stop=True)
                mm.then_inc(self_step, 1)
                at_("att_copy")
                for t in range(4):
                    mm = pe.matmul(bank[0][:, t * C:(t + 1) * C], oT[:, t * P:(t + 1) * P], woT, start=True, stop=True)
                mm.then_inc(self_step, 1)

        def scalar_self(act):
            with act.Fori(0, TG) as g:
                at_ = lambda s: act.wait_ge(self_step, g * NF + F[s])
                at_("turn")
                act.activation(xT, bank[0][0:C, :], ACT.Copy).then_inc(self_step, 1)
                at_("proj")
                act.activation(qT1, bank[1][0:C, :], ACT.Identity, bias=bq_c).then_inc(self_step, 1)
                at_("s_sub")
                act.activation(pr, pr, ACT.Exp, scale=float(C) ** -0.5).then_inc(self_step, 1)
                at_("pT")
                act.activation(pT, bank[6][0:C, :], ACT.Copy).then_inc(self_step, 1)
                at_("att")
                act.activation(oT, bank[7][0:C, :], ACT.Copy).then_inc(self_step, 1)

        def vector_self(dve):
            with dve.Fori(0, TG) as g:
                at_ = lambda s: dve.wait_ge(self_step, g * NF + F[s])
                then = lambda ins: ins.then_inc(self_step, 1)
                dve.wait_ge(self_step, g * NF + 1)
                then(dve.tensor_scalar(xg, x_tok[:, bass.ds(g * 4, 4), :], 1.0, None, ALU.mult))
                at_("qT")
                then(dve.tensor_scalar(kT1, bank[2][0:C, :], bk_c, None, ALU.add))
                at_("kT")
                then(dve.tensor_tensor(v1, bank[3][0:C, :].rearrange("p (b c) -> p b c", b=GI), row4(bv_b[0:C], GI), ALU.add))
                at_("v")
                then(dve.tensor_tensor(zt, bank[4][:, 0:8].rearrange("p (t a) -> p t a", t=4), row4(bqk0_b, 4, 2), ALU.add))
                at_("zero_sum")
                then(dve.tensor_scalar(zt, zt, 0.0, None, ALU.not_equal))
                at_("zero_test")
                then(dve.tensor_tensor(mk, zt[:, :, 0], zt[:, :, 1], ALU.mult))
                at_("score")
                sc = bank[5][:, 0:4 * C].rearrange("p (t j) -> p t j", t=4)
                then(dve.tensor_reduce(ps_[:, 0, :], sc, AX.X, ALU.max))
                at_("s_max")
                then(dve.tensor_tensor(pr, sc, ps_[:, 0, :].unsqueeze(2).to_broadcast([P, 4, C]), ALU.subtract))
                at_("s_exp")
                then(dve.tensor_reduce(ps_[:, 1, :], pr, AX.X, ALU.add))
                at_("s_sum")
                then(dve.reciprocal(ps_[:, 2, :], ps_[:, 1, :]))
                at_("s_inv")
                then(dve.tensor_tensor(ps_[:, 3, :], ps_[:, 2, :], mk, ALU.mult))
                at_("s_mask")
                then(dve.tensor_tensor(pr, pr, ps_[:, 3, :].unsqueeze(2).to_broadcast([P, 4, C]), ALU.mult))
                at_("out")
                then(dve.tensor_tensor(ob, bank[0][:, 0:4 * C].rearrange("p (t c) -> p t c", t=4), row4(bo_b), ALU.add))
                at_("bias")
                hg = h_tok[:, bass.ds(g * 4, 4), :]
                then(dve.tensor_tensor(hg, hg, ob, ALU.add))
            dve.wait_ge(self_step, TG * NF + 1)

        fin_step, out_stored = sem("fin_step"), sem("out_stored")

        def tail_sync(sp):
            sync_load_tokens(sp)
            sp.wait_ge(fin_step, 6)
            sp.dma_start(out.rearrange("(t p) c -> p t c", p=P), h_tok).then_inc(out_stored, 16)
            sp.wait_ge(out_stored, 16)

        def tail_tensor(pe):
            pe.wait_ge(tok_loaded, N_TOK)
            tensor_attention(pe)
            for m in range(2):
                if m == 1:
                    tensor_self(pe)
                tensor_gate(pe, m)
                tensor_experts(pe, m)

        def tail_scalar(act):
            act.wait_ge(tok_loaded, N_TOK)
            scalar_norm(act, 0)
            scalar_rms(act, 0)
            scalar_attention(act)
            scalar_rms(act, 1)
            for m in range(2):
                if m == 1:
                    scalar_norm(act, 2)
                    scalar_self(act)
                scalar_norm(act, (1, 3)[m])
                scalar_gate(act, m)
                scalar_top2(act, m)
                scalar_experts(act, m)
            scalar_norm(act, 4)

        def tail_vector(dve):
            for s in (ln_step, rms_step, gate_step, top_step, self_step):
                dve.sem_inc(s, 1)
            vector_attention(dve)
            for m in range(2):
                if m == 1:
                    vector_norm(dve, 2, h_tok, x_tok)
                    vector_self(dve)
                vector_norm(dve, (1, 3)[m], h_tok, x_tok)
                vector_gate(dve, m)
                dve.wait_ge(gate_step, (m + 1) * (TG * NGS) + 1)
                vector_top2(dve, m)
                vector_experts(dve, m)
                dve.wait_ge(ysum_taken, (m + 1) * TG + 1)
                if m == 0:
                    dve.tensor_tensor(h_tok, h_tok, o_tok, ALU.add).then_inc(fin_step, 1)
                    dve.wait_ge(fin_step, 1)
            dve.tensor_tensor(x_tok, x_tok, o_tok, ALU.add).then_inc(fin_step, 1)
            dve.wait_ge(fin_step, 2)
            vector_norm(dve, 4, x_tok, o_tok)
            dve.tensor_tensor(o_tok, o_tok, row4(gamma_b, NT), ALU.mult).then_inc(fin_step, 1)
            dve.wait_ge(fin_step, 3)
            dve.tensor_tensor(o_tok, o_tok, row4(beta_b, NT), ALU.add).then_inc(fin_step, 1)
            dve.wait_ge(fin_step, 4)
            dve.tensor_tensor(h_tok, h_tok, o_tok, ALU.add).then_inc(fin_step, 2)

        block = ctx.enter_context(nc.Block())
        TOWER = 3 * L

        @block.sync
        def _(sp):
            sync_spectrum0(sp)
            phase_end(sp, 1)
            sync_mix(sp, 0, True)
            phase_end(sp, 2)
            sync_inverse(sp, 0, True)
            phase_end(sp, 3)
            with sp.Fori(1, L) as l:
                sync_forward(sp, l - 1, False)
                phase_end(sp, l * 3 + 1)
                sync_mix(sp, l, False)
                phase_end(sp, l * 3 + 2)
                sync_inverse(sp, l, False)
                phase_end(sp, l * 3 + 3)
            sync_head(sp)
            phase_end(sp, TOWER + 1)
            tail_sync(sp)

        @block.tensor
        def _(pe):
            tensor_spectrum0(pe)
            phase_end(pe, 1)
            tensor_mix(pe, 0, True)
            phase_end(pe, 2)
            tensor_inverse(pe, 0, True)
            pe.sem_inc(ht_done, 8 * Q)
            phase_end(pe, 3)
            with pe.Fori(1, L) as l:
                tensor_forward(pe, l - 1)
                phase_end(pe, l * 3 + 1)
                tensor_mix(pe, l, False)
                phase_end(pe, l * 3 + 2)
                tensor_inverse(pe, l, False)
                phase_end(pe, l * 3 + 3)
            tensor_head(pe)
            phase_end(pe, TOWER + 1)
            tail_tensor(pe)

        @block.scalar
        def _(act):
            scalar_spectrum0(act)
            phase_end(act, 1)
            scalar_mix(act, 0, True)
            phase_end(act, 2)
            scalar_inverse(act, 0, True)
            act.sem_inc(ft_copied, 2)
            for v in range(2):
                act.sem_inc(spec_stored[v], 64)
            phase_end(act, 3)
            with act.Fori(1, L) as l:
                scalar_forward(act, l - 1, False)
                phase_end(act, l * 3 + 1)
                scalar_mix(act, l, False)
                phase_end(act, l * 3 + 2)
                scalar_inverse(act, l, False)
                phase_end(act, l * 3 + 3)
            scalar_head(act)
            phase_end(act, TOWER + 1)
            tail_scalar(act)

        @block.vector
        def _(dve):
            vector_spectrum0(dve)
            phase_end(dve, 1)
            vector_mix(dve, 0, True)
            phase_end(dve, 2)
            vector_inverse(dve, 0, True)
            dve.sem_inc(ht_copied, 2)
            dve.sem_inc(fc_copied, 2)
            dve.sem_inc(fr_copied, 2)
            phase_end(dve, 3)
            with dve.Fori(1, L) as l:
                vector_forward(dve, l - 1)
                phase_end(dve, l * 3 + 1)
                vector_mix(dve, l, False)
                phase_end(dve, l * 3 + 2)
                vector_inverse(dve, l, False)
                phase_end(dve, l * 3 + 3)
            vector_head(dve)
            phase_end(dve, TOWER + 1)
            tail_vector(dve)

        @block.gpsimd
        def _(pool):
            gpsimd_spectrum0(pool)
            phase_end(pool, 1)
            phase_end(pool, 2)
            gpsimd_inverse(pool, 0, True)
            phase_end(pool, 3)
            with pool.Fori(1, L) as l:
                phase_end(pool, l * 3 + 1)
                phase_end(pool, l * 3 + 2)
                gpsimd_inverse(pool, l, False)
                phase_end(pool, l * 3 + 3)
            gpsimd_head(pool, tok)
            phase_end(pool, TOWER + 1)
            pass


def block_layout(t, E, H):
    return np.ascontiguousarray(t.transpose(2, 0, 1).reshape(C, E * (H // P), P))


def kernel(x, **inputs):
    import concourse.bacc as bacc
    from concourse.bass_utils import run_bass_kernel_spmd as run

    v = {k: np.asarray(a) for k, a in inputs.items()}
    tower = {k[len("L0_tok_"):]: a for k, a in v.items() if k.startswith("L0_tok_")}
    arrays = dft_constants()
    arrays.update(tower_layout(x, *(tower[k] for k in ("fc0_w", "fc0_b", "w1r", "w1i", "w2r", "w2i", "pw_w"))))
    for k in ("pw_b", "gamma", "beta", "fc1_w", "fc1_b", "fc2_w", "fc2_b"):
        arrays[k] = tower[k]
    for k in ("w_qkv", "w_out", "b_out", "g_out", "g_pre"):
        arrays[k] = v["L0_attn_" + k]
    mem = v["L0_attn_mem_kv"]
    arrays["mem_k"] = np.ascontiguousarray(mem[0].reshape(P, -1))
    arrays["mem_v"] = np.ascontiguousarray(mem[1].reshape(P, -1).T)
    head = np.arange(P) // 32
    arrays["c_headmask"] = (head[:, None] == head[None, :]).astype(np.float32)
    arrays["c_rank"] = (16 - np.arange(16, dtype=np.float32))[None, :]
    arrays["wg0"] = np.ascontiguousarray(v["L0_ffn_Wg"].T)
    arrays["bg0"] = v["L0_ffn_bg"]
    W1, W2 = v["L0_ffn_W1"], v["L0_ffn_W2"]
    E, H, _ = W1.shape
    arrays["w1_0"] = block_layout(W1, E, H)
    arrays["b1_0"] = v["L0_ffn_b1"].reshape(-1)
    arrays["w2_0"] = np.ascontiguousarray(W2.transpose(0, 2, 1).reshape(E * H // P, P, C).transpose(1, 0, 2))
    arrays["b2_0"] = v["L0_ffn_b2"]
    arrays["wg1"] = v["L1_ffn_gate_w"]
    arrays["bg1"] = v["L1_ffn_gate_b"]
    arrays["w1_1"] = np.ascontiguousarray(v["L1_ffn_w1"].transpose(1, 0, 2))
    arrays["b1_1"] = v["L1_ffn_b1"].reshape(-1)
    arrays["w2_1"] = np.ascontiguousarray(v["L1_ffn_w2"].transpose(1, 0, 2))
    arrays["b2_1"] = v["L1_ffn_b2"]
    arrays["ln_gamma"], arrays["ln_beta"] = v["L1_ffn_gamma"], v["L1_ffn_beta"]
    for k in "qkvo":
        arrays[f"w{k}_t"] = np.ascontiguousarray(v["L1_attn_W" + k].T)
        arrays[f"b{k}"] = v["L1_attn_b" + k]
    arrays["wqk0"] = np.stack([v["L1_attn_Wq"][0], v["L1_attn_Wk"][0]], 1)
    arrays["bqk0"] = np.stack([v["L1_attn_bq"][0], v["L1_attn_bk"][0]])

    nc = bacc.Bacc("TRN2", target_bir_lowering=False, num_devices=1)
    d = {k: nc.dram_tensor("in_" + k, a.shape, F32, kind="ExternalInput").ap() for k, a in arrays.items()}
    B = x.shape[0]
    out = nc.dram_tensor("out", [B * S, S], F32, kind="ExternalOutput").ap()
    build(nc, d, B, out)
    r = run(nc, [{"in_" + k: a for k, a in arrays.items()}], core_ids=[0])
    return r.results[0]["out"].reshape(B, S, S)
```

```python
from contextlib import ExitStack

import numpy as np

import concourse.bass as bass
from concourse import mybir

F32 = mybir.dt.float32
F16 = mybir.dt.float16
ACT = mybir.ActivationFunctionType
ALU = mybir.AluOpType
AX = mybir.AxisListType

P = 128
C = 64
S = 64
PX = S * S
M1, M2 = 16, 16
K1 = 2 * M1
L = 4
CH = 4
NCH = K1 // CH
MC = CH * M2
Q = 4
GI = 2 * Q
BK = 512
EPS = 1e-5
ENGINES = 5


def dft_constants():
    h = np.arange(S)
    k1 = np.concatenate([np.arange(M1), np.arange(S - M1, S)])
    k2 = np.arange(M2)
    w_ang = 2 * np.pi * np.outer(h, k2) / S
    h_ang = 2 * np.pi * np.outer(h, k1) / S
    fw2 = np.kron(np.eye(2), np.stack([np.cos(w_ang), -np.sin(w_ang)], -1).reshape(S, 2 * M2))
    gh = np.block([[np.cos(h_ang), -np.sin(h_ang)], [np.sin(h_ang), np.cos(h_ang)]])
    ga = np.block([[np.cos(h_ang).T, np.sin(h_ang).T], [-np.sin(h_ang).T, np.cos(h_ang).T]]) / S
    ga = ga.reshape(2 * K1, 2, S)
    ga = np.stack([np.roll(ga, 2, axis=2), ga], 1)
    fb = np.stack([2 * np.cos(w_ang).T, -2 * np.sin(w_ang).T], 1)
    fb[0, 0], fb[0, 1] = 1.0, 0.0
    fb2 = np.kron(np.eye(2), fb.reshape(2 * M2, S) / S)
    g0 = np.stack([np.kron(np.eye(2), np.cos(h_ang)), np.kron(np.eye(2), -np.sin(h_ang))], 1)
    cs, sn = np.cos(w_ang), np.sin(w_ang)
    part = np.stack([np.stack([cs, -sn], 1), np.stack([sn, cs], 1)], 0)
    f0 = np.einsum("pwrk,ij->pwirjk", part, np.eye(3)).reshape(2, 2, 96, 6 * M2).transpose(2, 0, 1, 3)
    dc = np.zeros((1, K1))
    dc[0, 0] = PX
    consts = {"c_fw2": fw2, "c_gh": gh, "c_ga": ga.reshape(2 * K1, 4 * S), "c_fb2": fb2, "c_g0": g0.reshape(P, 4 * K1),
              "c_f0": f0.reshape(96, 4, 96), "c_dc": dc, "c_ident": np.eye(P),
              "c_half": np.kron(np.full((2, 2), 0.5), np.eye(C))}
    return {k: np.ascontiguousarray(v, dtype=np.float32) for k, v in consts.items()}


def tower_layout(x, fc0_w, fc0_b, w1r, w1i, w2r, w2i, pw_w):
    x, fc0_w, fc0_b, pw_w, w1r, w1i, w2r, w2i = (
        np.asarray(t) for t in (x, fc0_w, fc0_b, pw_w, w1r, w1i, w2r, w2i))
    B = x.shape[0]
    out = {}
    out["x_pair"] = np.ascontiguousarray(
        x.reshape(B // GI, 2, Q, PX, 3).transpose(0, 2, 1, 4, 3).reshape(B // 2, 6, PX))
    out["x_rows"] = np.ascontiguousarray(x.reshape(B // 2, 2 * S, S * 3))
    r, i = (np.concatenate(t, 3).reshape(L, C, C, NCH, MC).transpose(0, 3, 1, 4, 2)
            for t in ((w1r, w2r), (w1i, w2i)))
    out["w_modes"] = np.stack([r, i], 2).reshape(L, NCH, P, MC, C)
    out["pw_t"] = np.ascontiguousarray(pw_w.transpose(0, 2, 1))
    f = np.zeros((6 * M2 + 1, M2, 2, C), np.float32)
    for ri in range(2):
        for j in range(3):
            for k in range(M2):
                f[(ri * 3 + j) * M2 + k, k, ri] = fc0_w[j]
    f[6 * M2, 0, 0] = fc0_b
    out["fc0_modes"] = f.reshape(6 * M2 + 1, M2, P)
    out["fc0_t"] = np.ascontiguousarray(fc0_w.T)
    out["fc0_b"] = fc0_b
    return out


def build(nc, d, B, out):
    NP, NG = B // 2, B // GI
    MB = 16
    NB = B // MB

    with ExitStack() as ctx:
        def sem(name):
            return ctx.enter_context(nc.semaphore(name))

        def sb(name, shape):
            return ctx.enter_context(nc.sbuf_tensor(name, shape, F32))

        spec_in = nc.dram_tensor("spec_in", [2, C, NCH, B, MC], F32, kind="Internal").ap()
        spec_out = nc.dram_tensor("spec_out", [NG, 2, K1, C, GI * M2], F32, kind="Internal").ap()
        y_dram = nc.dram_tensor("y_dram", [NP, P, PX], F32, kind="Internal").ap()

        ident = sb("ident", [P, P])
        fw2 = sb("fw2", [P, 4 * M2])
        fw_halves = sb("fw_halves", [P, 4 * M2])
        fw_half = [fw_halves[:].bitcast(F16)[:, j * 4 * M2:(j + 1) * 4 * M2] for j in range(2)]
        gh = sb("gh", [P, 2 * K1])
        ga = sb("ga", [2 * K1, 4 * S])
        fb2 = sb("fb2", [P, 2 * S])
        half = sb("half", [P, P])
        pw = sb("pw", [P, P])
        wst = sb("wst", [P, C])
        pwb = sb("pwb", [P, 1])
        gamma = sb("gamma", [P, 1])
        beta = sb("beta", [P, 1])
        fc0t = sb("fc0t", [P, P])
        fc0b = sb("fc0b", [P, 1])
        scale = sb("scale", [P, 1])
        shift = sb("shift", [P, 1])
        bn = sb("bn", [P, 12])
        stats = sb("stats", [P, NP * 48])
        fc1 = sb("fc1", [P, P])
        fc1b = sb("fc1b", [P, 1])
        fc2 = sb("fc2", [P, 1])
        fc2b = sb("fc2b", [P, 1])
        ARENA = 45800
        arena = sb("arena", [P, ARENA])

        def at(off, *shape, parts=P):
            n = int(np.prod(shape))
            assert off + n <= ARENA, (off, shape)
            v = arena[0:parts, off:off + n]
            if len(shape) == 2:
                v = v.rearrange("p (a b) -> p a b", a=shape[0])
            if len(shape) == 3:
                v = v.rearrange("p (a b c) -> p a b c", a=shape[0], b=shape[1])
            if len(shape) == 4:
                v = v.rearrange("p (a b c e) -> p a b c e", a=shape[0], b=shape[1], c=shape[2])
            return v

        bank = [ctx.enter_context(nc.psum_tensor(f"bank{i}", [P, BK], F32)) for i in range(8)]

        phase_done = sem("phase_done")
        zeroed = sem("zeroed")
        waited = {e.engine: sem(f"waited_{n}") for n, e in (
            ("sync", nc.sync), ("tensor", nc.tensor), ("scalar", nc.scalar), ("vector", nc.vector), ("gpsimd", nc.gpsimd))}

        def phase_end(eng, n):
            eng.sem_inc(waited[eng.engine], 1)
            eng.drain().then_inc(phase_done, 1)
            eng.wait_ge(phase_done, ENGINES * n)
            eng.sem_inc(waited[eng.engine], 1)

        const_loaded = sem("const_loaded")
        x0_loaded = [sem("x0_loaded_even"), sem("x0_loaded_odd")]
        rows0_done, rows0_copied, cols0_done, cols0_copied = (
            sem("rows0_done"), sem("rows0_copied"), sem("cols0_done"), sem("cols0_copied"))
        fc0_done, fc0_copied, fw_split = sem("fc0_done"), sem("fc0_copied"), sem("fw_split")
        spec0_stored, pw0_done, pw0_copied = sem("spec0_stored"), sem("pw0_done"), sem("pw0_copied")

        x0 = [at(192 * u, 192) for u in range(2)]
        z0 = [at(384 + 256 * u, 256, parts=96) for u in range(2)]
        v0 = at(1024, B, K1, parts=6 * M2 + 1)
        f0m = at(1024 + B * K1, M2, P, parts=6 * M2 + 1)
        f0c = at(1024 + B * K1 + M2 * P, 4, 96, parts=96)
        g0 = at(1024 + B * K1 + M2 * P + 384, P)
        spec0 = [at(8192 + u * NCH * MB * MC, NCH, MB, CH, M2) for u in range(2)]
        assert 1024 + B * K1 + M2 * P + 512 <= 8192

        def sync_spectrum0(sp):
            loads = [(ident[:], "c_ident"), (fw2[:], "c_fw2"), (gh[:], "c_gh"), (ga[:], "c_ga"),
                     (half[:], "c_half"), (f0m, "fc0_modes"), (f0c, "c_f0"), (g0, "c_g0")]
            for dst, name in loads:
                sp.dma_start(dst, d[name]).then_inc(const_loaded, 16)
            for u in range(2):
                sp.dma_start(fb2[u * C:(u + 1) * C, :], d["c_fb2"]).then_inc(const_loaded, 16)
            sp.dma_start(v0[6 * M2:6 * M2 + 1, :, :],
                         d["c_dc"].rearrange("a (b k) -> a b k", b=1).to_broadcast([1, B, K1])).then_inc(const_loaded, 16)
            sp.wait_ge(zeroed, 3)
            for u in range(2):
                half_p = slice(u * C, (u + 1) * C)
                sp.dma_start(fc0b[half_p, :], d["fc0_b"].rearrange("(c a) -> c a", a=1)).then_inc(const_loaded, 16)
                sp.dma_start(fc0t[half_p, C * u:C * u + 3], d["fc0_t"]).then_inc(const_loaded, 16)
                sp.dma_start(pw[half_p, u * C:(u + 1) * C], d["pw_t"][0]).then_inc(const_loaded, 16)
                sp.dma_start(pwb[half_p, :], d["pw_b"][0].rearrange("(c a) -> c a", a=1)).then_inc(const_loaded, 16)
                sp.dma_start(fc1[half_p, :], d["fc1_w"]).then_inc(const_loaded, 16)
            sp.dma_start(fc1b[:], d["fc1_b"].rearrange("(c a) -> c a", a=1)).then_inc(const_loaded, 16)
            sp.dma_start(fc2[:], d["fc2_w"]).then_inc(const_loaded, 16)
            sp.dma_start(fc2b[:], d["fc2_b"].rearrange("(c a) -> c a", a=1).to_broadcast([P, 1])).then_inc(const_loaded, 16)
            with sp.Fori(0, NP // 2) as i:
                for u in range(2):
                    sp.wait_ge(rows0_done, i * 2 + (u + 1))
                    sp.dma_start(x0[u], d["x_rows"][i * 2 + u]).then_inc(x0_loaded[u], 16)

        N_CONST = 16 * (9 + 2 + 10 + 3)

        def tensor_spectrum0(pe):
            pe.sem_inc(rows0_done, 2)
            pe.wait_ge(const_loaded, N_CONST)
            pe.matmul(bank[0][:, 0:P], fc0t[:], pw[:], start=True, stop=True)
            pe.matmul(bank[1][:, 0:1], pw[:], fc0b[:], start=True, stop=True).then_inc(pw0_done, 1)
            pe.wait_ge(pw0_copied, 3)
            with pe.Fori(0, NP // 2) as i:
                for u in range(2):
                    pe.wait_ge(rows0_copied, i * 2 + (u + 1))
                    pe.wait_ge(x0_loaded[u], i * 16 + 16)
                    for wh in range(2):
                        mm = pe.matmul(bank[u][0:96, wh * P:(wh + 1) * P], x0[u][:, wh * 96:(wh + 1) * 96], g0,
                                       start=True, stop=True)
                    mm.then_inc(rows0_done, 1)
                    pe.wait_ge(rows0_copied, i * 2 + (u + 3))
                    pe.wait_ge(cols0_copied, i * 2 + (u + 1))
                    for k in range(4):
                        part, wh = k // 2, k % 2
                        mm = pe.matmul(bank[2 + u][0:96, 0:2 * K1], f0c[:, part * 2 + wh, :],
                                       z0[u][:, wh * P + part * 2 * K1:wh * P + (part + 1) * 2 * K1],
                                       start=(k == 0), stop=(k == 3))
                    mm.then_inc(cols0_done, 1)
            pe.wait_ge(cols0_copied, NP + 2)
            with pe.Fori(0, NB) as t:
                for k in range(M2):
                    pe.wait_ge(fc0_copied, t * M2 + (k + 1))
                    pe.matmul(bank[4 + k % 4][:], f0m[:, k, :],
                              v0[:, bass.ds(t * MB, MB), :].rearrange("p b k -> p (b k)"),
                              start=True, stop=True).then_inc(fc0_done, 1)

        def vector_spectrum0(dve):
            dve.sem_inc(rows0_copied, 2)
            dve.sem_inc(cols0_copied, 2)
            dve.sem_inc(fc0_copied, 4)
            dve.wait_ge(pw0_done, 1)
            dve.wait_ge(const_loaded, N_CONST)
            for u in range(2):
                half_p = slice(u * C, (u + 1) * C)
                dve.tensor_copy(wst[half_p, :], bank[0][half_p, u * C:(u + 1) * C]).then_inc(pw0_copied, 1)
            dve.tensor_tensor(pwb[:], bank[1][:, 0:1], pwb[:], ALU.add).then_inc(pw0_copied, 1)
            dve.tensor_copy(fw_half[0], fw2[:]).then_inc(fw_split, 1)
            dve.wait_ge(fw_split, 1)
            dve.tensor_tensor(fw_half[1], fw2[:], fw_half[0], ALU.subtract).then_inc(fw_split, 1)
            with dve.Fori(0, NP // 2) as i:
                for u in range(2):
                    dve.wait_ge(rows0_done, i * 2 + (u + 3))
                    dve.tensor_copy(z0[u], bank[u][0:96, 0:256]).then_inc(rows0_copied, 1)
                    dve.wait_ge(cols0_done, i * 2 + (u + 1))
                    dve.tensor_scalar(v0[0:96, bass.ds(i * 4 + 2 * u, 2), :].rearrange("p b k -> p (b k)"),
                                      bank[2 + u][0:96, 0:2 * K1], 1.0, None, ALU.mult).then_inc(cols0_copied, 1)
            with dve.Fori(0, NB // 2 if NB > 1 else 1) as t:
                for u in range(2 if NB > 1 else 1):
                    for k in range(M2):
                        dve.wait_ge(fc0_done, t * (2 * M2) + (u * M2 + k + 1))
                        if k == 0:
                            dve.wait_ge(spec0_free, t * 2 + (u + 1))
                        dve.tensor_copy(spec0[u][:, :, :, :, k].rearrange("p h b k -> p b h k"),
                                        bank[4 + k % 4][:].rearrange("p (b h k) -> p b h k", b=MB, h=NCH)).then_inc(fc0_copied, 1)

        spec0_free = sem("spec0_free")

        def scalar_spectrum0(act):
            act.sem_inc(spec0_free, 2)
            for t in range(NB):
                act.wait_ge(fc0_copied, 4 + M2 * (t + 1))
                for ri in range(2):
                    act.dma_start(spec_in[ri, :, :, t * MB:(t + 1) * MB, :],
                                  spec0[t % 2][ri * C:(ri + 1) * C].rearrange("p h b k m -> p h b (k m)")
                                  ).then_inc(spec0_stored, 16)
                act.wait_ge(spec0_stored, 32 * (t + 1))
                act.sem_inc(spec0_free, 1)

        def gpsimd_spectrum0(pool):
            pool.memset(fc0t[:], 0.0).then_inc(zeroed, 1)
            pool.memset(pw[:], 0.0).then_inc(zeroed, 1)
            pool.memset(bn[:], 0.0).then_inc(zeroed, 1)

        w_loaded = [sem("w_loaded_even"), sem("w_loaded_odd")]
        s_loaded = [sem("s_loaded_even"), sem("s_loaded_odd")]
        layer_loaded = sem("layer_loaded")
        imag_up, real_down, imag_negated = sem("imag_up"), sem("real_down"), sem("imag_negated")
        mix_done, mixed_by_act, mixed_by_dve = sem("mix_done"), sem("mixed_by_act"), sem("mixed_by_dve")
        mix_free, mixed_stored = sem("mix_free"), [sem("mixed_stored_even"), sem("mixed_stored_odd")]

        w_sb = [at(u * MC * C, MC, C) for u in range(2)]
        s_sb = [at(2 * MC * C + 2 * u * B * MC, 2, B, MC) for u in range(2)]
        m_sb = [at(2 * MC * C + 4 * B * MC + u * CH * B * M2, CH // 2, 2, B, M2) for u in range(2)]
        IT = NCH // 2

        def sync_mix(sp, l, first):
            def load(u, i2):
                sp.wait_ge(mix_free, l * NCH + (i2 + (u + 1)))
                for ri in range(2):
                    sp.dma_start(s_sb[u][ri * C:(ri + 1) * C, 0], spec_in[ri, :, i2 + u]).then_inc(s_loaded[u], 16)
                sp.dma_start(w_sb[u], d["w_modes"][l, i2 + u]).then_inc(w_loaded[u], 16)

            def store(u, i2):
                n = l * NCH + i2
                sp.wait_ge(mixed_by_act, n * 4 + (4 * u + 8))
                sp.wait_ge(mixed_by_dve, n * 4 + (4 * u + 8))
                for kk in range(CH):
                    h, k = kk // 2, kk % 2
                    for ri in range(2):
                        sp.dma_start(spec_out[:, ri, i2 * CH + (u * CH + kk)].rearrange("g c x -> c g x"),
                                     m_sb[u][h * C:(h + 1) * C, k, ri].rearrange("p (g b) k -> p g (b k)", g=NG)
                                     ).then_inc(mixed_stored[u], 16)

            for u in range(2):
                load(u, 0)
            with sp.Fori(0, IT - 1) as i:
                for u in range(2):
                    store(u, i * 2)
                    load(u, i * 2 + 2)
            for u in range(2):
                store(u, (IT - 1) * 2)
            for u in range(2):
                half_p = slice(u * C, (u + 1) * C)
                for dst, name in ((gamma, "gamma"), (beta, "beta")):
                    sp.dma_start(dst[half_p, :], d[name][l].rearrange("(c a) -> c a", a=1)).then_inc(layer_loaded, 16)
                if not first:
                    sp.dma_start(wst[half_p, :], d["pw_t"][l]).then_inc(layer_loaded, 16)
                    sp.dma_start(pwb[half_p, :], d["pw_b"][l].rearrange("(c a) -> c a", a=1)).then_inc(layer_loaded, 16)
            sp.wait_ge(layer_loaded, l * 128 + 64)
            for u in range(2):
                sp.wait_ge(mixed_stored[u], l * (IT * 128) + (IT * 128 + 128))
            sp.sem_inc(waited[sp.engine], 1)

        def tensor_mix(pe, l, first):
            if first:
                pe.sem_inc(mix_free, 2)
            with pe.Fori(0, IT) as i:
                for u in range(2):
                    n = l * NCH + i * 2
                    pe.wait_ge(w_loaded[u], (l * IT + i) * 16 + 16)
                    pe.wait_ge(real_down, n + (u + 1))
                    pe.wait_ge(imag_up, n + (u + 1))
                    pe.wait_ge(imag_negated, n + (u + 1))
                    for j in range(8):
                        by = mixed_by_act if j % 2 == 0 else mixed_by_dve
                        pe.wait_ge(by, n * 4 + (4 * u + j // 2 + 1))
                        pe.sem_inc(waited[pe.engine], 1)
                        for m in range(4):
                            for h in range(2):
                                mode = h * (MC // 2) + 4 * j + m
                                mm = pe.matmul(bank[j][h * C:(h + 1) * C, m * 2 * B:(m + 1) * 2 * B], w_sb[u][:, mode, :],
                                               s_sb[u][:, :, :, mode], start=True, stop=True)
                        mm.then_inc(mix_done, 1)
                    pe.wait_ge(mix_done, n * 8 + (8 * u + 8))
                    pe.sem_inc(mix_free, 1)

        def mixed_view(u, j):
            k = 4 * (j % 4)
            return [(m_sb[u][:, j // 4, r, :, k:k + 4],
                     bank[j][:, 0:8 * B].rearrange("p (m r b) -> p r b m", m=4, r=2)[:, r]) for r in range(2)]

        def scalar_mix(act, l, first):
            if first:
                act.sem_inc(mixed_by_act, 4)
                act.sem_inc(mixed_stored[0], 16 * 8)
                act.sem_inc(mixed_stored[1], 16 * 8)
            with act.Fori(0, IT) as i:
                for u in range(2):
                    n = l * NCH + i * 2
                    act.wait_ge(s_loaded[u], (l * IT + i) * 32 + 32)
                    act.activation(s_sb[u][0:C, 1], s_sb[u][C:P, 0], ACT.Copy).then_inc(imag_up, 1)
                    act.wait_ge(mixed_stored[u], (l * IT + i) * 128 + 128)
                    for j in range(0, 8, 2):
                        act.wait_ge(mix_done, n * 8 + (8 * u + j + 1))
                        for o, v in mixed_view(u, j):
                            c = act.activation(o, v, ACT.Copy)
                        c.then_inc(mixed_by_act, 1)

        def vector_mix(dve, l, first):
            if first:
                dve.sem_inc(mixed_by_dve, 4)
            with dve.Fori(0, IT) as i:
                for u in range(2):
                    n = l * NCH + i * 2
                    dve.wait_ge(s_loaded[u], (l * IT + i) * 32 + 32)
                    dve.sem_inc(waited[dve.engine], 1)
                    dve.tensor_copy(s_sb[u][C:P, 1], s_sb[u][0:C, 0]).then_inc(real_down, 1)
                    dve.wait_ge(imag_up, n + (u + 1))
                    dve.tensor_scalar(s_sb[u][C:P, 0], s_sb[u][C:P, 0], -1.0, None, ALU.mult).then_inc(imag_negated, 1)
                    dve.wait_ge(mixed_stored[u], (l * IT + i) * 128 + 128)
                    for j in range(1, 8, 2):
                        dve.wait_ge(mix_done, n * 8 + (8 * u + j + 1))
                        for o, v in mixed_view(u, j):
                            c = dve.tensor_copy(o, v)
                        c.then_inc(mixed_by_dve, 1)

        grp_loaded, grp_free, pair_ready = sem("grp_loaded"), sem("grp_free"), sem("pair_ready")
        in_loaded = [[sem(f"in_loaded{u}{v}") for v in range(2)] for u in range(2)]
        h_ready = sem("h_ready")
        rows_done, rows_copied, turn_done, turn_copied = (
            sem("rows_done"), sem("rows_copied"), sem("turn_done"), sem("turn_copied"))
        y_done, y_copied, y_seen = sem("y_done"), sem("y_copied"), sem("y_seen")
        y_stored = [sem("y_stored_even"), sem("y_stored_odd")]
        stat_taken, stat_kept = sem("stat_taken"), sem("stat_kept")
        bn_step, bn_sum, bn_root = sem("bn_step"), sem("bn_sum"), sem("bn_root")

        hin = [[at((2 * u + par) * PX, PX) for par in range(2)] for u in range(2)]
        yout = [at((4 + u) * PX, PX) for u in range(2)]
        O1 = 6 * PX
        grp = at(O1, C, GI, M2, parts=2 * K1)
        O1 += C * GI * M2
        prs = [at(O1 + u * M2 * P, M2, P, parts=2 * K1) for u in range(2)]
        O1 += 2 * M2 * P
        RP = S // 2
        a1 = [at(O1 + u * (S + 2) * 2 * M2, S + 2, 2 * M2) for u in range(2)]
        O1 += 2 * (S + 2) * 2 * M2
        a2 = [at(O1 + par * RP * C, RP, C) for par in range(2)]
        O1 += 2 * RP * C
        st = [at(O1 + u * 48, 48) for u in range(2)]
        CHAN = (slice(0, C), slice(C, P))
        FREQ = (slice(C, P), slice(0, C))
        h_zeroed, filled = sem("h_zeroed"), sem("filled")

        def sync_inverse(sp, l, first):
            if first:
                sp.sem_inc(grp_free, 1)
                for u in range(2):
                    sp.sem_inc(y_stored[u], 16)
            def load_group(g):
                sp.wait_ge(grp_free, l * NG + (g + 1))
                sp.dma_start(grp.rearrange("p c b k -> p (c b k)"),
                             spec_out[g].rearrange("r k c x -> (r k) (c x)")).then_inc(grp_loaded, 16)

            def load_pair(g, q):
                u = q % 2
                for v in range(2):
                    px = slice(v * 2048, (v + 1) * 2048)
                    sp.wait_ge(y_done, ((l * NG + g) * Q + q) * 8 + (4 * v + 4))
                    for par in range(2):
                        if first:
                            sp.dma_start(hin[u][par][C * par:C * par + 3, px],
                                         d["x_pair"][g * Q + q, 3 * par:3 * par + 3, px]).then_inc(in_loaded[u][v], 16)
                        else:
                            sp.dma_start(hin[u][par][CHAN[par], px],
                                         y_dram[g * Q + q, CHAN[par], px]).then_inc(in_loaded[u][v], 16)

            load_group(0)
            if first:
                sp.wait_ge(h_zeroed, 4)
            with sp.Fori(0, NG - 1) as g:
                for q in range(Q):
                    if q == Q - 1:
                        load_group(g + 1)
                    load_pair(g, q)
            for q in range(Q):
                load_pair(NG - 1, q)

        def gpsimd_inverse(pool, l, first):
            with pool.Fori(0, NG) as g:
                G = l * NG + g
                for q in range(Q):
                    pool.wait_ge(rows_done, (G * Q + q) * 4 + 4)
                    pool.wait_ge(grp_loaded, G * 16 + 16)
                    pool.sem_inc(waited[pool.engine], 1)
                    for par in range(2):
                        pool.tensor_copy(prs[q % 2][:, :, par * C:(par + 1) * C],
                                         grp[:, :, par * Q + q, :].rearrange("p c k -> p k c")).then_inc(pair_ready, 1)
                pool.wait_ge(pair_ready, G * (2 * Q) + 2 * Q)
                pool.sem_inc(waited[pool.engine], 1)
                pool.sem_inc(grp_free, 1)

        def tensor_inverse(pe, l, first):
            if first:
                pe.sem_inc(rows_done, 8)
                pe.sem_inc(y_done, 16)

            def rows(n, q, t):
                if t == 0:
                    pe.wait_ge(pair_ready, n * 2 + 2)
                pe.wait_ge(rows_copied, n * 5 + (t + 1))
                pe.sem_inc(waited[pe.engine], 1)
                for k in range(4):
                    for par in range(2):
                        mm = pe.matmul(bank[t % 2][CHAN[par], k * P:(k + 1) * P], prs[q % 2][:, 4 * t + k, par * C:(par + 1) * C],
                                       ga[:, par * P:(par + 1) * P], start=True, stop=True)
                mm.then_inc(rows_done, 1)

            def turn(n, q, t):
                if t == 0:
                    pe.wait_ge(rows_copied, n * 5 + 7)
                pe.wait_ge(turn_copied, n * 8 + (t + 1))
                for k in range(4):
                    mm = pe.transpose(bank[2 + t % 2][:, k * P:(k + 1) * P],
                                      a1[q % 2][:, 8 * t + 2 * k:8 * t + 2 * k + 4, :].rearrange("p h m -> p (h m)"), ident[:])
                mm.then_inc(turn_done, 1)

            def columns(n, q, t):
                if t % 4 == 0 and first:
                    pe.wait_ge(in_loaded[q % 2][t // 4], (n - q) * (32 // 2) + (q // 2 * 32 + 32))
                if t % 2 == 0 and not first:
                    pe.wait_ge(h_ready, n * 8 + (t + 2))
                pe.wait_ge(turn_copied, n * 8 + (t + 3))
                pe.wait_ge(y_copied, n * 8 + (t + 1))
                pe.sem_inc(waited[pe.engine], 1)
                for k in range(4):
                    for par in range(2):
                        j = 4 * t + k
                        mm = pe.matmul(bank[4 + t % 4][CHAN[par], k * P:(k + 1) * P], a2[par][:, j, :],
                                       hin[q % 2][par][:, j * P:(j + 1) * P], start=True, stop=True)
                mm.then_inc(y_done, 1)

            def group(G, last):
                for q in range(Q):
                    n = G * Q + q
                    for t in range(8):
                        columns(n, q, t)
                        if q < Q - 1 or not last:
                            if t < 4:
                                rows(n + 1, (q + 1) % Q, t)
                            else:
                                turn(n + 1, (q + 1) % Q, 2 * t - 8)
                                turn(n + 1, (q + 1) % Q, 2 * t - 7)

            for t in range(4):
                rows(l * (NG * Q), 0, t)
            for t in range(8):
                turn(l * (NG * Q), 0, t)
            pe.wait_ge(filled, l * 6 + 6)
            pe.sem_inc(waited[pe.engine], 1)
            with pe.Fori(0, NG - 1) as g:
                group(l * NG + g, False)
            group(l * NG + (NG - 1), True)
            pe.wait_ge(bn_step, l * BN_STEPS + 2)
            pe.wait_ge(y_copied, (l + 1) * (NP * 8) + 4)
            pe.matmul(bank[0][:, 0:1], half[:], bn[:, 0:1], start=True, stop=True).then_inc(bn_sum, 1)
            pe.wait_ge(bn_step, l * BN_STEPS + 4)
            pe.matmul(bank[1][:, 0:1], half[:], bn[:, 4:5], start=True, stop=True).then_inc(bn_sum, 1)

        BN_STEPS = 8

        def scalar_inverse(act, l, first):
            if first:
                act.sem_inc(y_copied, 4)
                act.sem_inc(h_ready, 8 * NP)

            def gelu(G, q, s):
                u, par = q % 2, s % 2
                if first:
                    return
                if s % 4 == 0:
                    act.wait_ge(in_loaded[u][s // 4], G * 64 + (q // 2 * 32 + 32))
                    act.sem_inc(waited[act.engine], 1)
                h = hin[u][par][CHAN[par], s // 2 * 1024:(s // 2 + 1) * 1024]
                act.activation(h, h, ACT.Gelu, bias=shift[CHAN[par], :], scale=scale[CHAN[par], :]).then_inc(h_ready, 1)

            def y_out(n, G, g, q, t):
                u = q % 2
                if t == 0:
                    act.wait_ge(y_stored[u], G * 32 + (q // 2 * 16 + 16))
                    act.wait_ge(y_seen, n * 8 + 8)
                act.wait_ge(y_done, n * 8 + (t + 17))
                act.activation(yout[u][:, t * BK:(t + 1) * BK], bank[4 + t % 4][:], ACT.Identity,
                               bias=pwb[:]).then_inc(y_copied, 1)
                if t == 7:
                    act.wait_ge(y_copied, n * 8 + 12)
                    act.dma_start(y_dram[g * Q + q], yout[u]).then_inc(y_stored[u], 16)

            def group(G, g, last):
                for q in range(Q):
                    n = G * Q + q
                    for t in range(8):
                        y_out(n, G, g, q, t)
                        if t < 4:
                            gelu(G, q, t + 4)
                        elif q < Q - 1:
                            gelu(G, q + 1, t - 4)
                        elif not last:
                            gelu(G + 1, 0, t - 4)

            for par in range(2):
                act.activation(a2[par][CHAN[par]], wst[CHAN[par], :].unsqueeze(1).to_broadcast([C, RP, C]),
                               ACT.Copy).then_inc(filled, 1)
            for s in range(4):
                gelu(l * NG, 0, s)
            with act.Fori(0, NG - 1) as g:
                group(l * NG + g, g, False)
            group(l * NG + (NG - 1), NG - 1, True)
            for u in range(2):
                act.wait_ge(y_stored[u], l * (NG * 32) + (NG * 32 + 16))
            act.wait_ge(bn_step, l * BN_STEPS + 5)
            act.sem_inc(waited[act.engine], 1)
            act.activation(bn[:, 6:7], bn[:, 5:6], ACT.Sqrt).then_inc(bn_root, 1)

        def vector_inverse(dve, l, first):
            if first:
                dve.sem_inc(rows_copied, 2)
                dve.sem_inc(turn_copied, 2)
                dve.sem_inc(stat_kept, 2)
                dve.sem_inc(y_seen, 16)

            def rows(n, q, t):
                dve.wait_ge(rows_done, n * 4 + (8 + t + 1))
                dve.tensor_copy(a1[q % 2][:, 0:S, 8 * t:8 * t + 8],
                                bank[t % 2][:].rearrange("p (m h) -> p h m", m=8)).then_inc(rows_copied, 1)
                if t == 3:
                    dve.wait_ge(rows_copied, n * 5 + 6)
                    dve.sem_inc(waited[dve.engine], 1)
                    dve.tensor_copy(a1[q % 2][:, S:S + 2, :], a1[q % 2][:, 0:2, :]).then_inc(rows_copied, 1)

            def turn(n, q, t):
                dve.wait_ge(turn_done, n * 8 + (t + 1))
                dve.wait_ge(y_done, n * 8 + (t + 9))
                for par in range(2):
                    c = dve.tensor_copy(a2[par][FREQ[par], 4 * t:4 * t + 4, :],
                                        bank[2 + t % 2][FREQ[par], :].rearrange("p (a b) -> p a b", a=4)[:, :, CHAN[par]])
                c.then_inc(turn_copied, 1)

            def moments(n, g, q, t):
                u = q % 2
                if t == 0:
                    dve.wait_ge(stat_kept, n + 1)
                dve.wait_ge(y_copied, n * 8 + (t + 5))
                s = dve.bn_stats(st[u][:, 6 * t:6 * t + 6], yout[u][:, t * BK:(t + 1) * BK])
                s.then_inc(y_seen, 1)
                if t == 7:
                    dve.wait_ge(y_seen, n * 8 + 24)
                    dve.tensor_scalar(stats[:, bass.ds((g * Q + q) * 48, 48)], st[u], 1.0, None,
                                      ALU.mult).then_inc(stat_kept, 1)

            def group(G, g, last):
                for q in range(Q):
                    n = G * Q + q
                    for t in range(8):
                        if q < Q - 1 or not last:
                            if t < 4:
                                rows(n + 1, (q + 1) % Q, t)
                            else:
                                turn(n + 1, (q + 1) % Q, 2 * t - 8)
                                turn(n + 1, (q + 1) % Q, 2 * t - 7)
                        moments(n, g, q, t)

            if first:
                for u in range(2):
                    for par in range(2):
                        dve.memset(hin[u][par][CHAN[par]], 0.0).then_inc(h_zeroed, 1)
            for u in range(2):
                for par in range(2):
                    dve.tensor_copy(hin[u][par][FREQ[par]].rearrange("p (a b) -> p a b", a=RP),
                                    fb2[FREQ[par], :].unsqueeze(1).to_broadcast([C, RP, P])).then_inc(filled, 1)
            for t in range(4):
                rows(l * (NG * Q), 0, t)
            for t in range(8):
                turn(l * (NG * Q), 0, t)
            with dve.Fori(0, NG - 1) as g:
                group(l * NG + g, g, False)
            group(l * NG + (NG - 1), NG - 1, True)
            base = l * BN_STEPS
            dve.wait_ge(stat_kept, (l + 1) * NP + 2)
            dve.sem_inc(waited[dve.engine], 1)
            dve.bn_aggr(bn[:, 0:2], stats[:]).then_inc(bn_step, 1)
            dve.wait_ge(bn_step, base + 1)
            dve.tensor_copy(bn[:, 2:3], bn[:, 0:1]).then_inc(bn_step, 1)
            dve.wait_ge(bn_sum, l * 2 + 1)
            dve.tensor_tensor(bn[:, 3:4], bn[:, 0:1], bank[0][:, 0:1], ALU.subtract).then_inc(bn_step, 1)
            dve.wait_ge(bn_step, base + 3)
            dve.scalar_tensor_tensor(out=bn[:, 4:5], in0=bn[:, 3:4], scalar=bn[:, 3:4], in1=bn[:, 1:2],
                                     op0=ALU.mult, op1=ALU.add).then_inc(bn_step, 1)
            dve.wait_ge(bn_sum, l * 2 + 2)
            dve.tensor_scalar(bn[:, 5:6], bank[1][:, 0:1], EPS, None, ALU.add).then_inc(bn_step, 1)
            dve.wait_ge(bn_root, l + 1)
            dve.reciprocal(bn[:, 7:8], bn[:, 6:7]).then_inc(bn_step, 1)
            dve.wait_ge(bn_step, base + 6)
            dve.tensor_tensor(scale[:], bn[:, 7:8], gamma[:], ALU.mult).then_inc(bn_step, 1)
            dve.wait_ge(bn_step, base + 7)
            dve.tensor_tensor(bn[:, 8:9], scale[:], bank[0][:, 0:1], ALU.mult).then_inc(bn_step, 1)
            dve.wait_ge(bn_step, base + 8)
            dve.tensor_tensor(shift[:], beta[:], bn[:, 8:9], ALU.subtract).then_inc(stat_taken, 1)
            dve.wait_ge(stat_taken, l + 1)
            dve.sem_inc(waited[dve.engine], 1)

        f_loaded = [sem(f"f_loaded{i}") for i in range(Q)]
        f_ready = sem("f_ready")
        ht_done, ht_copied, fc_done, fc_copied = sem("ht_done"), sem("ht_copied"), sem("fcol_done"), sem("fcol_copied")
        ft_done, ft_copied, fr_done, fr_copied = sem("ft_done"), sem("ft_copied"), sem("frow_done"), sem("frow_copied")
        spec_stored = [sem("spec_stored_a"), sem("spec_stored_b")]

        hf = [at(q * PX, PX) for q in range(Q)]
        FO = Q * PX
        HT_AT = FO + 6144 + 8192
        ht_hi = [at(HT_AT + u * BK, BK).bitcast(F16)[:, 0:BK] for u in range(4)]
        ht_lo = [at(HT_AT + u * BK, BK).bitcast(F16)[:, BK:2 * BK] for u in range(4)]
        turn_bank = (bank[0], bank[1], bank[5], bank[7])
        ht_high = sem("ht_high")
        t1 = [at(FO + 1024 + u * 2048, 2 * M2, S) for u in range(2)]
        t2 = [at(FO + 5120 + u * BK, 4, P) for u in range(2)]
        xs = [at(FO + 6144 + u * 4096, 2, NCH, 2, MC) for u in range(2)]

        def sync_forward(sp, lf):
            with sp.Fori(0, NG) as g:
                F = lf * NG + g
                for q in range(Q):
                    sp.wait_ge(ht_done, (F * Q + q) * 8 + 8)
                    sp.dma_start(hf[q], y_dram[g * Q + q]).then_inc(f_loaded[q], 16)

        def tensor_forward(pe, lf):
            def turn(n, q, t):
                pe.wait_ge(f_ready, n * 8 + (t + 1))
                pe.wait_ge(ht_copied, n * 8 + (t + 1))
                for k in range(4):
                    mm = pe.transpose(turn_bank[t % 4][:, k * P:(k + 1) * P], hf[q][:, (4 * t + k) * P:(4 * t + k + 1) * P], ident[:])
                mm.then_inc(ht_done, 1)

            def columns(n, t):
                pe.wait_ge(ht_copied, n * 8 + (t + 5))
                if t % 2 == 0:
                    pe.wait_ge(fc_copied, n * 4 + (t // 2 + 1))
                b = bank[2 + t // 2 % 2]
                for k in range(4):
                    o = b[:, (t % 2) * 256 + k * 64:(t % 2) * 256 + (k + 1) * 64]
                    for i, h in enumerate((ht_hi, ht_lo)):
                        for j in range(2):
                            mm = pe.matmul(o, h[t % 4][:, k * P:(k + 1) * P], fw_half[j], start=(i + j == 0), stop=(i + j == 2))
                mm.then_inc(fc_done, 1)

            def turn_rows(n, q, t):
                if t == 0:
                    pe.wait_ge(fc_copied, n * 4 + 6)
                pe.wait_ge(ft_copied, n * 4 + (t + 1))
                for k in range(4):
                    mm = pe.transpose(bank[4][:, k * P:(k + 1) * P],
                                      t1[q % 2][:, 8 * t + 2 * k:8 * t + 2 * k + 2, :].rearrange("p m h -> p (m h)"), ident[:])
                mm.then_inc(ft_done, 1)

            def rows(n, t):
                pe.wait_ge(ft_copied, n * 4 + (t + 2))
                if t % 2 == 0:
                    pe.wait_ge(fr_copied, n * 2 + (t // 2 + 1))
                for k in range(4):
                    mm = pe.matmul(bank[6][:, (t % 2) * 256 + k * 64:(t % 2) * 256 + (k + 1) * 64], t2[t % 2][:, k, :],
                                   gh[:], start=True, stop=True)
                mm.then_inc(fr_done, 1)

            def group(F, first):
                for q in range(Q):
                    n = F * Q + q
                    before = q > 0 or not first
                    for t in range(8):
                        turn(n, q, t)
                        if t > 1:
                            columns(n, t - 2)
                        elif before:
                            columns(n - 1, 6 + t)
                        if before and 3 <= t < 7:
                            turn_rows(n - 1, (q - 1) % Q, t - 3)
                        if before and 4 <= t < 8:
                            rows(n - 1, t - 4)

            group(lf * NG, True)
            with pe.Fori(1, NG) as g:
                group(lf * NG + g, False)
            n = lf * NP + (NP - 1)
            columns(n, 6)
            columns(n, 7)
            for t in range(5):
                if t < 4:
                    turn_rows(n, Q - 1, t)
                if t > 0:
                    rows(n, t - 1)

        def scalar_forward(act, lf):
            def gelu(F, q, v):
                if v == 0:
                    act.wait_ge(f_loaded[q], F * 16 + 16)
                    act.sem_inc(waited[act.engine], 1)
                x = hf[q][:, v * BK:(v + 1) * BK]
                act.activation(x, x, ACT.Gelu, bias=shift[:], scale=scale[:]).then_inc(f_ready, 1)

            def ht_cast(n, t):
                act.wait_ge(ht_done, n * 8 + (8 * Q + t + 1))
                act.activation(ht_hi[t % 4], turn_bank[t % 4][:], ACT.Copy).then_inc(ht_high, 1)

            def t2_copy(n, t):
                act.wait_ge(ft_done, n * 4 + (t + 1))
                act.activation(t2[t % 2].rearrange("p a b -> p (a b)"), bank[4][:], ACT.Copy).then_inc(ft_copied, 1)

            def store(n_last, b0, v):
                act.wait_ge(fr_copied, n_last * 2 + 3)
                for ri in range(2):
                    for par in range(2):
                        act.dma_start(spec_in[ri, :, :, bass.ds(b0 + (par * Q + 2 * v), 2), :],
                                      xs[v][par * C:(par + 1) * C, ri]).then_inc(spec_stored[v], 16)

            def group(F, g, first, last):
                for q in range(Q):
                    n = F * Q + q
                    for t in range(8):
                        ht_cast(n, t)
                        if (q > 0 or not first) and 3 <= t < 7:
                            t2_copy(n - 1, t - 3)
                        if q < Q - 1:
                            gelu(F, q + 1, t)
                        elif not last:
                            gelu(F + 1, 0, t)
                    if q == 3:
                        store(n - 2, g * GI, 0)
                    if q == 1 and not first:
                        store(n - 2, g * GI - GI, 1)

            for v in range(8):
                gelu(lf * NG, 0, v)
            group(lf * NG, 0, True, False)
            if NG > 2:
                with act.Fori(1, NG - 1) as g:
                    group(lf * NG + g, g, False, False)
            group(lf * NG + (NG - 1), NG - 1, False, True)
            n = lf * NP + (NP - 1)
            for t in range(4):
                t2_copy(n, t)
            store(n, (NG - 1) * GI, 1)
            for v in range(2):
                act.wait_ge(spec_stored[v], lf * (NG * 64) + (NG * 64 + 64))
            act.sem_inc(waited[act.engine], 1)

        def vector_forward(dve, lf):
            def ht_copy(n, t):
                dve.wait_ge(ht_high, n * 8 + (t + 1))
                dve.tensor_tensor(ht_lo[t % 4], turn_bank[t % 4][:], ht_hi[t % 4], ALU.subtract).then_inc(ht_copied, 1)

            def column_copy(n, q, t):
                dve.wait_ge(fc_done, n * 8 + (2 * t + 2))
                dve.tensor_copy(t1[q % 2][:, :, 16 * t:16 * t + 16],
                                bank[2 + t % 2][:].rearrange("p (h m) -> p m h", h=16)).then_inc(fc_copied, 1)

            def row_copy(n, q, t):
                v = q // 2
                if q % 2 == 0 and t == 0:
                    dve.wait_ge(spec_stored[v], (n - q) * (64 // Q) + 64)
                dve.wait_ge(fr_done, n * 4 + (2 * t + 2))
                for ri in range(2):
                    o = xs[v][:, ri, :, q % 2, :].rearrange("p h (k m) -> p h k m", k=CH)[:, :, :, 8 * t:8 * t + 8]
                    cp = dve.tensor_copy(o, bank[6][:].rearrange("p (m r h k) -> p r h k m", m=8, r=2, h=NCH)[:, ri])
                cp.then_inc(fr_copied, 1)

            def group(F, first):
                for q in range(Q):
                    n = F * Q + q
                    before = q > 0 or not first
                    for t in range(8):
                        ht_copy(n, t)
                        if t == 1 and before:
                            column_copy(n - 1, (q - 1) % Q, 3)
                        if t % 2 == 1 and t > 1:
                            column_copy(n, q, (t - 3) // 2)
                        if before and t in (5, 7):
                            row_copy(n - 1, (q - 1) % Q, (t - 5) // 2)

            group(lf * NG, True)
            with dve.Fori(1, NG) as g:
                group(lf * NG + g, False)
            n = lf * NP + (NP - 1)
            column_copy(n, Q - 1, 3)
            for t in range(2):
                row_copy(n, Q - 1, t)

        e_loaded = [sem(f"e_loaded{i}") for i in range(Q)]
        e_ready, fc1_done, fc1_gelu, g_split, fc2_used = (
            sem("e_ready"), sem("fc1_done"), sem("fc1_gelu"), sem("g_split"), sem("fc2_used"))
        fc2_ready, fc2_copied, fc2_summed, tok_ready, tok_stored, tok_free = (
            sem("fc2_ready"), sem("fc2_copied"), sem("fc2_summed"), sem("tok_ready"), sem("tok_stored"), sem("tok_free"))
        g_high = sem("g_high")
        NB_G = 4
        NB_S = 6
        HO = FO
        gb = [at(HO + u * BK, BK) for u in range(NB_G)]
        HO += NB_G * BK
        g_hi = [at(HO + u * BK, BK).bitcast(F16)[:, 0:BK] for u in range(NB_S)]
        g_lo = [at(HO + u * BK, BK).bitcast(F16)[:, BK:2 * BK] for u in range(NB_S)]
        HO += NB_S * BK
        RG = GI * 8
        win = [at(HO + u * 96, 96).bitcast(F16) for u in range(2)]
        HO += 192
        w_hi, w_lo = at(HO, 1).bitcast(F16)[:, 0:1], at(HO + 1, 1).bitcast(F16)[:, 0:1]
        w_rest = at(HO + 2, 1)
        fold = at(HO + 4, C)
        HO += 4 + C
        fsum = at(HO, BK)
        tokb = at(HO + BK, BK, parts=RG)
        TB = 16
        LAG = 4
        FIRSTS = Q * TB

        def sync_head(sp):
            with sp.Fori(0, NG) as g:
                for q in range(Q):
                    sp.wait_ge(fc1_done, (g * Q + q) * TB + TB)
                    sp.dma_start(hf[q], y_dram[g * Q + q]).then_inc(e_loaded[q], 16)

        def chunk(i):
            q, t = i // TB, i % TB
            return q, t, ((t // 8) * Q + q) * 8 + t % 8

        def tensor_head(pe):
            pe.sem_inc(fc1_done, TB * Q)
            pe.sem_inc(fc2_used, NB_S)
            pe.wait_ge(fc2_ready, 6)

            def first(g, i):
                q, t, _ = chunk(i)
                par, tt = t // 8, t % 8
                if t == 0:
                    pe.wait_ge(e_ready, (g * Q + q) * 2 + 2)
                pe.wait_ge(fc1_gelu, g * FIRSTS + (i + 1))
                pe.matmul(bank[i % 4][:], fc1[par * C:(par + 1) * C, :], hf[q][par * C:(par + 1) * C, tt * BK:(tt + 1) * BK],
                          start=True, stop=True).then_inc(fc1_done, 1)

            def second(g, i):
                _, _, r = chunk(i)
                pe.wait_ge(g_split, g * FIRSTS + (i + 1 + NB_G))
                w = win[(r + 1) % 2]
                a = RG - 1 - r + (r + 1) % 2
                pe.matmul(bank[6][:], w[:, a:a + P], g_hi[i % NB_S], start=(i == 0), stop=False)
                pe.matmul(bank[6][:], w[:, a:a + P], g_lo[i % NB_S], start=False, stop=(i == FIRSTS - 1)).then_inc(fc2_used, 1)

            with pe.Fori(0, NG) as g:
                for i in range(FIRSTS + LAG):
                    if i < FIRSTS:
                        first(g, i)
                    if i >= LAG:
                        if i == LAG:
                            pe.wait_ge(fc2_copied, g + 1)
                        second(g, i - LAG)
                pe.wait_ge(fc2_copied, g + 2)
                pe.wait_ge(tok_ready, g + 1)
                pe.matmul(bank[7][0:RG, :], fold, fsum, start=True, stop=True).then_inc(fc2_summed, 1)

        def scalar_head(act):
            act.sem_inc(fc1_gelu, 4)

            def gelu(G, q, v):
                if v == 0:
                    act.wait_ge(e_loaded[q], G * 16 + 16)
                    act.sem_inc(waited[act.engine], 1)
                x = hf[q][:, v * 2048:(v + 1) * 2048]
                act.activation(x, x, ACT.Gelu, bias=shift[:], scale=scale[:]).then_inc(e_ready, 1)

            def hidden(g, i):
                act.wait_ge(fc1_done, g * FIRSTS + (i + TB * Q + 1))
                act.wait_ge(g_split, g * FIRSTS + (i + 1))
                act.activation(gb[i % NB_G], bank[i % 4][:], ACT.Gelu, bias=fc1b[:]).then_inc(fc1_gelu, 1)

            def group(g, last):
                for i in range(FIRSTS):
                    hidden(g, i)
                    q, t = i // TB, i % TB
                    if t in (4, 10) and (q < Q - 1 or not last):
                        v = (t - 4) // 6
                        if q < Q - 1:
                            gelu(g, q + 1, v)
                        else:
                            gelu(g + 1, 0, v)

            for v in range(2):
                gelu(0, 0, v)
            with act.Fori(0, NG - 1) as g:
                group(g, False)
            group(NG - 1, True)

        def vector_head(dve):
            dve.sem_inc(g_split, NB_G)
            dve.sem_inc(fc2_copied, 1)
            dve.sem_inc(tok_ready, 1)
            for u in range(2):
                dve.memset(win[u], 0.0).then_inc(fc2_ready, 1)
            dve.tensor_copy(w_hi, fc2[:]).then_inc(fc2_ready, 1)
            dve.wait_ge(fc2_ready, 3)
            dve.tensor_tensor(w_rest, fc2[:], w_hi, ALU.subtract).then_inc(fc2_ready, 1)
            dve.wait_ge(fc2_ready, 4)
            dve.tensor_copy(w_lo, w_rest).then_inc(fc2_ready, 1)
            dve.wait_ge(fc2_ready, 5)
            dve.tensor_tensor(fold, ident[:, 0:C], ident[:, C:P], ALU.add)
            for u in range(2):
                dve.tensor_copy(win[u][:, RG - 1 + u:RG + u], w_hi)
                c = dve.tensor_copy(win[u][:, 2 * RG - 1 + u:2 * RG + u], w_lo)
            c.then_inc(fc2_ready, 1)
            with dve.Fori(0, NG) as g:
                for i in range(FIRSTS):
                    dve.wait_ge(fc1_gelu, g * FIRSTS + (i + 5))
                    dve.wait_ge(fc2_used, g * FIRSTS + (i + 1))
                    dve.tensor_copy(g_hi[i % NB_S], gb[i % NB_G]).then_inc(g_high, 1)
                    dve.wait_ge(g_high, g * FIRSTS + (i + 1))
                    dve.tensor_tensor(g_lo[i % NB_S], gb[i % NB_G], g_hi[i % NB_S], ALU.subtract).then_inc(g_split, 1)
                dve.wait_ge(fc2_used, g * FIRSTS + (FIRSTS + NB_S))
                dve.tensor_copy(fsum, bank[6][:]).then_inc(fc2_copied, 1)
                dve.wait_ge(fc2_summed, g + 1)
                dve.wait_ge(tok_free, g + 1)
                dve.tensor_scalar(tokb, bank[7][0:RG, :], fc2b[0:RG], None, ALU.add).then_inc(tok_ready, 1)

        def gpsimd_head(pool, tok):
            pool.sem_inc(tok_free, 1)
            with pool.Fori(0, NG) as g:
                pool.wait_ge(tok_ready, g + 2)
                pool.dma_start(tok[bass.ds(g * RG, RG), :], tokb).then_inc(tok_stored, 16)
                pool.wait_ge(tok_stored, g * 16 + 16)
                pool.sem_inc(tok_free, 1)
            pool.wait_ge(tok_stored, NG * 16)

        tok = nc.dram_tensor("tok", [B * S, S], F32, kind="Internal").ap().rearrange("(a r) x -> a (r x)", r=GI)

        NT = B * S // P
        TG = NT // 4
        HD, HEADS, MEM = 32, 4, 4
        HID = HEADS * HD
        E0, E1 = 8, 16

        h_tok = at(0, NT, C)
        x_tok = at(NT * C, NT, C)
        o_tok = at(2 * NT * C, NT, C)
        sq = at(3 * NT * C, NT, C)
        TO = 4 * NT * C
        red = at(TO, 8, NT); TO += 8 * NT
        wqkv = at(TO, 3 * HID, parts=C); TO += 3 * HID
        w_out = at(TO, C); TO += C
        gpre_b = at(TO, C); TO += C
        gout_b = at(TO, C); TO += C
        bout_b = at(TO, C); TO += C
        memk = at(TO, MEM); TO += MEM
        memk_max = at(TO, 4); TO += 4
        headmask = at(TO, HID); TO += HID
        wg = [at(TO, E0, parts=C), at(TO + E0, E1, parts=C)]; TO += E0 + E1
        bg_b = [at(TO, E0), at(TO + E0, E1)]; TO += E0 + E1
        w1 = [at(TO, E0 * 2, P, parts=C + 1), at(TO + E0 * 2 * P, E1, P, parts=C + 1)]; TO += 2 * E0 * 2 * P
        w2 = [at(TO, 16, C), at(TO + 16 * C, 16, C)]; TO += 32 * C
        b2 = [at(TO, C, parts=E0), at(TO + C, C, parts=E1)]; TO += 2 * C
        wqT, wkT, wvT, woT = (at(TO + i * C, C, parts=C) for i in range(4)); TO += 4 * C
        wqk0 = at(TO, 2, parts=C); TO += 2
        bqk0_b = at(TO, 2); TO += 2
        bq_c, bk_c = at(TO, 1, parts=C), at(TO + 1, 1, parts=C); TO += 2
        bv_b, bo_b, gamma_b, beta_b = (at(TO + i * C, C) for i in range(4)); TO += 4 * C
        rank = at(TO, E1); TO += E1
        xgs = [at(TO + u * 4 * C, 4, C) for u in range(2)]; TO += 8 * C
        xTs = [at(TO + u * BK, BK, parts=C) for u in range(2)]; TO += 2 * BK
        xg, xT = xgs[0], xTs[0]
        work = TO

        tok_loaded, ln_step, rms_step = sem("tok_loaded"), sem("ln_step"), sem("rms_step")
        attn_step = [sem("attn_step_even"), sem("attn_step_odd")]
        self_step = [sem("self_step_even"), sem("self_step_odd")]
        gate_step, top_step, attn_end = sem("gate_step"), sem("top_step"), sem("attn_end")

        def steps(*names):
            return {n: i + 2 for i, n in enumerate(names)}, len(names)

        def over_c(v):
            return v.unsqueeze(2).to_broadcast([P, NT, C])

        def row4(v, n=4, w=C):
            return v.unsqueeze(1).to_broadcast([v.shape[0], n, w])

        def sync_load_tokens(sp):
            load = lambda dst, src: sp.dma_start(dst, src).then_inc(tok_loaded, 16)
            row = lambda name: d[name].rearrange("(a c) -> a c", a=1)
            load(h_tok, tok.rearrange("a (r x) -> (a r) x", r=GI).rearrange("(t p) c -> p t c", p=P))
            load(wqkv, d["w_qkv"])
            load(w_out, d["w_out"])
            load(gpre_b, row("g_pre").to_broadcast([P, C]))
            load(gout_b, row("g_out").to_broadcast([P, C]))
            load(bout_b, row("b_out").to_broadcast([P, C]))
            load(memk, d["mem_k"])
            for u in range(4):
                load(vmem[u // 2][u % 2], d["mem_v"].unsqueeze(1).to_broadcast([MEM, GI // 2, HID]))
            load(headmask, d["c_headmask"])
            load(rank, d["c_rank"].to_broadcast([P, E1]))
            for m in range(2):
                load(wg[m], d[f"wg{m}"])
                load(bg_b[m], row(f"bg{m}").to_broadcast([P, (E0, E1)[m]]))
                load(w1[m][0:C], d[f"w1_{m}"])
                load(w1[m][C:C + 1].rearrange("p i h -> p (i h)"), row(f"b1_{m}"))
                load(w2[m], d[f"w2_{m}"])
                load(b2[m], d[f"b2_{m}"])
            for dst, name in ((wqT, "wq_t"), (wkT, "wk_t"), (wvT, "wv_t"), (woT, "wo_t")):
                load(dst, d[name])
            load(wqk0, d["wqk0"])
            load(bqk0_b, row("bqk0").to_broadcast([P, 2]))
            load(bq_c, d["bq"].rearrange("(c a) -> c a", a=1))
            load(bk_c, d["bk"].rearrange("(c a) -> c a", a=1))
            for dst, name in ((bv_b, "bv"), (bo_b, "bo"), (gamma_b, "ln_gamma"), (beta_b, "ln_beta")):
                load(dst, row(name).to_broadcast([P, C]))

        N_TOK = 16 * (7 + 4 + 2 + 12 + 4 + 2 + 2 + 4)

        LN, NLN = steps("sum", "mean", "centre", "square", "sumsq", "var", "root", "inverse", "scale")

        def vector_norm(dve, k, src, dst):
            base = k * NLN
            dve.tensor_reduce(red[:, 0, :], src, AX.X, ALU.add).then_inc(ln_step, 1)
            dve.wait_ge(ln_step, base + LN["sum"])
            dve.tensor_scalar(red[:, 1, :], red[:, 0, :], -1.0 / C, None, ALU.mult).then_inc(ln_step, 1)
            dve.wait_ge(ln_step, base + LN["mean"])
            dve.tensor_tensor(dst, src, over_c(red[:, 1, :]), ALU.add).then_inc(ln_step, 1)
            dve.wait_ge(ln_step, base + LN["centre"])
            dve.tensor_tensor(sq, dst, dst, ALU.mult).then_inc(ln_step, 1)
            dve.wait_ge(ln_step, base + LN["square"])
            dve.tensor_reduce(red[:, 2, :], sq, AX.X, ALU.add).then_inc(ln_step, 1)
            dve.wait_ge(ln_step, base + LN["sumsq"])
            dve.tensor_scalar(red[:, 3, :], red[:, 2, :], 1.0 / C, EPS, ALU.mult, ALU.add).then_inc(ln_step, 1)
            dve.wait_ge(ln_step, base + LN["root"])
            dve.reciprocal(red[:, 5, :], red[:, 4, :]).then_inc(ln_step, 1)
            dve.wait_ge(ln_step, base + LN["inverse"])
            dve.tensor_tensor(dst, dst, over_c(red[:, 5, :]), ALU.mult).then_inc(ln_step, 1)
            dve.wait_ge(ln_step, base + LN["scale"])

        def scalar_norm(act, k):
            act.wait_ge(ln_step, k * NLN + LN["var"])
            act.activation(red[:, 4, :], red[:, 3, :], ACT.Sqrt).then_inc(ln_step, 1)

        RMS, NRMS = steps("square", "sumsq", "root", "floor", "inverse", "scale")

        def vector_rms(dve, k, src):
            base = k * NRMS
            dve.tensor_tensor(sq, src, src, ALU.mult).then_inc(rms_step, 1)
            dve.wait_ge(rms_step, base + RMS["square"])
            dve.tensor_reduce(red[:, 2, :], sq, AX.X, ALU.add).then_inc(rms_step, 1)
            dve.wait_ge(rms_step, base + RMS["root"])
            dve.tensor_scalar(red[:, 5, :], red[:, 4, :], 1e-12, None, ALU.max).then_inc(rms_step, 1)
            dve.wait_ge(rms_step, base + RMS["floor"])
            dve.reciprocal(red[:, 6, :], red[:, 5, :]).then_inc(rms_step, 1)
            dve.wait_ge(rms_step, base + RMS["inverse"])
            dve.tensor_scalar(red[:, 7, :], red[:, 6, :], float(C) ** 0.5, None, ALU.mult).then_inc(rms_step, 1)
            dve.wait_ge(rms_step, base + RMS["scale"])

        def scalar_rms(act, k):
            act.wait_ge(rms_step, k * NRMS + RMS["sumsq"])
            act.activation(red[:, 4, :], red[:, 2, :], ACT.Sqrt).then_inc(rms_step, 1)

        A, NA = steps("xr", "xn", "turn", "xT", "proj", "k_max", "k_top", "k_sub", "k_exp", "k_sum", "k_inv", "kT", "kT_copy",
                      "ctx", "ctx_scale", "ctx_mask", "q_max", "q_sub", "q_exp", "q_sum", "q_inv", "q_scale", "q_norm",
                      "qT", "qT_copy", "att", "att_copy", "out", "out_bias")
        lane_bank = (bank[0:4], bank[4:8])
        next_free = [work]

        def lanes(*shape, parts=P):
            n, start = int(np.prod(shape)), next_free[0]
            next_free[0] += 2 * n
            return [at(start + u * n, *shape, parts=parts) for u in range(2)]

        vkv = [lanes(4, HID) for u in range(2)]
        vmem = [[v[C:C + MEM] for v in lane] for lane in vkv]
        ke = lanes(GI, C + MEM)
        kst = lanes(4, GI)
        kTs = lanes(GI, HID, parts=C + MEM)
        ctx_s = lanes(GI, HID)
        qs = lanes(4, HID)
        qst = lanes(4, 16)
        qT = lanes(BK)
        attT = lanes(BK)
        SCALE = HD ** -0.5

        def tensor_attention(pe):
            with pe.Fori(0, TG // 2) as r:
                def at_(u, s):
                    pe.wait_ge(attn_step[u], r * NA + A[s])
                    pe.sem_inc(waited[pe.engine], 1)

                for u in range(2):
                    at_(u, "xn")
                    for t in range(4):
                        mm = pe.transpose(lane_bank[u][0][0:C, t * P:(t + 1) * P], xgs[u][:, t, :], ident[:])
                    mm.then_inc(attn_step[u], 1)
                for u in range(2):
                    at_(u, "xT")
                    pe.matmul(lane_bank[u][1][:], wqkv[:, HID:2 * HID], xTs[u], start=True, stop=True)
                    for t in range(4):
                        pe.matmul(lane_bank[u][2][:, t * P:(t + 1) * P], xTs[u][:, t * P:(t + 1) * P], wqkv[:, 0:HID], start=True, stop=True)
                    for b in range(GI):
                        mm = pe.matmul(lane_bank[u][3 * (b // 4)][0:C, b % 4 * HID:(b % 4 + 1) * HID], xTs[u][:, b * S:(b + 1) * S],
                                       wqkv[:, 2 * HID:3 * HID], start=True, stop=True)
                    mm.then_inc(attn_step[u], 1)
                for u in range(2):
                    at_(u, "k_inv")
                    for b in range(GI):
                        mm = pe.transpose(lane_bank[u][3 * (b // 4)][0:C + MEM, b % 4 * HID:(b % 4 + 1) * HID], ke[u][:, b, :], ident[:])
                    mm.then_inc(attn_step[u], 1)
                for u in range(2):
                    at_(u, "kT_copy")
                    for b in range(GI):
                        mm = pe.matmul(lane_bank[u][3 * (b // 4)][:, b % 4 * HID:(b % 4 + 1) * HID], kTs[u][:, b, :], vkv[u][b // 4][0:C + MEM, b % 4, :],
                                       start=True, stop=True)
                    mm.then_inc(attn_step[u], 1)
                for u in range(2):
                    at_(u, "q_norm")
                    for t in range(4):
                        mm = pe.transpose(lane_bank[u][1][:, t * P:(t + 1) * P], qs[u][:, t, :], ident[:])
                    mm.then_inc(attn_step[u], 1)
                for u in range(2):
                    at_(u, "qT_copy")
                    for b in range(GI):
                        mm = pe.matmul(lane_bank[u][2][:, b * S:(b + 1) * S], ctx_s[u][:, b, :], qT[u][:, b * S:(b + 1) * S], start=True, stop=True)
                    mm.then_inc(attn_step[u], 1)
                for u in range(2):
                    at_(u, "att_copy")
                    for t in range(4):
                        mm = pe.matmul(lane_bank[u][0][:, t * C:(t + 1) * C], attT[u][:, t * P:(t + 1) * P], w_out, start=True, stop=True)
                    mm.then_inc(attn_step[u], 1)

        def scalar_attention(act):
            with act.Fori(0, TG // 2) as r:
                at_ = lambda u, s: act.wait_ge(attn_step[u], r * NA + A[s])
                for u in range(2):
                    at_(u, "turn")
                    act.activation(xTs[u], lane_bank[u][0][0:C, :], ACT.Copy).then_inc(attn_step[u], 1)
                for u in range(2):
                    at_(u, "k_sub")
                    act.activation(ke[u], ke[u], ACT.Exp).then_inc(attn_step[u], 1)
                for u in range(2):
                    at_(u, "kT")
                    for i in range(2):
                        c = act.activation(kTs[u][:, 4 * i:4 * i + 4, :], lane_bank[u][3 * i][0:C + MEM, :].rearrange("p (b x) -> p b x", b=4), ACT.Copy)
                    c.then_inc(attn_step[u], 1)
                for u in range(2):
                    at_(u, "q_sub")
                    act.activation(qs[u], qs[u], ACT.Exp).then_inc(attn_step[u], 1)
                for u in range(2):
                    at_(u, "qT")
                    act.activation(qT[u], lane_bank[u][1][:], ACT.Copy).then_inc(attn_step[u], 1)
                for u in range(2):
                    at_(u, "att")
                    act.activation(attT[u], lane_bank[u][2][:], ACT.Copy).then_inc(attn_step[u], 1)

        def vector_attention(dve):
            dve.wait_ge(tok_loaded, N_TOK)
            dve.tensor_reduce(memk_max[:, 0:1], memk, AX.X, ALU.max).then_inc(attn_step[0], 1)
            dve.wait_ge(attn_step[0], 1)
            dve.sem_inc(attn_step[1], 1)
            vector_norm(dve, 0, h_tok, x_tok)
            vector_rms(dve, 0, x_tok)
            with dve.Fori(0, TG // 2) as r:
                at_ = lambda u, s: dve.wait_ge(attn_step[u], r * NA + A[s])
                then = lambda u, ins: ins.then_inc(attn_step[u], 1)
                k_of = lambda u: lane_bank[u][1][:].rearrange("p (b n) -> p b n", b=GI)
                q_of = lambda u: lane_bank[u][2][:].rearrange("p (a e) -> p a e", e=HD)
                qs_of = lambda u: qs[u].rearrange("p t (a e) -> p (t a) e", e=HD)

                for u in range(2):
                    dve.wait_ge(attn_step[u], r * NA + 1)
                    then(u, dve.tensor_tensor(xgs[u], x_tok[:, bass.ds(r * 8 + 4 * u, 4), :],
                                           red[:, 7, bass.ds(r * 8 + 4 * u, 4)].unsqueeze(2).to_broadcast([P, 4, C]), ALU.mult))
                for u in range(2):
                    at_(u, "xr")
                    then(u, dve.tensor_tensor(xgs[u], xgs[u], row4(gpre_b), ALU.mult))
                for u in range(2):
                    at_(u, "proj")
                    for i in range(2):
                        dve.tensor_copy(vkv[u][i][0:C], lane_bank[u][3 * i][0:C, :].rearrange("p (b x) -> p b x", b=4))
                    then(u, dve.tensor_reduce(kst[u][:, 0, :], k_of(u), AX.X, ALU.max))
                for u in range(2):
                    at_(u, "k_max")
                    then(u, dve.tensor_scalar(kst[u][:, 1, :], kst[u][:, 0, :], memk_max[:, 0:1], None, ALU.max))
                for u in range(2):
                    at_(u, "k_top")
                    dve.tensor_tensor(ke[u][:, :, C:C + MEM], memk.unsqueeze(1).to_broadcast([P, GI, MEM]),
                                      kst[u][:, 1, :].unsqueeze(2).to_broadcast([P, GI, MEM]), ALU.subtract)
                    then(u, dve.tensor_tensor(ke[u][:, :, 0:C], k_of(u), kst[u][:, 1, :].unsqueeze(2).to_broadcast([P, GI, C]), ALU.subtract))
                for u in range(2):
                    at_(u, "k_exp")
                    then(u, dve.tensor_reduce(kst[u][:, 2, :], ke[u], AX.X, ALU.add))
                for u in range(2):
                    at_(u, "k_sum")
                    then(u, dve.reciprocal(kst[u][:, 3, :], kst[u][:, 2, :]))
                for u in range(2):
                    at_(u, "ctx")
                    for i in range(2):
                        c = dve.tensor_tensor(ctx_s[u][:, 4 * i:4 * i + 4, :], lane_bank[u][3 * i][:].rearrange("p (b x) -> p b x", b=4),
                                              kst[u][:, 3, 4 * i:4 * i + 4].unsqueeze(2).to_broadcast([P, 4, HID]), ALU.mult)
                    then(u, c)
                for u in range(2):
                    at_(u, "ctx_scale")
                    then(u, dve.tensor_tensor(ctx_s[u], ctx_s[u], row4(headmask, GI, HID), ALU.mult))
                for u in range(2):
                    at_(u, "ctx_mask")
                    then(u, dve.tensor_reduce(qst[u][:, 0, :], q_of(u), AX.X, ALU.max))
                for u in range(2):
                    at_(u, "q_max")
                    then(u, dve.tensor_tensor(qs_of(u), q_of(u), qst[u][:, 0, :].unsqueeze(2).to_broadcast([P, 16, HD]), ALU.subtract))
                for u in range(2):
                    at_(u, "q_exp")
                    then(u, dve.tensor_reduce(qst[u][:, 1, :], qs_of(u), AX.X, ALU.add))
                for u in range(2):
                    at_(u, "q_sum")
                    then(u, dve.reciprocal(qst[u][:, 2, :], qst[u][:, 1, :]))
                for u in range(2):
                    at_(u, "q_inv")
                    then(u, dve.tensor_scalar(qst[u][:, 3, :], qst[u][:, 2, :], SCALE, None, ALU.mult))
                for u in range(2):
                    at_(u, "q_scale")
                    then(u, dve.tensor_tensor(qs_of(u), qs_of(u), qst[u][:, 3, :].unsqueeze(2).to_broadcast([P, 16, HD]), ALU.mult))
                for u in range(2):
                    at_(u, "out")
                    then(u, dve.tensor_tensor(o_tok[:, bass.ds(r * 8 + 4 * u, 4), :], lane_bank[u][0][:, 0:4 * C].rearrange("p (t c) -> p t c", t=4),
                                           row4(bout_b), ALU.add))
            for u in range(2):
                dve.wait_ge(attn_step[u], TG // 2 * NA + 1)
            vector_rms(dve, 1, o_tok)
            for i, (a, b) in enumerate(((o_tok, over_c(red[:, 7, :])), (o_tok, row4(gout_b, NT)))):
                dve.tensor_tensor(a, a, b, ALU.mult).then_inc(attn_end, 1)
                dve.wait_ge(attn_end, i + 1)
            dve.tensor_tensor(o_tok, o_tok, x_tok, ALU.add).then_inc(attn_end, 1)
            dve.wait_ge(attn_end, 3)
            dve.tensor_tensor(h_tok, h_tok, o_tok, ALU.add).then_inc(attn_end, 1)
            dve.wait_ge(attn_end, 4)

        ME = (E0, E1)
        HT = (2, 1)
        G, NGS = steps("xg", "turn", "xT", "gate", "score")
        T_, NTS = steps("m1", "eq1", "rk1", "top1", "oh1", "keep", "rest", "low", "m2", "eq2", "rk2", "top2", "oh2",
                        "diff", "p", "p1", "r1", "r2", "c1", "c2", "comb")
        W = work
        score, s2, oh1, oh2, tw = (at(W + i * NT * E1, NT, E1) for i in range(5)); W += 5 * NT * E1
        comb = at(W, NT, E1); W += NT * E1
        tp = at(W, 8, NT); W += 8 * NT
        hid = [at(W + i * BK, BK) for i in range(4)]; W += 4 * BK
        x_st = [at(W + i * 4 * (C + 1), 4, C + 1) for i in range(2)]; W += 8 * (C + 1)
        x_sc = [at(W + i * 4 * (C + 1), 4, C + 1) for i in range(2)]; W += 8 * (C + 1)
        xeT = [at(W + i * BK, BK, parts=C + 1) for i in range(2)]; W += 2 * BK
        c_st = [at(W + i * 4 * E1, 4, E1) for i in range(2)]; W += 8 * E1
        combT = at(W, BK, parts=E1); W += BK
        yT = at(W, BK, parts=C); W += BK
        ones_set, staged, x_scaled, x_turned, x_copied = (
            sem("ones_set"), sem("staged"), sem("x_scaled"), sem("x_turned"), sem("x_copied"))
        hid_done, ex_used, relu_done = sem("hid_done"), sem("ex_used"), [sem("relu_by_act"), sem("relu_by_dve")]
        c_turned, c_copied = sem("c_turned"), sem("c_copied")
        y_sum, ysum_copied, ysum_turned, ysum_taken = sem("y_sum"), sem("ysum_copied"), sem("ysum_turned"), sem("ysum_taken")

        def tensor_gate(pe, m):
            with pe.Fori(0, TG) as g:
                def at_(s):
                    pe.wait_ge(gate_step, (m * TG + g) * NGS + G[s])
                    pe.sem_inc(waited[pe.engine], 1)

                at_("xg")
                for t in range(4):
                    mm = pe.transpose(bank[0][0:C, t * P:(t + 1) * P], xg[:, t, :], ident[:])
                mm.then_inc(gate_step, 1)
                at_("xT")
                for t in range(4):
                    mm = pe.matmul(bank[1][:, t * ME[m]:(t + 1) * ME[m]], xT[:, t * P:(t + 1) * P], wg[m], start=True, stop=True)
                mm.then_inc(gate_step, 1)

        def scalar_gate(act, m):
            with act.Fori(0, TG) as g:
                act.wait_ge(gate_step, (m * TG + g) * NGS + G["turn"])
                act.activation(xT, bank[0][0:C, :], ACT.Copy).then_inc(gate_step, 1)

        def vector_gate(dve, m):
            with dve.Fori(0, TG) as g:
                base = (m * TG + g) * NGS
                dve.wait_ge(gate_step, base + 1)
                dve.tensor_scalar(xg, x_tok[:, bass.ds(g * 4, 4), :], 1.0, None, ALU.mult).then_inc(gate_step, 1)
                dve.wait_ge(gate_step, base + G["gate"])
                dve.tensor_tensor(score[:, bass.ds(g * 4, 4), 0:ME[m]], bank[1][:, 0:4 * ME[m]].rearrange("p (t e) -> p t e", t=4),
                                  row4(bg_b[m], 4, ME[m]), ALU.add).then_inc(gate_step, 1)

        def vector_top2(dve, m):
            E = ME[m]
            base = m * NTS
            f = lambda v: v[:, :, 0:E]
            e = lambda v: v.unsqueeze(2).to_broadcast([P, NT, E])
            sc, lo, o1, o2, w, cb = (f(v) for v in (score, s2, oh1, oh2, tw, comb))
            rk = rank[:, 0:E].unsqueeze(1).to_broadcast([P, NT, E])
            at_ = lambda s: dve.wait_ge(top_step, base + T_[s])
            then = lambda ins: ins.then_inc(top_step, 1)

            def pick(s, one, i, n):
                then(dve.tensor_reduce(tp[:, i, :], s, AX.X, ALU.max))
                at_("m" + n)
                then(dve.tensor_tensor(one, s, e(tp[:, i, :]), ALU.is_equal))
                at_("eq" + n)
                then(dve.tensor_tensor(w, one, rk, ALU.mult))
                at_("rk" + n)
                then(dve.tensor_reduce(tp[:, 2, :], w, AX.X, ALU.max))
                at_("top" + n)
                then(dve.tensor_tensor(one, w, e(tp[:, 2, :]), ALU.is_equal))
                at_("oh" + n)

            pick(sc, o1, 0, "1")
            then(dve.tensor_scalar(w, o1, -1.0, 1.0, ALU.mult, ALU.add))
            at_("keep")
            then(dve.tensor_tensor(lo, sc, w, ALU.mult))
            at_("rest")
            then(dve.scalar_tensor_tensor(out=lo, in0=o1, scalar=-3.0e38, in1=lo, op0=ALU.mult, op1=ALU.add))
            at_("low")
            pick(lo, o2, 1, "2")
            then(dve.tensor_tensor(tp[:, 3, :], tp[:, 1, :], tp[:, 0, :], ALU.subtract))
            at_("p")
            then(dve.tensor_scalar(tp[:, 5, :], tp[:, 4, :], 1.0, None, ALU.add))
            at_("p1")
            then(dve.reciprocal(tp[:, 6, :], tp[:, 5, :]))
            at_("r1")
            then(dve.tensor_tensor(tp[:, 7, :], tp[:, 4, :], tp[:, 6, :], ALU.mult))
            at_("r2")
            then(dve.tensor_tensor(w, o1, e(tp[:, 6, :]), ALU.mult))
            at_("c1")
            then(dve.tensor_tensor(lo, o2, e(tp[:, 7, :]), ALU.mult))
            at_("c2")
            then(dve.tensor_tensor(cb, w, lo, ALU.add))
            at_("comb")

        def scalar_top2(act, m):
            act.wait_ge(top_step, m * NTS + T_["diff"])
            act.activation(tp[:, 4, :], tp[:, 3, :], ACT.Exp).then_inc(top_step, 1)

        HN = ME[0] * HT[0]
        assert HN == ME[1] * HT[1] and HN % 4 == 0

        def passes(eng, m):
            loop = eng.Fori(0, TG // 2)
            return loop, lambda r: (r * 2 + m * TG, r * (2 * HN) + m * TG * HN, r * (2 * ME[m]) + m * TG * ME[0])

        def tensor_experts(pe, m):
            if m == 0:
                pe.sem_inc(x_turned, 2)
                pe.sem_inc(hid_done, 4)
                pe.sem_inc(ex_used, 4)
                pe.sem_inc(y_sum, 1)
                pe.sem_inc(ysum_turned, 1)
                pe.sem_inc(c_turned, 2)
            loop, before = passes(pe, m)
            E, H = ME[m], HT[m]
            with loop as r:
                gb, hb, eb = before(r)

                def held():
                    pe.sem_inc(waited[pe.engine], 1)

                def turn(e):
                    pe.wait_ge(x_scaled, eb + (e + 1))
                    pe.wait_ge(x_copied, eb + (e + 1))
                    held()
                    for t in range(4):
                        mm = pe.transpose(bank[e % 2][0:C + 1, t * P:(t + 1) * P], x_sc[e % 2][:, t, :], ident[:])
                    mm.then_inc(x_turned, 1)

                def hidden(i):
                    pe.wait_ge(x_copied, eb + (i // H + 3))
                    pe.wait_ge(relu_done[i % 2], hb // 2 + (i // 2 + 1))
                    held()
                    pe.matmul(bank[2 + i % 4][:], w1[m][:, i % HN, :], xeT[i // H % 2], start=True, stop=True).then_inc(hid_done, 1)

                def second(i):
                    if i % HN == 0:
                        pe.wait_ge(ysum_copied, gb + (i // HN + 1))
                    pe.wait_ge(relu_done[i % 2], hb // 2 + (i // 2 + 3))
                    held()
                    pe.matmul(bank[6][0:C, :], w2[m][:, i % HN, :], hid[i % 4], start=(i % HN == 0), stop=False).then_inc(ex_used, 1)

                def bias(u):
                    pe.wait_ge(c_copied, gb + (u + 1))
                    held()
                    pe.matmul(bank[6][0:C, :], b2[m], combT[0:E], start=False, stop=True).then_inc(y_sum, 1)

                def turn_comb(u):
                    pe.wait_ge(staged, gb + (u + 1))
                    pe.wait_ge(ysum_taken, gb + (u + 1))
                    held()
                    for t in range(4):
                        mm = pe.transpose(bank[7][0:E, t * P:(t + 1) * P], c_st[u][:, t, 0:E], ident[:])
                    mm.then_inc(c_turned, 1)

                def turn_y(u):
                    pe.wait_ge(ysum_copied, gb + (u + 2))
                    held()
                    for t in range(4):
                        mm = pe.transpose(bank[7][:, t * C:(t + 1) * C], yT[:, t * P:(t + 1) * P], ident[0:C, 0:C])
                    mm.then_inc(ysum_turned, 1)

                turn(0)
                turn(1)
                for i in range(2 * HN + 2):
                    if i < 2 * HN:
                        hidden(i)
                        if i % H == H - 1 and i // H + 2 < 2 * E:
                            turn(i // H + 2)
                    if i in (3, HN + 6):
                        turn_comb(i // HN)
                    if i >= 2:
                        second(i - 2)
                        if (i - 2) % HN == HN - 1:
                            bias((i - 2) // HN)
                    if i == HN + 4:
                        turn_y(0)
                turn_y(1)

        def scalar_experts(act, m):
            if m == 0:
                act.sem_inc(x_copied, 2)
                act.sem_inc(relu_done[0], 2)
                act.sem_inc(ysum_copied, 1)
            loop, before = passes(act, m)
            E, H = ME[m], HT[m]
            with loop as r:
                gb, hb, eb = before(r)

                def copy_x(e):
                    act.wait_ge(x_turned, eb + (e + 3))
                    act.wait_ge(hid_done, hb + ((e - 1) * H + 4))
                    act.activation(xeT[e % 2], bank[e % 2][0:C + 1, :], ACT.Copy).then_inc(x_copied, 1)

                def copy_y(u):
                    act.wait_ge(ysum_turned, gb + (u + 1))
                    act.wait_ge(y_sum, gb + (u + 2))
                    act.activation(yT, bank[6][0:C, :], ACT.Copy).then_inc(ysum_copied, 1)

                copy_x(0)
                copy_x(1)
                for i in range(2 * HN):
                    if i % 2 == 0:
                        act.wait_ge(hid_done, hb + (i + 5))
                        act.wait_ge(ex_used, hb + (i + 1))
                        act.activation(hid[i % 4], bank[2 + i % 4][:], ACT.Relu).then_inc(relu_done[0], 1)
                    if i % H == H - 1 and i // H + 2 < 2 * E:
                        copy_x(i // H + 2)
                    if i == HN + 1:
                        copy_y(0)
                copy_y(1)

        def vector_experts(dve, m):
            if m == 0:
                dve.sem_inc(relu_done[1], 2)
                dve.sem_inc(ysum_taken, 1)
            for u in range(2):
                dve.memset(x_st[u][:, :, C:C + 1], 1.0).then_inc(ones_set, 1)
            dve.wait_ge(ones_set, 2 * m + 2)
            loop, before = passes(dve, m)
            E, H = ME[m], HT[m]
            with loop as r:
                gb, hb, eb = before(r)

                def stage(u):
                    dve.wait_ge(c_turned, gb + (u + 1))
                    dve.tensor_scalar(x_st[u][:, :, 0:C], x_tok[:, bass.ds(r * 8 + 4 * u, 4), :], 1.0, None, ALU.mult)
                    dve.tensor_scalar(c_st[u][:, :, 0:E], comb[:, bass.ds(r * 8 + 4 * u, 4), 0:E], 1.0, None, ALU.mult).then_inc(staged, 1)

                def scale_x(e):
                    u = e // E
                    if e % E == 0:
                        dve.wait_ge(staged, gb + (u + 1))
                    dve.wait_ge(x_turned, eb + (e + 1))
                    dve.tensor_tensor(x_sc[e % 2], x_st[u], c_st[u][:, :, e % E:e % E + 1].to_broadcast([P, 4, C + 1]),
                                      ALU.mult).then_inc(x_scaled, 1)

                def copy_comb(u):
                    dve.wait_ge(y_sum, gb + (u + 1))
                    dve.wait_ge(c_turned, gb + (u + 3))
                    dve.tensor_scalar(combT[0:E], bank[7][0:E, :], 1.0, None, ALU.mult).then_inc(c_copied, 1)

                def take_y(u):
                    dve.wait_ge(ysum_turned, gb + (u + 2))
                    dve.tensor_scalar(o_tok[:, bass.ds(r * 8 + 4 * u, 4), :],
                                      bank[7][:, 0:4 * C].rearrange("p (t c) -> p t c", t=4), 1.0, None, ALU.mult).then_inc(ysum_taken, 1)

                stage(0)
                scale_x(0)
                scale_x(1)
                stage(1)
                for i in range(2 * HN):
                    if i % H == 0 and i // H + 2 < 2 * E:
                        scale_x(i // H + 2)
                    if i % 2 == 1:
                        dve.wait_ge(hid_done, hb + (i + 5))
                        dve.wait_ge(ex_used, hb + (i + 1))
                        dve.tensor_scalar(hid[i % 4], bank[2 + i % 4][:], 0.0, None, ALU.max).then_inc(relu_done[1], 1)
                    if i in (3, HN + 6):
                        copy_comb(i // HN)
                    if i == HN + 4:
                        take_y(0)
                take_y(1)

        F, NF = steps("xg", "turn", "xT", "proj", "qT", "kT", "v", "zero_sum", "zero_test", "mask", "score", "s_max", "s_sub", "s_exp",
                      "s_sum", "s_inv", "s_mask", "s_norm", "pT", "pT_copy", "att", "att_copy", "out", "bias", "add")
        next_free[0] = work
        qT1, kT1 = lanes(BK, parts=C), lanes(BK, parts=C)
        v1 = lanes(GI, C, parts=C)
        zt = lanes(4, 2)
        mk = lanes(4)
        pr = lanes(4, C)
        ps_ = lanes(4, 4)
        pT = lanes(BK, parts=C)
        oT = lanes(BK, parts=C)
        ob = lanes(4, C)

        def tensor_self(pe):
            with pe.Fori(0, TG // 2) as r:
                def at_(u, s):
                    pe.wait_ge(self_step[u], r * NF + F[s])
                    pe.sem_inc(waited[pe.engine], 1)

                for u in range(2):
                    at_(u, "xg")
                    for t in range(4):
                        mm = pe.transpose(lane_bank[u][0][0:C, t * P:(t + 1) * P], xgs[u][:, t, :], ident[:])
                    mm.then_inc(self_step[u], 1)
                for u in range(2):
                    at_(u, "xT")
                    pe.matmul(lane_bank[u][1][0:C, :], wqT, xTs[u], start=True, stop=True)
                    pe.matmul(lane_bank[u][2][0:C, :], wkT, xTs[u], start=True, stop=True)
                    for b in range(GI):
                        pe.matmul(lane_bank[u][3][0:C, b * C:(b + 1) * C], xTs[u][:, b * S:(b + 1) * S], wvT, start=True, stop=True)
                    for t in range(4):
                        mm = pe.matmul(lane_bank[u][0][:, 2 * t:2 * t + 2], xTs[u][:, t * P:(t + 1) * P], wqk0, start=True, stop=True)
                    mm.then_inc(self_step[u], 1)
                for u in range(2):
                    at_(u, "mask")
                    for b in range(GI):
                        hp = slice(b % 2 * C, (b % 2 + 1) * C)
                        mm = pe.matmul(lane_bank[u][1][hp, b // 2 * C:(b // 2 + 1) * C], qT1[u][:, b * S:(b + 1) * S], kT1[u][:, b * S:(b + 1) * S],
                                       start=True, stop=True)
                    mm.then_inc(self_step[u], 1)
                for u in range(2):
                    at_(u, "s_norm")
                    for t in range(4):
                        mm = pe.transpose(lane_bank[u][2][0:C, t * P:(t + 1) * P], pr[u][:, t, :], ident[:])
                    mm.then_inc(self_step[u], 1)
                for u in range(2):
                    at_(u, "pT_copy")
                    for b in range(GI):
                        mm = pe.matmul(lane_bank[u][3][0:C, b * S:(b + 1) * S], v1[u][:, b, :], pT[u][:, b * S:(b + 1) * S], start=True, stop=True)
                    mm.then_inc(self_step[u], 1)
                for u in range(2):
                    at_(u, "att_copy")
                    for t in range(4):
                        mm = pe.matmul(lane_bank[u][0][:, t * C:(t + 1) * C], oT[u][:, t * P:(t + 1) * P], woT, start=True, stop=True)
                    mm.then_inc(self_step[u], 1)

        def scalar_self(act):
            with act.Fori(0, TG // 2) as r:
                at_ = lambda u, s: act.wait_ge(self_step[u], r * NF + F[s])
                for u in range(2):
                    at_(u, "turn")
                    act.activation(xTs[u], lane_bank[u][0][0:C, :], ACT.Copy).then_inc(self_step[u], 1)
                for u in range(2):
                    at_(u, "proj")
                    act.activation(qT1[u], lane_bank[u][1][0:C, :], ACT.Identity, bias=bq_c).then_inc(self_step[u], 1)
                for u in range(2):
                    at_(u, "s_sub")
                    act.activation(pr[u], pr[u], ACT.Exp, scale=float(C) ** -0.5).then_inc(self_step[u], 1)
                for u in range(2):
                    at_(u, "pT")
                    act.activation(pT[u], lane_bank[u][2][0:C, :], ACT.Copy).then_inc(self_step[u], 1)
                for u in range(2):
                    at_(u, "att")
                    act.activation(oT[u], lane_bank[u][3][0:C, :], ACT.Copy).then_inc(self_step[u], 1)

        def vector_self(dve):
            with dve.Fori(0, TG // 2) as r:
                at_ = lambda u, s: dve.wait_ge(self_step[u], r * NF + F[s])
                then = lambda u, ins: ins.then_inc(self_step[u], 1)
                sc_of = lambda u: lane_bank[u][1][:, 0:4 * C].rearrange("p (t j) -> p t j", t=4)
                for u in range(2):
                    dve.wait_ge(self_step[u], r * NF + 1)
                    then(u, dve.tensor_scalar(xgs[u], x_tok[:, bass.ds(r * 8 + 4 * u, 4), :], 1.0, None, ALU.mult))
                for u in range(2):
                    at_(u, "qT")
                    then(u, dve.tensor_scalar(kT1[u], lane_bank[u][2][0:C, :], bk_c, None, ALU.add))
                for u in range(2):
                    at_(u, "kT")
                    then(u, dve.tensor_tensor(v1[u], lane_bank[u][3][0:C, :].rearrange("p (b c) -> p b c", b=GI), row4(bv_b[0:C], GI), ALU.add))
                for u in range(2):
                    at_(u, "v")
                    then(u, dve.tensor_tensor(zt[u], lane_bank[u][0][:, 0:8].rearrange("p (t a) -> p t a", t=4), row4(bqk0_b, 4, 2), ALU.add))
                for u in range(2):
                    at_(u, "zero_sum")
                    then(u, dve.tensor_scalar(zt[u], zt[u], 0.0, None, ALU.not_equal))
                for u in range(2):
                    at_(u, "zero_test")
                    then(u, dve.tensor_tensor(mk[u], zt[u][:, :, 0], zt[u][:, :, 1], ALU.mult))
                for u in range(2):
                    at_(u, "score")
                    then(u, dve.tensor_reduce(ps_[u][:, 0, :], sc_of(u), AX.X, ALU.max))
                for u in range(2):
                    at_(u, "s_max")
                    then(u, dve.tensor_tensor(pr[u], sc_of(u), ps_[u][:, 0, :].unsqueeze(2).to_broadcast([P, 4, C]), ALU.subtract))
                for u in range(2):
                    at_(u, "s_exp")
                    then(u, dve.tensor_reduce(ps_[u][:, 1, :], pr[u], AX.X, ALU.add))
                for u in range(2):
                    at_(u, "s_sum")
                    then(u, dve.reciprocal(ps_[u][:, 2, :], ps_[u][:, 1, :]))
                for u in range(2):
                    at_(u, "s_inv")
                    then(u, dve.tensor_tensor(ps_[u][:, 3, :], ps_[u][:, 2, :], mk[u], ALU.mult))
                for u in range(2):
                    at_(u, "s_mask")
                    then(u, dve.tensor_tensor(pr[u], pr[u], ps_[u][:, 3, :].unsqueeze(2).to_broadcast([P, 4, C]), ALU.mult))
                for u in range(2):
                    at_(u, "out")
                    then(u, dve.tensor_tensor(ob[u], lane_bank[u][0][:, 0:4 * C].rearrange("p (t c) -> p t c", t=4), row4(bo_b), ALU.add))
                for u in range(2):
                    at_(u, "bias")
                    hg = h_tok[:, bass.ds(r * 8 + 4 * u, 4), :]
                    then(u, dve.tensor_tensor(hg, hg, ob[u], ALU.add))
            for u in range(2):
                dve.wait_ge(self_step[u], TG // 2 * NF + 1)

        fin_step, out_stored = sem("fin_step"), sem("out_stored")

        def tail_sync(sp):
            sync_load_tokens(sp)
            sp.wait_ge(fin_step, 6)
            sp.dma_start(out.rearrange("(t p) c -> p t c", p=P), h_tok).then_inc(out_stored, 16)
            sp.wait_ge(out_stored, 16)

        def tail_tensor(pe):
            pe.wait_ge(tok_loaded, N_TOK)
            tensor_attention(pe)
            for m in range(2):
                if m == 1:
                    tensor_self(pe)
                tensor_gate(pe, m)
                tensor_experts(pe, m)

        def tail_scalar(act):
            act.wait_ge(tok_loaded, N_TOK)
            scalar_norm(act, 0)
            scalar_rms(act, 0)
            scalar_attention(act)
            scalar_rms(act, 1)
            for m in range(2):
                if m == 1:
                    scalar_norm(act, 2)
                    scalar_self(act)
                scalar_norm(act, (1, 3)[m])
                scalar_gate(act, m)
                scalar_top2(act, m)
                scalar_experts(act, m)
            scalar_norm(act, 4)

        def tail_vector(dve):
            for s in (ln_step, rms_step, gate_step, top_step, *self_step):
                dve.sem_inc(s, 1)
            vector_attention(dve)
            for m in range(2):
                if m == 1:
                    vector_norm(dve, 2, h_tok, x_tok)
                    vector_self(dve)
                vector_norm(dve, (1, 3)[m], h_tok, x_tok)
                vector_gate(dve, m)
                dve.wait_ge(gate_step, (m + 1) * (TG * NGS) + 1)
                vector_top2(dve, m)
                vector_experts(dve, m)
                dve.wait_ge(ysum_taken, (m + 1) * TG + 1)
                if m == 0:
                    dve.tensor_tensor(h_tok, h_tok, o_tok, ALU.add).then_inc(fin_step, 1)
                    dve.wait_ge(fin_step, 1)
            dve.tensor_tensor(x_tok, x_tok, o_tok, ALU.add).then_inc(fin_step, 1)
            dve.wait_ge(fin_step, 2)
            vector_norm(dve, 4, x_tok, o_tok)
            dve.tensor_tensor(o_tok, o_tok, row4(gamma_b, NT), ALU.mult).then_inc(fin_step, 1)
            dve.wait_ge(fin_step, 3)
            dve.tensor_tensor(o_tok, o_tok, row4(beta_b, NT), ALU.add).then_inc(fin_step, 1)
            dve.wait_ge(fin_step, 4)
            dve.tensor_tensor(h_tok, h_tok, o_tok, ALU.add).then_inc(fin_step, 2)

        block = ctx.enter_context(nc.Block())
        TOWER = 3 * L

        @block.sync
        def _(sp):
            sync_spectrum0(sp)
            phase_end(sp, 1)
            sync_mix(sp, 0, True)
            phase_end(sp, 2)
            sync_inverse(sp, 0, True)
            phase_end(sp, 3)
            with sp.Fori(1, L) as l:
                sync_forward(sp, l - 1)
                phase_end(sp, l * 3 + 1)
                sync_mix(sp, l, False)
                phase_end(sp, l * 3 + 2)
                sync_inverse(sp, l, False)
                phase_end(sp, l * 3 + 3)
            sync_head(sp)
            phase_end(sp, TOWER + 1)
            tail_sync(sp)

        @block.tensor
        def _(pe):
            tensor_spectrum0(pe)
            phase_end(pe, 1)
            tensor_mix(pe, 0, True)
            phase_end(pe, 2)
            tensor_inverse(pe, 0, True)
            pe.sem_inc(ht_done, 8 * Q)
            phase_end(pe, 3)
            with pe.Fori(1, L) as l:
                tensor_forward(pe, l - 1)
                phase_end(pe, l * 3 + 1)
                tensor_mix(pe, l, False)
                phase_end(pe, l * 3 + 2)
                tensor_inverse(pe, l, False)
                phase_end(pe, l * 3 + 3)
            tensor_head(pe)
            phase_end(pe, TOWER + 1)
            tail_tensor(pe)

        @block.scalar
        def _(act):
            scalar_spectrum0(act)
            phase_end(act, 1)
            scalar_mix(act, 0, True)
            phase_end(act, 2)
            scalar_inverse(act, 0, True)
            act.sem_inc(ft_copied, 1)
            for v in range(2):
                act.sem_inc(spec_stored[v], 64)
            phase_end(act, 3)
            with act.Fori(1, L) as l:
                scalar_forward(act, l - 1)
                phase_end(act, l * 3 + 1)
                scalar_mix(act, l, False)
                phase_end(act, l * 3 + 2)
                scalar_inverse(act, l, False)
                phase_end(act, l * 3 + 3)
            scalar_head(act)
            phase_end(act, TOWER + 1)
            tail_scalar(act)

        @block.vector
        def _(dve):
            vector_spectrum0(dve)
            phase_end(dve, 1)
            vector_mix(dve, 0, True)
            phase_end(dve, 2)
            vector_inverse(dve, 0, True)
            dve.sem_inc(ht_copied, 4)
            dve.sem_inc(fc_copied, 2)
            dve.sem_inc(fr_copied, 1)
            phase_end(dve, 3)
            with dve.Fori(1, L) as l:
                vector_forward(dve, l - 1)
                phase_end(dve, l * 3 + 1)
                vector_mix(dve, l, False)
                phase_end(dve, l * 3 + 2)
                vector_inverse(dve, l, False)
                phase_end(dve, l * 3 + 3)
            vector_head(dve)
            phase_end(dve, TOWER + 1)
            tail_vector(dve)

        @block.gpsimd
        def _(pool):
            gpsimd_spectrum0(pool)
            phase_end(pool, 1)
            phase_end(pool, 2)
            gpsimd_inverse(pool, 0, True)
            phase_end(pool, 3)
            with pool.Fori(1, L) as l:
                phase_end(pool, l * 3 + 1)
                phase_end(pool, l * 3 + 2)
                gpsimd_inverse(pool, l, False)
                phase_end(pool, l * 3 + 3)
            gpsimd_head(pool, tok)
            phase_end(pool, TOWER + 1)


def block_layout(t, E, H):
    return np.ascontiguousarray(t.transpose(2, 0, 1).reshape(C, E * (H // P), P))


def kernel(x, **inputs):
    import concourse.bacc as bacc
    from concourse.bass_utils import run_bass_kernel_spmd as run

    v = {k: np.asarray(a) for k, a in inputs.items()}
    tower = {k[len("L0_tok_"):]: a for k, a in v.items() if k.startswith("L0_tok_")}
    arrays = dft_constants()
    arrays.update(tower_layout(x, *(tower[k] for k in ("fc0_w", "fc0_b", "w1r", "w1i", "w2r", "w2i", "pw_w"))))
    for k in ("pw_b", "gamma", "beta", "fc1_w", "fc1_b", "fc2_w", "fc2_b"):
        arrays[k] = tower[k]
    for k in ("w_qkv", "w_out", "b_out", "g_out", "g_pre"):
        arrays[k] = v["L0_attn_" + k]
    mem = v["L0_attn_mem_kv"]
    arrays["mem_k"] = np.ascontiguousarray(mem[0].reshape(P, -1))
    arrays["mem_v"] = np.ascontiguousarray(mem[1].reshape(P, -1).T)
    head = np.arange(P) // 32
    arrays["c_headmask"] = (head[:, None] == head[None, :]).astype(np.float32)
    arrays["c_rank"] = (16 - np.arange(16, dtype=np.float32))[None, :]
    arrays["wg0"] = np.ascontiguousarray(v["L0_ffn_Wg"].T)
    arrays["bg0"] = v["L0_ffn_bg"]
    W1, W2 = v["L0_ffn_W1"], v["L0_ffn_W2"]
    E, H, _ = W1.shape
    arrays["w1_0"] = block_layout(W1, E, H)
    arrays["b1_0"] = v["L0_ffn_b1"].reshape(-1)
    arrays["w2_0"] = np.ascontiguousarray(W2.transpose(0, 2, 1).reshape(E * H // P, P, C).transpose(1, 0, 2))
    arrays["b2_0"] = v["L0_ffn_b2"]
    arrays["wg1"] = v["L1_ffn_gate_w"]
    arrays["bg1"] = v["L1_ffn_gate_b"]
    arrays["w1_1"] = np.ascontiguousarray(v["L1_ffn_w1"].transpose(1, 0, 2))
    arrays["b1_1"] = v["L1_ffn_b1"].reshape(-1)
    arrays["w2_1"] = np.ascontiguousarray(v["L1_ffn_w2"].transpose(1, 0, 2))
    arrays["b2_1"] = v["L1_ffn_b2"]
    arrays["ln_gamma"], arrays["ln_beta"] = v["L1_ffn_gamma"], v["L1_ffn_beta"]
    for k in "qkvo":
        arrays[f"w{k}_t"] = np.ascontiguousarray(v["L1_attn_W" + k].T)
        arrays[f"b{k}"] = v["L1_attn_b" + k]
    arrays["wqk0"] = np.stack([v["L1_attn_Wq"][0], v["L1_attn_Wk"][0]], 1)
    arrays["bqk0"] = np.stack([v["L1_attn_bq"][0], v["L1_attn_bk"][0]])

    nc = bacc.Bacc("TRN2", target_bir_lowering=False, num_devices=1)
    d = {k: nc.dram_tensor("in_" + k, a.shape, F32, kind="ExternalInput").ap() for k, a in arrays.items()}
    B = x.shape[0]
    out = nc.dram_tensor("out", [B * S, S], F32, kind="ExternalOutput").ap()
    build(nc, d, B, out)
    r = run(nc, [{"in_" + k: a for k, a in arrays.items()}], core_ids=[0])
    return r.results[0]["out"].reshape(B, S, S)
```
